# Optimizing a Trainium2 kernel written in Bass

```python
import numpy as np
import jax
import jax.numpy as jnp

def _softmax(x, axis=-1):
    return jax.nn.softmax(x, axis=axis)

def _gelu(x):
    return jax.nn.gelu(x, approximate=True)

def _silu(x):
    return jax.nn.silu(x)

def _sigmoid(x):
    return jax.nn.sigmoid(x)

def _layernorm(x, axis=-1, eps=1e-05):
    m = jnp.mean(x, axis=axis, keepdims=True)
    v = jnp.var(x, axis=axis, keepdims=True)
    return (x - m) / jnp.sqrt(v + eps)

def _scatter_add(tgt, idx, src, axis=0):
    return tgt.at[idx].add(src)

def _segment_sum(src, seg, n):
    return jax.ops.segment_sum(src, seg, n)
kernel_name = 'mk_seq_postln_d1_jaxref_r4_962933'

def setup_inputs(seed: int=0):
    np.random.seed(seed)
    _w = jnp.asarray

    def _L0_attn_setup():
        import jax, jax.numpy as jnp
        import numpy as np
        H = 16

        def _kernel(x, gamma, beta):
            mean = x.mean(axis=-1, keepdims=True)
            std = jnp.std(x, axis=-1, ddof=1, keepdims=True)
            xn = (x - mean) / (std + 1e-06)
            return jnp.square(gamma * xn + beta)
        key = jax.random.key(seed)
        ks = jax.random.split(key, 9)
        B, T, C = (2, 512, 256)
        x = jax.random.normal(ks[0], (B, T, C), jnp.float32)
        Wqkv = jax.random.normal(ks[1], (C, 3 * C), jnp.float32) * 0.02
        bqkv = jnp.zeros((3 * C,), jnp.float32)
        gamma_q = jax.random.uniform(ks[2], (C,), jnp.float32)
        beta_q = jax.random.uniform(ks[3], (C,), jnp.float32)
        gamma_k = jax.random.uniform(ks[4], (C,), jnp.float32)
        beta_k = jax.random.uniform(ks[5], (C,), jnp.float32)
        Wo = jax.random.normal(ks[6], (C, C), jnp.float32) * 0.02
        bo = jnp.zeros((C,), jnp.float32)
        return {'x': x, 'Wqkv': Wqkv, 'bqkv': bqkv, 'gamma_q': gamma_q, 'beta_q': beta_q, 'gamma_k': gamma_k, 'beta_k': beta_k, 'Wo': Wo, 'bo': bo}
    _L0_attn_in = _L0_attn_setup()

    def _L0_ffn_setup():
        import jax, jax.numpy as jnp
        import numpy as np
        H = 256
        I = 512
        E = 8
        TOP_K = 2
        NUM_SHARED = 1
        key = jax.random.key(seed)
        ks = jax.random.split(key, 9)
        s = 0.02
        x = jax.random.normal(ks[0], (2, 512, H), dtype=jnp.float32)
        sg_w = jax.random.normal(ks[1], (I, H), dtype=jnp.float32) * s
        su_w = jax.random.normal(ks[2], (I, H), dtype=jnp.float32) * s
        sd_w = jax.random.normal(ks[3], (H, I), dtype=jnp.float32) * s
        router_w = jax.random.normal(ks[4], (E, H), dtype=jnp.float32) * s
        routing_bias = jnp.zeros((E,), dtype=jnp.float32)
        wg = jax.random.normal(ks[5], (E, I, H), dtype=jnp.float32) * s
        wu = jax.random.normal(ks[6], (E, I, H), dtype=jnp.float32) * s
        wd = jax.random.normal(ks[7], (E, H, I), dtype=jnp.float32) * s
        return {'x': x, 'sg_w': sg_w, 'su_w': su_w, 'sd_w': sd_w, 'router_w': router_w, 'routing_bias': routing_bias, 'wg': wg, 'wu': wu, 'wd': wd}
    _L0_ffn_in = _L0_ffn_setup()
    _d = {'L0_attn_x': _L0_attn_in['x'], 'L0_attn_Wqkv': _L0_attn_in['Wqkv'], 'L0_attn_bqkv': _L0_attn_in['bqkv'], 'L0_attn_gamma_q': _L0_attn_in['gamma_q'], 'L0_attn_beta_q': _L0_attn_in['beta_q'], 'L0_attn_gamma_k': _L0_attn_in['gamma_k'], 'L0_attn_beta_k': _L0_attn_in['beta_k'], 'L0_attn_Wo': _L0_attn_in['Wo'], 'L0_attn_bo': _L0_attn_in['bo'], 'L0_ffn_sg_w': _L0_ffn_in['sg_w'], 'L0_ffn_su_w': _L0_ffn_in['su_w'], 'L0_ffn_sd_w': _L0_ffn_in['sd_w'], 'L0_ffn_router_w': _L0_ffn_in['router_w'], 'L0_ffn_routing_bias': _L0_ffn_in['routing_bias'], 'L0_ffn_wg': _L0_ffn_in['wg'], 'L0_ffn_wu': _L0_ffn_in['wu'], 'L0_ffn_wd': _L0_ffn_in['wd']}
    _x0 = _d['L0_attn_x']
    _d['L0_attn_x'] = jax.random.normal(jax.random.fold_in(jax.random.key(seed), 1), (1, 4096, 256), dtype=_x0.dtype)
    del _x0
    return _d

def reference(L0_attn_x, L0_attn_Wqkv, L0_attn_bqkv, L0_attn_gamma_q, L0_attn_beta_q, L0_attn_gamma_k, L0_attn_beta_k, L0_attn_Wo, L0_attn_bo, L0_ffn_sg_w, L0_ffn_su_w, L0_ffn_sd_w, L0_ffn_router_w, L0_ffn_routing_bias, L0_ffn_wg, L0_ffn_wu, L0_ffn_wd):

    def _L0_attn_ref(x, Wqkv, bqkv, gamma_q, beta_q, gamma_k, beta_k, Wo, bo):
        import jax, jax.numpy as jnp
        import numpy as np
        H = 16

        def _kernel(x, gamma, beta):
            mean = x.mean(axis=-1, keepdims=True)
            std = jnp.std(x, axis=-1, ddof=1, keepdims=True)
            xn = (x - mean) / (std + 1e-06)
            return jnp.square(gamma * xn + beta)
        B, T, C = x.shape
        D = C // H
        qkv = x @ Wqkv + bqkv
        q, k, v = jnp.split(qkv, 3, axis=2)
        kerq = _kernel(q, gamma_q, beta_q)
        kerk = _kernel(k, gamma_k, beta_k)
        kerq = kerq.reshape(B, T, H, D).transpose(0, 2, 1, 3)
        kerk = kerk.reshape(B, T, H, D).transpose(0, 2, 1, 3)
        vh = v.reshape(B, T, H, D).transpose(0, 2, 1, 3)
        kv = jnp.cumsum(jnp.einsum('bhtf,bhtg->bhtfg', kerk, vh), axis=2)
        out = jnp.einsum('bhtf,bhtfg->bhtg', kerq, kv)
        Z = 1.0 / (jnp.einsum('bhtf,bhtf->bht', kerq, jnp.cumsum(kerk, axis=2)) + 1e-06)
        out = out * Z[..., None]
        out = out.transpose(0, 2, 1, 3).reshape(B, T, C)
        return out @ Wo + bo

    def _L0_ffn_ref(x, sg_w, su_w, sd_w, router_w, routing_bias, wg, wu, wd):
        import jax, jax.numpy as jnp
        import numpy as np
        H = 256
        I = 512
        E = 8
        TOP_K = 2
        NUM_SHARED = 1
        orig_shape = x.shape
        xt = x.reshape(-1, H)
        T = xt.shape[0]
        shared = jax.nn.silu(xt @ sg_w.T) * (xt @ su_w.T) @ sd_w.T
        shared = shared / NUM_SHARED
        logits = xt @ router_w.T + routing_bias
        probs = jax.nn.sigmoid(logits)
        topk_p, topk_idx = jax.lax.top_k(probs, TOP_K)
        topk_p = topk_p / jnp.sum(topk_p, axis=-1, keepdims=True)
        w = jnp.zeros((T, E), dtype=xt.dtype)
        w = w.at[jnp.arange(T)[:, None], topk_idx].add(topk_p)
        g = jnp.einsum('th,eih->tei', xt, wg)
        u = jnp.einsum('th,eih->tei', xt, wu)
        h = jax.nn.silu(g) * u
        y = jnp.einsum('tei,ehi->teh', h, wd)
        routed = jnp.einsum('te,teh->th', w, y)
        return (shared + routed).reshape(orig_shape)
    x = L0_attn_x
    x = _layernorm(x + _L0_attn_ref(x, L0_attn_Wqkv, L0_attn_bqkv, L0_attn_gamma_q, L0_attn_beta_q, L0_attn_gamma_k, L0_attn_beta_k, L0_attn_Wo, L0_attn_bo), axis=-1)
    x = _layernorm(x + _L0_ffn_ref(x, L0_ffn_sg_w, L0_ffn_su_w, L0_ffn_sd_w, L0_ffn_router_w, L0_ffn_routing_bias, L0_ffn_wg, L0_ffn_wu, L0_ffn_wd), axis=-1)
    return x

_drawn_inputs = setup_inputs


def setup_inputs(seed=0):
    import zlib

    import numpy as np

    out = dict(_drawn_inputs(seed))
    spreads = {'L0_attn_bqkv': (0.0, 0.1), 'L0_attn_bo': (0.0, 0.1), 'L0_ffn_routing_bias': (0.0, 0.8)}
    factors = {'L0_attn_Wqkv': 8.0,
     'L0_attn_gamma_q': 8.0,
     'L0_attn_beta_q': 8.0,
     'L0_attn_gamma_k': 8.0,
     'L0_attn_beta_k': 8.0,
     'L0_ffn_router_w': 3.941,
     'L0_ffn_wg': 3.388,
     'L0_ffn_wu': 3.346,
     'L0_ffn_wd': 3.349,
     'L0_ffn_sg_w': 2.846,
     'L0_ffn_su_w': 2.678,
     'L0_ffn_sd_w': 2.689}
    for name, (base, spread) in spreads.items():
        noise = np.random.default_rng([zlib.crc32(name.encode()), seed]).standard_normal(out[name].shape)
        drawn = base * np.exp(spread * noise) if base else spread * noise
        out[name] = jnp.asarray(drawn.astype(out[name].dtype))
    for name, factor in factors.items():
        out[name] = (out[name] * factor).astype(out[name].dtype)
    return out
```

```python
from contextlib import ExitStack

import concourse.bass as bass
from concourse import mybir

ALU = mybir.AluOpType
ACT = mybir.ActivationFunctionType
AX_X = mybir.AxisListType.X
F32 = mybir.dt.float32
I32 = mybir.dt.int32

P = 128
HEADS = 16
D = 16
EPS_LN = 1e-5
EPS_ATTN = 1e-6
TOP_K = 2


class Tile:

    def __init__(self, it, d):
        self.index = it * 2 + d
        self.round = it + d // 2
        self.parity = d % 2
        self.later = not isinstance(self.round, int) or self.round > 0


def wait(eng, sem, value):
    if not isinstance(value, int) or value > 0:
        eng.wait_ge(sem, value)


def post_ln_block(nc, xT, x, wqkv, bqkv, gb_cols, gk_row, bk_row, wo, bo, router, router_bias, ffn_w,
                  out, x_rows, y_rows):
    tiles, _, C = x.shape
    halves = C // P
    hpg = P // D
    experts = ffn_w.shape[0] - 1
    E = experts
    FW = ffn_w.shape[2]
    I = FW // (3 * halves)
    inner = I // P
    slot_tiles = x_rows.shape[0] // P - tiles
    ffn_tiles = tiles + slot_tiles
    assert slot_tiles >= tiles * TOP_K + E - 1 and ffn_tiles % 2 == 0 and tiles % 2 == 0
    TE = tiles * E
    UP, DOWN = halves * I, 2 * halves * I
    VD = P + D

    with ExitStack() as ctx:
        def sb(name, shape, dt=F32):
            return ctx.enter_context(nc.sbuf_tensor(name, [P, *shape], dt))

        def sem(name):
            return ctx.enter_context(nc.semaphore(name))

        bank = [ctx.enter_context(nc.psum_tensor(f"bank{n}", [P, 512], F32)) for n in range(8)]
        qk_ps = bank[0][:, :]
        v_ps = bank[1][:, 0:C]
        qkT_ps = bank[2][:, :]
        score_ps = [bank[3][:, :], bank[4][:, :]]
        num_ps = bank[5][:, 0:C].rearrange("p (a t) -> p a t", a=halves)
        den_ps = bank[5][:, C:2 * C].rearrange("p (a t) -> p a t", a=halves)
        state_ps = bank[6][:, 0:C].rearrange("p (a t) -> p a t", a=halves)
        wo_ps = bank[7][:, 0:C]
        x1T_ps = bank[7][:, C:2 * C].rearrange("p (a t) -> p a t", a=halves)
        logit_ps = bank[7][:, 0:E]
        rank_ps, total_ps = bank[5][:, 0:TE], bank[6][:, 0:TE]
        gate_ps, up_ps = bank[0][:, :], bank[1][:, :]
        inT_ps = bank[2][:, 0:C].rearrange("p (a t) -> p a t", a=halves)
        hT_ps = bank[3][:, :].rearrange("p (m t) -> p m t", m=inner)
        y_ps = bank[4][:, 0:C]

        ffn_sb = sb("ffn_sb", [E + 1, FW])
        wqkv_sb = sb("wqkv_sb", [halves, 3 * C])
        wo_sb = sb("wo_sb", [halves, C])
        router_sb = sb("router_sb", [halves, E])
        bqkv_sb = sb("bqkv_sb", [3 * C])
        bo_sb = sb("bo_sb", [C])
        gk_sb = sb("gk_sb", [C])
        bk_sb = sb("bk_sb", [C])
        rbias_sb = sb("rbias_sb", [E])
        gb_sb = sb("gb_sb", [2, 2 * halves])
        ident = sb("ident", [P])
        ones = sb("ones", [P])
        head_block = sb("head_block", [P])
        head_of = sb("head_of", [hpg])
        causal = sb("causal", [P])
        before = sb("before", [P])
        eps_ln = sb("eps_ln", [1])
        xT_sb = sb("xT_sb", [2, halves, P])
        x_sb = sb("x_sb", [2, C])
        xb_sb = sb("xb_sb", [2, C])
        qk_sb = sb("qk_sb", [2 * C])
        stats = sb("stats", [2, 6])
        moments = sb("moments", [2, 2])
        std = sb("std", [2])
        std_eps = sb("std_eps", [2])
        inv_std = sb("inv_std", [2])
        qkn = sb("qkn", [2, 2 * C])
        kerT = sb("kerT", [2, 2 * halves, P])
        ksumT = sb("ksumT", [2, halves, P])
        prod = sb("prod", [2, halves, P])
        ktok = sb("ktok", [2, C])
        q_diag = sb("q_diag", [2, halves, hpg, P])
        v_diag = sb("v_diag", [2, halves, hpg * VD])
        scores = sb("scores", [2, HEADS, P])
        state = sb("state", [halves, P])
        den = sb("den", [halves, P])
        attnT = sb("attnT", [2, halves, P])
        res = sb("res", [C])
        ln_stats = sb("ln_stats", [6])
        ln_moments = sb("ln_moments", [2])
        ln_std = sb("ln_std", [1])
        ln_inv = sb("ln_inv", [1])
        x1_sb = sb("x1_sb", [2, C])
        x1T_sb = sb("x1T_sb", [halves, P])
        logits = sb("logits", [tiles, E])
        scores_flat = scores[:, :, :, :].rearrange("p b h t -> p (b h t)")
        used = [0]

        def room(*shape):
            n, at = 1, used[0]
            for x in shape:
                n *= x
            used[0] += n
            flat_room = scores_flat[:, at:at + n]
            return flat_room.rearrange("p (a b) -> p a b", b=shape[1]) if len(shape) > 1 else flat_room

        def flat(ap):
            return ap.rearrange("p a b -> p (a b)")

        probs, is_top, rest, onehot1, onehot2, member, position, picked = (room(tiles, E) for _ in range(8))
        totals_by_expert, running_by_expert, reset_by_expert = (room(E, tiles) for _ in range(3))
        max1, max2, first, p_sum, p_inv = (room(tiles) for _ in range(5))
        weight, position_f = room(TOP_K, tiles), room(TOP_K, tiles)
        position_i = room(TOP_K, tiles).bitcast(I32)
        tile_n = room(E).bitcast(I32)
        tile_f, tile_end, slot_base = (room(E) for _ in range(3))
        expert_cmp = room(slot_tiles, E)[0:1]
        expert_f = room(slot_tiles)[0:1]
        expert_i = room(ffn_tiles).bitcast(I32)[0:1]
        countdown = sb("countdown", [E])
        slot_number = sb("slot_number", [slot_tiles])
        q_flat = q_diag[:, :, :, :, :].rearrange("p b a h t -> p (b a h t)")
        in_sb = q_flat[:, 0:2 * C].rearrange("p (b c) -> p b c", b=2)
        inT_sb = q_flat[:, 2 * C:4 * C].rearrange("p (b a t) -> p b a t", b=2, a=halves)
        silu_sb = q_flat[:, 4 * C:4 * C + I]
        h_sb = q_flat[:, 4 * C + I:4 * C + 2 * I]
        hT_sb = q_flat[:, 4 * C + 2 * I:4 * C + 4 * I].rearrange("p (b m t) -> p b m t", b=2, m=inner)
        y_sb = q_flat[:, 4 * C + 4 * I:6 * C + 4 * I].rearrange("p (b c) -> p b c", b=2)
        v_flat = v_diag[:, :, :, :].rearrange("p b a n -> p (b a n)")
        send_sb = v_flat[:, 0:2 * C].rearrange("p (b c) -> p b c", b=2)
        own_sb = v_flat[:, 2 * C:6 * C].rearrange("p (b s c) -> p b s c", b=2, s=2)
        got_sb = v_flat[:, 6 * C:10 * C].rearrange("p (b s c) -> p b s c", b=2, s=TOP_K)
        out_sb = v_flat[:, 10 * C:12 * C].rearrange("p (b c) -> p b c", b=2)
        sum_sb = v_flat[:, 12 * C:16 * C].rearrange("p (b s c) -> p b s c", b=2, s=2)
        index_sb = sb("index_sb", [2, TOP_K], I32)
        gather_sb = sb("gather_sb", [2, TOP_K], I32)
        weight_sb = sb("weight_sb", [2, TOP_K])
        turn = sb("turn", [1])
        f_moments = sb("f_moments", [2, 2])
        f_std = sb("f_std", [2, 1])

        names = """consts_set masks_set params_loaded zero_set zero_filled ffn_loaded last_loaded
            qk_mm v_mm qk_biased v_ready stats_done aggr_done std_done std_eps_done inv_std_done norm_done
            qkT_mm ker_done qexp_done scan_done prod_done ktok_done score_mm mask_done num_mm av_done
            den_done inv_den_done attn_done state_ready wo_mm xb_done res_done ln_stats_done ln_aggr_done
            ln_std_done ln_inv_done x1_done x1T_mm x1T_done logit_mm logit_done
            eps_set sums_zeroed probs_done route member_done rank_mm total_mm position_done experts_done
            index_set turn_done inT_mm inT_done gu_mm silu_done h_done hT_mm hT_done y_mm y_done
            gather_set sum_done mix_done f_stats_done f_aggr_done f_std_done f_inv_done out_done"""
        s = {n: sem(n) for n in names.split()}
        (consts_set, masks_set, params_loaded, zero_set, zero_filled, ffn_loaded, last_loaded,
         qk_mm, v_mm, qk_biased, v_ready, stats_done, aggr_done, std_done, std_eps_done, inv_std_done, norm_done,
         qkT_mm, ker_done, qexp_done, scan_done, prod_done, ktok_done, score_mm, mask_done, num_mm, av_done,
         den_done, inv_den_done, attn_done, state_ready, wo_mm, xb_done, res_done, ln_stats_done, ln_aggr_done,
         ln_std_done, ln_inv_done, x1_done, x1T_mm, x1T_done, logit_mm, logit_done,
         eps_set, sums_zeroed, probs_done, route, member_done, rank_mm, total_mm, position_done, experts_done,
         index_set, turn_done, inT_mm, inT_done, gu_mm, silu_done, h_done, hT_mm, hT_done, y_mm, y_done,
         gather_set, sum_done, mix_done, f_stats_done, f_aggr_done, f_std_done, f_inv_done, out_done) = s.values()
        x_loaded = [sem(f"x_loaded{b}") for b in range(2)]
        x1_stored = [sem(f"x1_stored{b}") for b in range(2)]
        send_loaded = [sem(f"send_loaded{b}") for b in range(2)]
        sent = [sem(f"sent{b}") for b in range(2)]
        in_loaded = [sem(f"in_loaded{b}") for b in range(2)]
        y_stored = [sem(f"y_stored{b}") for b in range(2)]
        own_loaded = [sem(f"own_loaded{b}") for b in range(2)]
        gathered = [sem(f"gathered{b}") for b in range(2)]
        out_stored = [sem(f"out_stored{b}") for b in range(2)]

        params = [(wqkv_sb[:, :, :], wqkv), (wo_sb[:, :, :], wo), (router_sb[:, :, :], router),
                  (gb_sb[:, :, :], gb_cols), (bqkv_sb[:, :], bqkv.partition_broadcast(P)),
                  (bo_sb[:, :], bo.partition_broadcast(P)), (gk_sb[:, :], gk_row.partition_broadcast(P)),
                  (bk_sb[:, :], bk_row.partition_broadcast(P)), (rbias_sb[:, :], router_bias.partition_broadcast(P))]
        ALL_PARAMS = 16 * len(params)
        ZERO_ROWS = FW // C
        ZERO_FILLS = slot_tiles // ZERO_ROWS
        assert ZERO_FILLS * ZERO_ROWS == slot_tiles
        ZEROED = E - 1
        SHARED = E

        def row_tile(dram, n):
            return dram.rearrange("(n p) c -> n p c", p=P)[bass.ds(n, 1), :, :].rearrange("n p c -> p (n c)")

        block = ctx.enter_context(nc.Block())

        @block.sync
        def _(sp):
            def load_x(t):
                if t.later:
                    sp.wait_ge(v_mm, t.index - 1)
                    sp.wait_ge(xb_done, t.index - 1)
                b = t.parity
                sp.dma_start(xT_sb[:, b, :, :],
                             xT[bass.ds(t.index, 1)].rearrange("n p a t -> p (n a) t")).then_inc(x_loaded[b], 16)
                sp.dma_start(x_sb[:, b, :],
                             x[bass.ds(t.index, 1)].rearrange("n p c -> p (n c)")).then_inc(x_loaded[b], 16)

            load_x(Tile(0, 0))
            for dst, src in params:
                sp.dma_start(dst, src).then_inc(params_loaded, 16)
            load_x(Tile(0, 1))
            sp.wait_ge(zero_set, 1)
            fill = x_rows[tiles * P:, :].rearrange("(n p r) c -> n p (r c)", p=P, r=ZERO_ROWS)
            for n in range(ZERO_FILLS):
                sp.dma_start(fill[n], ffn_sb[:, ZEROED, :]).then_inc(zero_filled, 16)
            for e in [SHARED, *range(ZEROED)]:
                sp.dma_start(ffn_sb[:, e, :], ffn_w[e]).then_inc(ffn_loaded, 16)
            with sp.Fori(1, tiles // 2) as it:
                load_x(Tile(it, 0))
                load_x(Tile(it, 1))
            sp.wait_ge(zero_filled, 16 * ZERO_FILLS)
            sp.dma_start(ffn_sb[:, ZEROED, :], ffn_w[ZEROED]).then_inc(last_loaded, 16)

            def load_in(t, first=False):
                if not first:
                    sp.wait_ge(inT_mm, t.index - 1)
                sp.dma_start(in_sb[:, t.parity, :], row_tile(x_rows, t.index)).then_inc(in_loaded[t.parity], 16)

            for b in range(2):
                sp.wait_ge(x1_stored[b], 16 * (tiles // 2))
            sp.wait_ge(logit_done, tiles)
            load_in(Tile(0, 0), first=True)
            load_in(Tile(0, 1), first=True)
            with sp.Fori(1, tiles // 2) as it:
                load_in(Tile(it, 0))
                load_in(Tile(it, 1))
            for b in range(2):
                sp.wait_ge(sent[b], 16 * TOP_K * (tiles // 2))
            with sp.Fori(tiles // 2, ffn_tiles // 2) as it:
                load_in(Tile(it, 0))
                load_in(Tile(it, 1))

            def load_own(t):
                b = t.parity
                if t.later:
                    sp.wait_ge(sum_done, t.index - 1)
                sp.dma_start(own_sb[:, b, 0, :], row_tile(x_rows, t.index)).then_inc(own_loaded[b], 16)
                sp.dma_start(own_sb[:, b, 1, :], row_tile(y_rows, t.index)).then_inc(own_loaded[b], 16)

            for b in range(2):
                sp.wait_ge(y_stored[b], 16 * (tiles // 2))
            load_own(Tile(0, 0))
            load_own(Tile(0, 1))
            with sp.Fori(1, tiles // 2) as it:
                load_own(Tile(it, 0))
                load_own(Tile(it, 1))

        @block.gpsimd
        def _(pool):
            pool.memset(ident[:, :], 0.0).then_inc(consts_set, 1)
            pool.memset(head_block[:, :], 1.0).then_inc(consts_set, 1)
            pool.memset(head_of[:, :], 1.0).then_inc(consts_set, 1)
            pool.memset(causal[:, :], 1.0).then_inc(consts_set, 1)
            pool.memset(before[:, :], 1.0).then_inc(consts_set, 1)
            pool.memset(ones[:, :], 1.0).then_inc(consts_set, 1)
            pool.wait_ge(consts_set, 6)
            blocks = head_block[:, :].rearrange("p (h d) -> p h d", d=D)
            pool.affine_select(out=ident[:, :], in_=ident[:, :], compare_op=ALU.not_equal, fill=1.0,
                               base=0, pattern=[[-1, P]], channel_multiplier=1).then_inc(masks_set, 1)
            pool.affine_select(out=causal[:, :], in_=causal[:, :], compare_op=ALU.is_ge, fill=0.0,
                               base=0, pattern=[[1, P]], channel_multiplier=-1).then_inc(masks_set, 1)
            pool.affine_select(out=before[:, :], in_=before[:, :], compare_op=ALU.is_ge, fill=0.0,
                               base=-1, pattern=[[1, P]], channel_multiplier=-1).then_inc(masks_set, 1)
            pool.affine_select(out=blocks, in_=blocks, compare_op=ALU.is_ge, fill=0.0,
                               base=0, pattern=[[-D, hpg], [0, D]], channel_multiplier=1).then_inc(masks_set, 1)
            pool.affine_select(out=head_of[:, :], in_=head_of[:, :], compare_op=ALU.is_ge, fill=0.0,
                               base=0, pattern=[[-D, hpg]], channel_multiplier=1).then_inc(masks_set, 1)
            pool.wait_ge(masks_set, 5)
            pool.affine_select(out=blocks, in_=blocks, compare_op=ALU.is_ge, fill=0.0,
                               base=D - 1, pattern=[[D, hpg], [0, D]], channel_multiplier=-1).then_inc(masks_set, 1)
            pool.affine_select(out=head_of[:, :], in_=head_of[:, :], compare_op=ALU.is_ge, fill=0.0,
                               base=D - 1, pattern=[[D, hpg]], channel_multiplier=-1).then_inc(masks_set, 1)
            pool.memset(v_diag[:, :, :, :], 0.0).then_inc(masks_set, 1)
            pool.iota(countdown[:, :], pattern=[[-1, E]], base=E, channel_multiplier=0,
                      allow_small_or_imprecise_dtypes=True).then_inc(masks_set, 1)
            pool.iota(slot_number[:, :], pattern=[[1, slot_tiles]], base=0, channel_multiplier=0,
                      allow_small_or_imprecise_dtypes=True).then_inc(masks_set, 1)
            pool.wait_ge(masks_set, 10)
            pool.wait_ge(params_loaded, ALL_PARAMS)

            def tile_side(t):
                i, b = t.index, t.parity
                k = ktok[:, b, :]
                pool.wait_ge(norm_done, i * 2 + 2)
                wait(pool, av_done, i - 1)
                pool.tensor_tensor(k, qkn[:, b, C:2 * C], gk_sb[:, :], ALU.mult).then_inc(ktok_done, 1)
                pool.wait_ge(ktok_done, i * 3 + 1)
                pool.tensor_tensor(k, k, bk_sb[:, :], ALU.add).then_inc(ktok_done, 1)
                pool.wait_ge(ktok_done, i * 3 + 2)
                pool.tensor_tensor(k, k, k, ALU.mult).then_inc(ktok_done, 1)
                for a in range(halves):
                    pool.wait_ge(ker_done, i * 4 + a + 1)
                    wait(pool, score_mm, i * 4 - 4)
                    pool.tensor_tensor(q_diag[:, b, a, :, :],
                                       kerT[:, b, a, :].unsqueeze(1).broadcast_to([P, hpg, P]),
                                       head_of[:, :].unsqueeze(2).broadcast_to([P, hpg, P]),
                                       ALU.mult).then_inc(qexp_done, 1)
                pool.wait_ge(x_loaded[b], t.round * 32 + 32)
                wait(pool, res_done, i - 1)
                pool.tensor_tensor(xb_sb[:, b, :], x_sb[:, b, :], bo_sb[:, :], ALU.add).then_inc(xb_done, 1)
                pool.wait_ge(scan_done, i * 2 + 2)
                pool.tensor_tensor(prod[:, b, :, :], kerT[:, b, 0:halves, :], ksumT[:, b, :, :],
                                   ALU.mult).then_inc(prod_done, 1)

            tile_side(Tile(0, 0))
            tile_side(Tile(0, 1))
            with pool.Fori(1, tiles // 2) as it:
                tile_side(Tile(it, 0))
                tile_side(Tile(it, 1))

            def send(t):
                i, b = t.index, t.parity
                if t.later:
                    pool.wait_ge(sent[b], t.round * 32)
                pool.dma_start(send_sb[:, b, :], row_tile(x_rows, i)).then_inc(send_loaded[b], 16)
                pool.tensor_copy(index_sb[:, b, :],
                                 position_i[:, :, bass.ds(i, 1)].rearrange("p k n -> p (k n)")).then_inc(index_set, 1)
                wait(pool, turn_done, i)
                pool.wait_ge(index_set, i + 1)
                pool.wait_ge(send_loaded[b], t.round * 16 + 16)
                pool.tensor_tensor(turn[:, :], ones[:, 0:1], ones[:, 0:1], ALU.mult).then_inc(turn_done, 1)
                for k in range(TOP_K):
                    pool.indirect_dma_start(
                        out=x_rows, out_offset=bass.IndirectOffsetOnAxis(ap=index_sb[:, b, k:k + 1], axis=0),
                        in_=send_sb[:, b, :], in_offset=None).then_inc(sent[b], 16)

            pool.wait_ge(logit_done, tiles)
            for b in range(2):
                pool.wait_ge(x1_stored[b], 16 * (tiles // 2))
            pool.wait_ge(zero_filled, 16 * ZERO_FILLS)
            pool.wait_ge(position_done, 1)
            send(Tile(0, 0))
            send(Tile(0, 1))
            with pool.Fori(1, tiles // 2) as it:
                send(Tile(it, 0))
                send(Tile(it, 1))

            def fetch(t):
                i, b = t.index, t.parity
                wait(pool, mix_done, i * 2 - 2)
                pool.tensor_copy(gather_sb[:, b, :],
                                 position_i[:, :, bass.ds(i, 1)].rearrange("p k n -> p (k n)")).then_inc(gather_set, 1)
                pool.tensor_copy(weight_sb[:, b, :],
                                 weight[:, :, bass.ds(i, 1)].rearrange("p k n -> p (k n)")).then_inc(gather_set, 1)
                pool.wait_ge(own_loaded[b], t.round * 32 + 32)
                wait(pool, out_done, i - 1)
                pool.wait_ge(gather_set, i * 2 + 2)
                pool.tensor_tensor(sum_sb[:, b, 0, :], own_sb[:, b, 0, :], own_sb[:, b, 1, :],
                                   ALU.add).then_inc(sum_done, 1)
                for k in range(TOP_K):
                    pool.indirect_dma_start(
                        out=got_sb[:, b, k, :], out_offset=None, in_=y_rows,
                        in_offset=bass.IndirectOffsetOnAxis(ap=gather_sb[:, b, k:k + 1], axis=0)
                    ).then_inc(gathered[b], 16)

            for b in range(2):
                pool.wait_ge(y_stored[b], 16 * (ffn_tiles // 2))
            fetch(Tile(0, 0))
            fetch(Tile(0, 1))
            with pool.Fori(1, tiles // 2) as it:
                fetch(Tile(it, 0))
                fetch(Tile(it, 1))

        @block.tensor
        def _(pe):
            def qkv(t):
                i, b = t.index, t.parity
                pe.wait_ge(x_loaded[b], t.round * 32 + 32)
                wait(pe, qk_biased, i)
                for a in range(halves):
                    mm = pe.matmul(qk_ps, xT_sb[:, b, a, :], wqkv_sb[:, a, 0:2 * C], start=a == 0, stop=a == halves - 1)
                mm.then_inc(qk_mm, 1)
                wait(pe, v_ready, i)
                for a in range(halves):
                    mm = pe.matmul(v_ps, xT_sb[:, b, a, :], wqkv_sb[:, a, 2 * C:3 * C], start=a == 0, stop=a == halves - 1)
                mm.then_inc(v_mm, 1)

            def turn_qk(t):
                i, b = t.index, t.parity
                pe.wait_ge(norm_done, i * 2 + 2)
                wait(pe, ker_done, i * 4)
                for n in range(2 * halves):
                    mm = pe.transpose(qkT_ps[:, n * P:(n + 1) * P], qkn[:, b, n * P:(n + 1) * P], ident[:, :])
                mm.then_inc(qkT_mm, 1)

            def score(t):
                i, b = t.index, t.parity
                pe.wait_ge(ker_done, i * 4 + 4)
                for c in range(HEADS // 4):
                    a, h = c * 4 // hpg, c * 4 % hpg
                    pe.wait_ge(qexp_done, i * 2 + a + 1)
                    wait(pe, mask_done, i * 4 + c - 1)
                    pe.matmul(score_ps[c % 2], kerT[:, b, halves + a, :],
                              q_diag[:, b, a, h:h + 4, :].rearrange("p h t -> p (h t)"),
                              start=True, stop=True).then_inc(score_mm, 1)

            def attend(t):
                i, b = t.index, t.parity
                pe.wait_ge(mask_done, i * 4 + 4)
                pe.wait_ge(v_ready, i + 1)
                pe.wait_ge(state_ready, i + 1)
                wait(pe, attn_done, i)
                for a in range(halves):
                    pe.matmul(num_ps[:, a, :], state[:, a, :], kerT[:, b, a, :], start=True, stop=False)
                    for h in range(hpg):
                        pe.matmul(num_ps[:, a, :], v_diag[:, b, a, h * P:(h + 1) * P], scores[:, b, a * hpg + h, :],
                                  start=False, stop=h == hpg - 1)
                pe.wait_ge(prod_done, i + 1)
                for a in range(halves):
                    mm = pe.matmul(den_ps[:, a, :], head_block[:, :], prod[:, b, a, :], start=True, stop=True)
                mm.then_inc(num_mm, 1)
                pe.wait_ge(ktok_done, i * 3 + 3)
                for a in range(halves):
                    v = v_diag[:, b, a, :].rearrange("p (h n) -> p h n", n=VD)[:, :, 0:D]
                    mm = pe.matmul(state_ps[:, a, :], ktok[:, b, a * P:(a + 1) * P], v,
                                   start=False, stop=False, skip_group_check=True)
                mm.then_inc(av_done, 1)

            def project(t):
                i, b = t.index, t.parity
                pe.wait_ge(attn_done, i + 1)
                wait(pe, logit_done, i)
                for a in range(halves):
                    mm = pe.matmul(wo_ps, attnT[:, b, a, :], wo_sb[:, a, :], start=a == 0, stop=a == halves - 1)
                mm.then_inc(wo_mm, 1)

            def turn_x1(t):
                i, b = t.index, t.parity
                pe.wait_ge(x1_done, i + 1)
                wait(pe, x1T_done, i)
                for a in range(halves):
                    mm = pe.transpose(x1T_ps[:, a, :], x1_sb[:, b, a * P:(a + 1) * P], ident[:, :])
                mm.then_inc(x1T_mm, 1)

            def logit(t):
                pe.wait_ge(x1T_done, t.index + 1)
                for a in range(halves):
                    mm = pe.matmul(logit_ps, x1T_sb[:, a, :], router_sb[:, a, :], start=a == 0, stop=a == halves - 1)
                mm.then_inc(logit_mm, 1)

            def step(after, now, last):
                if after:
                    qkv(after)
                if last:
                    project(last)
                score(now)
                if after:
                    turn_qk(after)
                if last:
                    turn_x1(last)
                attend(now)
                if last:
                    logit(last)

            pe.wait_ge(masks_set, 10)
            pe.wait_ge(params_loaded, ALL_PARAMS)
            pe.wait_ge(zero_set, 1)
            pe.matmul(bank[6][:, 0:C], ffn_sb[:, ZEROED, 0:P], ffn_sb[:, ZEROED, 0:C], start=True, stop=False,
                      skip_group_check=True)
            qkv(Tile(0, 0))
            turn_qk(Tile(0, 0))
            step(Tile(0, 1), Tile(0, 0), None)
            step(Tile(0, 2), Tile(0, 1), Tile(0, 0))
            step(Tile(0, 3), Tile(0, 2), Tile(0, 1))
            with pe.Fori(1, tiles // 2 - 1) as it:
                step(Tile(it, 2), Tile(it, 1), Tile(it, 0))
                step(Tile(it, 3), Tile(it, 2), Tile(it, 1))
            END = tiles // 2 - 1
            step(None, Tile(END, 1), Tile(END, 0))
            project(Tile(END, 1))
            turn_x1(Tile(END, 1))
            logit(Tile(END, 1))

            def turn_in(t):
                i, b = t.index, t.parity
                pe.wait_ge(in_loaded[b], t.round * 16 + 16)
                wait(pe, inT_done, i)
                for a in range(halves):
                    mm = pe.transpose(inT_ps[:, a, :], in_sb[:, b, a * P:(a + 1) * P], ident[:, :])
                mm.then_inc(inT_mm, 1)

            def weights(e, at, n):
                return ffn_sb[:, bass.ds(e, 1), at:at + n].rearrange("p e n -> p (e n)")

            def gate_up(t, e):
                i, b = t.index, t.parity
                pe.wait_ge(inT_done, i + 1)
                wait(pe, h_done, i)
                for dst, at in ((gate_ps, 0), (up_ps, UP)):
                    for a in range(halves):
                        mm = pe.matmul(dst, inT_sb[:, b, a, :], weights(e, at + a * I, I),
                                       start=a == 0, stop=a == halves - 1)
                    mm.then_inc(gu_mm, 1)

            def turn_h(t):
                i = t.index
                pe.wait_ge(h_done, i + 1)
                wait(pe, hT_done, i)
                for m in range(inner):
                    mm = pe.transpose(hT_ps[:, m, :], h_sb[:, m * P:(m + 1) * P], ident[:, :])
                mm.then_inc(hT_mm, 1)

            def down(t, e):
                i, b = t.index, t.parity
                pe.wait_ge(hT_done, i + 1)
                wait(pe, y_done, i)
                for m in range(inner):
                    mm = pe.matmul(y_ps, hT_sb[:, b, m, :], weights(e, DOWN + m * C, C), start=m == 0, stop=m == inner - 1)
                mm.then_inc(y_mm, 1)

            def ffn_step(now, e, last, e_last, after=None):
                gate_up(now, e)
                if after:
                    turn_in(after)
                if last:
                    down(last, e_last)
                turn_h(now)

            pe.wait_ge(logit_done, tiles)
            pe.wait_ge(ffn_loaded, 16 * E)
            pe.wait_ge(last_loaded, 16)
            turn_in(Tile(0, 0))
            ffn_step(Tile(0, 0), SHARED, None, None, Tile(0, 1))
            pe.wait_ge(member_done, 1)
            pe.matmul(rank_ps, before[:, :], member.rearrange("p i e -> p (i e)"), start=True, stop=True).then_inc(rank_mm, 1)
            pe.matmul(total_ps, ones[:, :], member.rearrange("p i e -> p (i e)"), start=True, stop=True).then_inc(total_mm, 1)
            ffn_step(Tile(0, 1), SHARED, Tile(0, 0), SHARED, Tile(0, 2))
            ffn_step(Tile(0, 2), SHARED, Tile(0, 1), SHARED, Tile(0, 3))
            with pe.Fori(1, tiles // 2 - 1) as it:
                ffn_step(Tile(it, 1), SHARED, Tile(it, 0), SHARED, Tile(it, 2))
                ffn_step(Tile(it, 2), SHARED, Tile(it, 1), SHARED, Tile(it, 3))
            ffn_step(Tile(END, 1), SHARED, Tile(END, 0), SHARED, Tile(END, 2))
            pe.wait_ge(experts_done, 1)

            def expert(i):
                return pe.value_load(expert_i[0:1, bass.ds(i, 1)], min_val=0, max_val=E)

            with pe.Fori(tiles // 2, ffn_tiles // 2 - 1) as it:
                e = [expert(it * 2 + d) for d in (-1, 0, 1)]
                ffn_step(Tile(it, 0), e[1], Tile(it, -1), e[0], Tile(it, 1))
                ffn_step(Tile(it, 1), e[2], Tile(it, 0), e[1], Tile(it, 2))
            LAST = ffn_tiles // 2 - 1
            e = [expert(LAST * 2 + d) for d in (-1, 0, 1)]
            ffn_step(Tile(LAST, 0), e[1], Tile(LAST, -1), e[0], Tile(LAST, 1))
            ffn_step(Tile(LAST, 1), e[2], Tile(LAST, 0), e[1])
            down(Tile(LAST, 1), e[2])

        @block.scalar
        def _(act):
            def qk_std(t):
                act.wait_ge(aggr_done, t.index * 2 + 2)
                wait(act, std_eps_done, t.index)
                act.activation(std[:, :], moments[:, :, 1], ACT.Sqrt, scale=C / (C - 1)).then_inc(std_done, 1)

            def features(t):
                i, b = t.index, t.parity
                act.wait_ge(qkT_mm, i + 1)
                wait(act, av_done, i - 1)
                for n in range(2 * halves):
                    act.activation(kerT[:, b, n, :], qkT_ps[:, n * P:(n + 1) * P], ACT.Square,
                                   scale=gb_sb[:, 0, n:n + 1], bias=gb_sb[:, 1, n:n + 1]).then_inc(ker_done, 1)

            def x1_std(t):
                act.wait_ge(ln_aggr_done, t.index + 1)
                act.activation(ln_std[:, :], ln_moments[:, 1:2], ACT.Sqrt, bias=eps_ln[:, :]).then_inc(ln_std_done, 1)

            def x1_out(t):
                i, b = t.index, t.parity
                act.wait_ge(x1_done, i + 1)
                act.dma_start(row_tile(x_rows, i), x1_sb[:, b, :]).then_inc(x1_stored[b], 16)
                act.wait_ge(x1T_mm, i + 1)
                wait(act, logit_mm, i)
                act.activation(x1T_sb[:, :, :], x1T_ps, ACT.Copy).then_inc(x1T_done, 1)

            def step(after, last):
                if after:
                    qk_std(after)
                if last:
                    x1_std(last)
                if after:
                    features(after)
                if last:
                    x1_out(last)

            act.wait_ge(eps_set, 1)
            act.wait_ge(params_loaded, ALL_PARAMS)
            step(Tile(0, 0), None)
            step(Tile(0, 1), None)
            step(Tile(0, 2), Tile(0, 0))
            step(Tile(0, 3), Tile(0, 1))
            with act.Fori(1, tiles // 2 - 1) as it:
                step(Tile(it, 2), Tile(it, 0))
                step(Tile(it, 3), Tile(it, 1))
            END = tiles // 2 - 1
            step(None, Tile(END, 0))
            step(None, Tile(END, 1))

            act.wait_ge(logit_done, tiles)
            act.activation(probs, logits[:, :, :], ACT.Sigmoid).then_inc(probs_done, 1)

            def copy_in(t):
                i, b = t.index, t.parity
                act.wait_ge(inT_mm, i + 1)
                wait(act, gu_mm, i * 2 - 2)
                act.activation(inT_sb[:, b, :, :], inT_ps, ACT.Copy).then_inc(inT_done, 1)

            def silu(t):
                i = t.index
                act.wait_ge(gu_mm, i * 2 + 1)
                wait(act, h_done, i)
                act.activation(silu_sb, gate_ps, ACT.Silu).then_inc(silu_done, 1)

            def store_y(t):
                i, b = t.index, t.parity
                act.wait_ge(y_mm, i + 1)
                if t.later:
                    act.wait_ge(y_stored[b], t.round * 16)
                act.activation(y_sb[:, b, :], y_ps, ACT.Copy).then_inc(y_done, 1)
                act.wait_ge(y_done, i + 1)
                act.dma_start(row_tile(y_rows, i), y_sb[:, b, :]).then_inc(y_stored[b], 16)

            def ffn_step(now, after, last):
                silu(now)
                if after:
                    copy_in(after)
                if last:
                    store_y(last)

            copy_in(Tile(0, 0))
            ffn_step(Tile(0, 0), Tile(0, 1), None)
            ffn_step(Tile(0, 1), Tile(0, 2), Tile(0, 0))
            ffn_step(Tile(0, 2), Tile(0, 3), Tile(0, 1))
            with act.Fori(1, ffn_tiles // 2 - 1) as it:
                ffn_step(Tile(it, 1), Tile(it, 2), Tile(it, 0))
                ffn_step(Tile(it, 2), Tile(it, 3), Tile(it, 1))
            LAST = ffn_tiles // 2 - 1
            ffn_step(Tile(LAST, 1), None, Tile(LAST, 0))
            store_y(Tile(LAST, 1))

            def finish(t):
                i, b = t.index, t.parity
                act.wait_ge(f_aggr_done, i + 1)
                wait(act, f_inv_done, i - 1)
                act.activation(f_std[:, b, :], f_moments[:, b, 1:2], ACT.Sqrt, bias=eps_ln[:, :]).then_inc(f_std_done, 1)
                act.wait_ge(out_done, i + 1)
                act.dma_start(row_tile(out, i), out_sb[:, b, :]).then_inc(out_stored[b], 16)

            finish(Tile(0, 0))
            finish(Tile(0, 1))
            with act.Fori(1, tiles // 2) as it:
                finish(Tile(it, 0))
                finish(Tile(it, 1))
            for b in range(2):
                act.wait_ge(out_stored[b], 16 * (tiles // 2))

        @block.vector
        def _(dve):
            def bias(t):
                i, b = t.index, t.parity
                dve.wait_ge(qk_mm, i + 1)
                wait(dve, norm_done, i * 2)
                dve.tensor_tensor(qk_sb[:, :], qk_ps, bqkv_sb[:, 0:2 * C], ALU.add).then_inc(qk_biased, 1)
                wait(dve, aggr_done, i * 2)
                dve.wait_ge(qk_biased, i + 1)
                for n in range(2):
                    dve.bn_stats(stats[:, n, :], qk_sb[:, n * C:(n + 1) * C]).then_inc(stats_done, 1)
                dve.wait_ge(v_mm, i + 1)
                wait(dve, av_done, i - 1)
                dve.wait_ge(stats_done, i * 2 + 2)
                dve.tensor_tensor(
                    v_diag[:, b, :, :].rearrange("p a (h n) -> p a h n", n=VD)[:, :, :, 0:D],
                    v_ps.rearrange("p (a h d) -> p a h d", a=halves, d=D),
                    bqkv_sb[:, 2 * C:3 * C].rearrange("p (a h d) -> p a h d", a=halves, d=D),
                    ALU.add).then_inc(v_ready, 1)
                for n in range(2):
                    dve.bn_aggr(moments[:, n, :], stats[:, n, :]).then_inc(aggr_done, 1)

            def normalise(t):
                i, b = t.index, t.parity
                dve.wait_ge(std_done, i + 1)
                dve.tensor_scalar(std_eps[:, :], std[:, :], EPS_ATTN, None, ALU.add).then_inc(std_eps_done, 1)
                dve.wait_ge(std_eps_done, i + 1)
                dve.reciprocal(inv_std[:, :], std_eps[:, :]).then_inc(inv_std_done, 1)
                dve.wait_ge(inv_std_done, i + 1)
                wait(dve, qkT_mm, i - 1)
                wait(dve, ktok_done, i * 3 - 3)
                for n in range(2):
                    dve.tensor_scalar(qkn[:, b, n * C:(n + 1) * C], qk_sb[:, n * C:(n + 1) * C],
                                      moments[:, n, 0:1], inv_std[:, n:n + 1],
                                      ALU.subtract, ALU.mult).then_inc(norm_done, 1)

            def mask(t, groups, last=None):
                i, b = t.index, t.parity
                if last:
                    dve.wait_ge(ln_stats_done, last.index + 1)
                wait(dve, av_done, i - 1)
                for c in groups:
                    dve.wait_ge(score_mm, i * 4 + c + 1)
                    dve.tensor_tensor(scores[:, b, 4 * c:4 * c + 4, :],
                                      score_ps[c % 2].rearrange("p (h t) -> p h t", t=P),
                                      causal[:, :].unsqueeze(1).broadcast_to([P, 4, P]), ALU.mult).then_inc(mask_done, 1)

            def key_sums(t):
                i, b = t.index, t.parity
                dve.wait_ge(ker_done, i * 4 + 4)
                wait(dve, prod_done, i - 1)
                for a in range(halves):
                    wait(dve, scan_done, i * 2)
                    dve.tensor_tensor_scan(ksumT[:, b, a, :], ones[:, :], kerT[:, b, halves + a, :],
                                           ksumT[:, 1 - b, a, P - 1:P], ALU.mult, ALU.add).then_inc(scan_done, 1)

            def attn_out(t):
                i, b = t.index, t.parity
                dve.wait_ge(num_mm, i + 1)
                wait(dve, attn_done, i)
                dve.tensor_scalar(den[:, :, :], den_ps, EPS_ATTN, None, ALU.add).then_inc(den_done, 1)
                dve.wait_ge(den_done, i + 1)
                dve.reciprocal(den[:, :, :], den[:, :, :]).then_inc(inv_den_done, 1)
                dve.wait_ge(inv_den_done, i + 1)
                wait(dve, wo_mm, i - 1)
                dve.tensor_tensor(attnT[:, b, :, :], num_ps, den[:, :, :], ALU.mult).then_inc(attn_done, 1)
                dve.wait_ge(av_done, i + 1)
                dve.tensor_tensor(state[:, :, :], state_ps,
                                  head_block[:, :].unsqueeze(1).broadcast_to([P, halves, P]),
                                  ALU.mult).then_inc(state_ready, 1)

            def residual(t):
                i, b = t.index, t.parity
                dve.wait_ge(wo_mm, i + 1)
                dve.wait_ge(xb_done, i + 1)
                wait(dve, x1_done, i)
                dve.tensor_tensor(res[:, :], wo_ps, xb_sb[:, b, :], ALU.add).then_inc(res_done, 1)
                dve.wait_ge(res_done, i + 1)
                wait(dve, ln_aggr_done, i)
                dve.bn_stats(ln_stats[:, :], res[:, :]).then_inc(ln_stats_done, 1)

            def ln_moments_of(t):
                dve.bn_aggr(ln_moments[:, :], ln_stats[:, :]).then_inc(ln_aggr_done, 1)

            def make_x1(t):
                i, b = t.index, t.parity
                dve.wait_ge(ln_std_done, i + 1)
                dve.reciprocal(ln_inv[:, :], ln_std[:, :]).then_inc(ln_inv_done, 1)
                dve.wait_ge(ln_inv_done, i + 1)
                if t.later:
                    dve.wait_ge(x1_stored[b], t.round * 16)
                    dve.wait_ge(x1T_mm, i - 1)
                dve.tensor_scalar(x1_sb[:, b, :], res[:, :], ln_moments[:, 0:1], ln_inv[:, 0:1],
                                  ALU.subtract, ALU.mult).then_inc(x1_done, 1)

            def logit_out(t):
                i = t.index
                dve.wait_ge(logit_mm, i + 1)
                dve.tensor_tensor(logits[:, bass.ds(i, 1), :].rearrange("p n e -> p (n e)"), logit_ps, rbias_sb[:, :],
                                  ALU.add).then_inc(logit_done, 1)

            def step(after, now, last):
                if after:
                    bias(after)
                if last:
                    residual(last)
                mask(now, (0,), last)
                if last:
                    ln_moments_of(last)
                mask(now, (1,))
                if after:
                    normalise(after)
                mask(now, (2, 3))
                if last:
                    make_x1(last)
                if after:
                    key_sums(after)
                attn_out(now)
                if last:
                    logit_out(last)

            dve.memset(ffn_sb[:, ZEROED, :], 0.0).then_inc(zero_set, 1)
            dve.memset(eps_ln[:, :], EPS_LN).then_inc(eps_set, 1)
            dve.memset(state[:, :, :], 0.0).then_inc(state_ready, 1)
            dve.memset(ksumT[:, 1, :, :], 0.0).then_inc(sums_zeroed, 1)
            dve.wait_ge(sums_zeroed, 1)
            dve.wait_ge(masks_set, 10)
            dve.wait_ge(params_loaded, ALL_PARAMS)
            bias(Tile(0, 0))
            normalise(Tile(0, 0))
            key_sums(Tile(0, 0))
            step(Tile(0, 1), Tile(0, 0), None)
            step(Tile(0, 2), Tile(0, 1), Tile(0, 0))
            step(Tile(0, 3), Tile(0, 2), Tile(0, 1))
            with dve.Fori(1, tiles // 2 - 1) as it:
                step(Tile(it, 2), Tile(it, 1), Tile(it, 0))
                step(Tile(it, 3), Tile(it, 2), Tile(it, 1))
            END = tiles // 2 - 1
            step(None, Tile(END, 1), Tile(END, 0))
            residual(Tile(END, 1))
            dve.wait_ge(ln_stats_done, tiles)
            ln_moments_of(Tile(END, 1))
            make_x1(Tile(END, 1))
            logit_out(Tile(END, 1))

            chained = [0]

            def link(ins):
                chained[0] += 1
                ins.then_inc(route, 1)
                dve.wait_ge(route, chained[0])

            def over_experts(x):
                return x.unsqueeze(2).broadcast_to([P, tiles, E])

            def over_tiles(x):
                return x.unsqueeze(1).broadcast_to([P, tiles, E])

            def pick(onehot, values, best):
                link(dve.tensor_reduce(best, values, AX_X, ALU.max))
                link(dve.tensor_tensor(is_top, values, over_experts(best), ALU.is_equal))
                link(dve.tensor_tensor(picked, is_top, over_tiles(countdown[:, :]), ALU.mult))
                link(dve.tensor_reduce(first, picked, AX_X, ALU.max))
                link(dve.tensor_tensor(onehot, over_tiles(countdown[:, :]), over_experts(first), ALU.is_equal))

            dve.wait_ge(logit_done, tiles)
            dve.wait_ge(probs_done, 1)
            pick(onehot1, probs, max1)
            link(dve.scalar_tensor_tensor(out=rest, in0=onehot1, scalar=-4.0, in1=probs, op0=ALU.mult, op1=ALU.add))
            pick(onehot2, rest, max2)
            dve.tensor_tensor(member, onehot1, onehot2, ALU.add).then_inc(member_done, 1)

            def hidden(t):
                i = t.index
                dve.wait_ge(silu_done, i + 1)
                dve.wait_ge(gu_mm, i * 2 + 2)
                wait(dve, hT_mm, i)
                dve.tensor_tensor(h_sb, up_ps, silu_sb, ALU.mult).then_inc(h_done, 1)

            def copy_h(t):
                i, b = t.index, t.parity
                dve.wait_ge(hT_mm, i + 1)
                wait(dve, y_mm, i - 1)
                dve.tensor_copy(hT_sb[:, b, :, :], hT_ps).then_inc(hT_done, 1)

            def ffn_step(t):
                hidden(t)
                copy_h(t)

            ffn_step(Tile(0, 0))

            link(dve.tensor_tensor(p_sum, max1, max2, ALU.add))
            link(dve.reciprocal(p_inv, p_sum))
            link(dve.tensor_tensor(weight[:, 0, :], max1, p_inv, ALU.mult))
            link(dve.tensor_tensor(weight[:, 1, :], max2, p_inv, ALU.mult))
            link(dve.memset(reset_by_expert, 1.0))
            link(dve.memset(reset_by_expert[:, :, 0:1], 0.0))
            dve.wait_ge(total_mm, 1)
            link(dve.tensor_copy(totals_by_expert, total_ps.rearrange("p (i e) -> p e i", e=E)))
            link(dve.tensor_tensor_scan(flat(running_by_expert), flat(reset_by_expert), flat(totals_by_expert), 0.0,
                                        ALU.mult, ALU.add))
            link(dve.tensor_scalar(tile_n, running_by_expert[:, :, tiles - 1], float(P - 1), None, ALU.add))
            link(dve.tensor_scalar(tile_n, tile_n, P.bit_length() - 1, None, ALU.arith_shift_right))
            link(dve.tensor_copy(tile_f, tile_n))
            link(dve.tensor_tensor_scan(tile_end, ones[:, 0:E], tile_f, 0.0, ALU.mult, ALU.add))
            link(dve.tensor_tensor(slot_base, tile_end, tile_f, ALU.subtract))
            link(dve.tensor_scalar(slot_base, slot_base, float(P), float(tiles * P), ALU.mult, ALU.add))
            link(dve.tensor_tensor(position, running_by_expert.rearrange("p e i -> p i e"),
                                   totals_by_expert.rearrange("p e i -> p i e"), ALU.subtract))
            link(dve.tensor_tensor(position, position, over_tiles(slot_base), ALU.add))
            link(dve.tensor_tensor(position, rank_ps.rearrange("p (i e) -> p i e", e=E), position, ALU.add))
            for k, onehot in enumerate((onehot1, onehot2)):
                link(dve.tensor_tensor(picked, position, onehot, ALU.mult))
                link(dve.tensor_reduce(position_f[:, k, :], picked, AX_X, ALU.add))
            dve.tensor_copy(position_i, position_f).then_inc(position_done, 1)
            link(dve.tensor_tensor(expert_cmp,
                                   slot_number[0:1, :].unsqueeze(2).broadcast_to([1, slot_tiles, E]),
                                   tile_end[0:1, :].unsqueeze(1).broadcast_to([1, slot_tiles, E]), ALU.is_ge))
            link(dve.tensor_reduce(expert_f, expert_cmp, AX_X, ALU.add))
            link(dve.memset(expert_i[:, 0:tiles], SHARED))
            dve.tensor_scalar(expert_i[:, tiles:], expert_f, float(E - 1), None, ALU.min).then_inc(experts_done, 1)

            ffn_step(Tile(0, 1))
            with dve.Fori(1, ffn_tiles // 2) as it:
                ffn_step(Tile(it, 0))
                ffn_step(Tile(it, 1))

            def mix(t):
                i, b = t.index, t.parity
                dve.wait_ge(gathered[b], t.round * 32 + 32)
                dve.wait_ge(gather_set, i * 2 + 2)
                dve.wait_ge(sum_done, i + 1)
                dve.scalar_tensor_tensor(out=sum_sb[:, b, 1, :], in0=got_sb[:, b, 0, :], scalar=weight_sb[:, b, 0:1],
                                         in1=sum_sb[:, b, 0, :], op0=ALU.mult, op1=ALU.add).then_inc(mix_done, 1)
                dve.wait_ge(mix_done, i * 2 + 1)
                dve.scalar_tensor_tensor(out=sum_sb[:, b, 0, :], in0=got_sb[:, b, 1, :], scalar=weight_sb[:, b, 1:2],
                                         in1=sum_sb[:, b, 1, :], op0=ALU.mult, op1=ALU.add).then_inc(mix_done, 1)
                dve.wait_ge(mix_done, i * 2 + 2)
                wait(dve, f_aggr_done, i)
                dve.bn_stats(ln_stats[:, :], sum_sb[:, b, 0, :]).then_inc(f_stats_done, 1)

            def moments_of(t):
                dve.bn_aggr(f_moments[:, t.parity, :], ln_stats[:, :]).then_inc(f_aggr_done, 1)

            def make_out(t, following=None):
                i, b = t.index, t.parity
                dve.wait_ge(f_std_done, i + 1)
                wait(dve, out_done, i)
                if following:
                    dve.wait_ge(f_stats_done, following.index + 1)
                dve.reciprocal(ln_inv[:, :], f_std[:, b, :]).then_inc(f_inv_done, 1)
                dve.wait_ge(f_inv_done, i + 1)
                if t.later:
                    dve.wait_ge(out_stored[b], t.round * 16)
                dve.tensor_scalar(out_sb[:, b, :], sum_sb[:, b, 0, :], f_moments[:, b, 0:1], ln_inv[:, 0:1],
                                  ALU.subtract, ALU.mult).then_inc(out_done, 1)

            def last_step(t, before):
                mix(t)
                make_out(before, t)
                moments_of(t)

            mix(Tile(0, 0))
            dve.wait_ge(f_stats_done, 1)
            moments_of(Tile(0, 0))
            last_step(Tile(0, 1), Tile(0, 0))
            with dve.Fori(1, tiles // 2) as it:
                last_step(Tile(it, 0), Tile(it, -1))
                last_step(Tile(it, 1), Tile(it, 0))
            make_out(Tile(END, 1))


def kernel(L0_attn_x, L0_attn_Wqkv, L0_attn_bqkv, L0_attn_gamma_q, L0_attn_beta_q, L0_attn_gamma_k,
           L0_attn_beta_k, L0_attn_Wo, L0_attn_bo, L0_ffn_sg_w, L0_ffn_su_w, L0_ffn_sd_w, L0_ffn_router_w,
           L0_ffn_routing_bias, L0_ffn_wg, L0_ffn_wu, L0_ffn_wd):
    import numpy as np
    import concourse.bacc as bacc
    from concourse.bass_utils import run_bass_kernel_spmd

    x = np.asarray(L0_attn_x)
    B, T, C = x.shape
    tiles, halves = B * T // P, C // P
    E = L0_ffn_wg.shape[0]
    slot_tiles = tiles * TOP_K + E

    def by_feature(w):
        return np.asarray(w).reshape(-1, P, w.shape[1]).transpose(1, 0, 2)

    def expert_rows(gate, up, down):
        return np.concatenate([by_feature(np.asarray(w).T).reshape(P, -1) for w in (gate, up, down)], axis=1)

    rows = x.reshape(tiles, P, C)
    columns = [np.asarray(v).reshape(halves, P).T
               for v in (L0_attn_gamma_q, L0_attn_gamma_k, L0_attn_beta_q, L0_attn_beta_k)]
    arrays = {
        "xT": rows.reshape(tiles, P, halves, P).transpose(0, 3, 2, 1),
        "x": rows,
        "wqkv": by_feature(L0_attn_Wqkv),
        "bqkv": L0_attn_bqkv,
        "gb_cols": np.stack(columns, axis=1).reshape(P, 2, 2 * halves),
        "gk_row": L0_attn_gamma_k,
        "bk_row": L0_attn_beta_k,
        "wo": by_feature(L0_attn_Wo),
        "bo": L0_attn_bo,
        "router": by_feature(np.asarray(L0_ffn_router_w).T),
        "router_bias": L0_ffn_routing_bias,
        "ffn_w": np.stack([expert_rows(L0_ffn_wg[e], L0_ffn_wu[e], L0_ffn_wd[e]) for e in range(E)]
                          + [expert_rows(L0_ffn_sg_w, L0_ffn_su_w, L0_ffn_sd_w)]),
    }
    arrays = {name: np.ascontiguousarray(a) for name, a in arrays.items()}
    nc = bacc.Bacc("TRN2", target_bir_lowering=False, num_devices=1)
    ins = {name: nc.dram_tensor(name, a.shape, F32, kind="ExternalInput").ap() for name, a in arrays.items()}
    out = nc.dram_tensor("out", (tiles * P, C), F32, kind="ExternalOutput").ap()
    x_rows = nc.dram_tensor("x_rows", ((tiles + slot_tiles) * P, C), F32, kind="Internal").ap()
    y_rows = nc.dram_tensor("y_rows", ((tiles + slot_tiles) * P, C), F32, kind="Internal").ap()
    post_ln_block(nc, **ins, out=out, x_rows=x_rows, y_rows=y_rows)
    got = run_bass_kernel_spmd(nc, [arrays], core_ids=[0])
    return got.results[0]["out"].reshape(B, T, C)
```

```python
from contextlib import ExitStack

import concourse.bass as bass
from concourse import mybir

ALU = mybir.AluOpType
ACT = mybir.ActivationFunctionType
AX_X = mybir.AxisListType.X
F32 = mybir.dt.float32
F32R = mybir.dt.float32r
I32 = mybir.dt.int32

P = 128
HEADS = 16
D = 16
EPS_LN = 1e-5
EPS_ATTN = 1e-6
TOP_K = 2


class Tile:

    def __init__(self, it, d, buffers=2):
        self.index = it * buffers + d
        self.round = it + d // buffers
        self.parity = d % buffers
        self.later = not isinstance(self.round, int) or self.round > 0


def wait(eng, sem, value):
    if not isinstance(value, int) or value > 0:
        eng.wait_ge(sem, value)


def post_ln_block(nc, xT, x, wqkv, bqkv, gb_cols, gk_row, bk_row, wo, bo, router, router_bias, ffn_w,
                  out, x1_rows, sum_rows, slot_rows, slot_y):
    tiles, _, C = x.shape
    halves = C // P
    hpg = P // D
    E = ffn_w.shape[0] - 1
    I = ffn_w.shape[2] // (3 * halves)
    inner = I // P
    GU, DN = 2 * halves * I, inner * C
    CHUNK = GU // 2
    slot_tiles = slot_rows.shape[0] // P
    ffn_tiles = tiles + slot_tiles
    early = tiles // 2 + 2
    routed_end = early + slot_tiles
    pairs = tiles // 2
    quads = tiles // 4
    assert slot_tiles >= tiles * TOP_K + E - 1 and slot_tiles % 2 == 0 and tiles % 4 == 0
    assert 2 * E <= early - 2
    TE = tiles * E
    VH = 2 * D
    VB = 3 * VH

    with ExitStack() as ctx:
        def sb(name, shape, dt=F32, stack=ctx, partitions=P):
            return stack.enter_context(nc.sbuf_tensor(name, [partitions, *shape], dt))

        def sem(name):
            return ctx.enter_context(nc.semaphore(name))

        psum = ctx.enter_context(nc.psum_tensor("psum", [P, 8, 512], F32))
        bank = [psum[:, n, :] for n in range(8)]
        qk_ps = qkT_ps = bank[0]
        score_ps = psum[:, 1:5, :]
        num_ps = bank[5][:, 0:C].rearrange("p (a t) -> p a t", a=halves)
        den_ps = bank[5][:, C:2 * C].rearrange("p (a t) -> p a t", a=halves)
        state_ps = bank[6][:, 0:halves * VH].rearrange("p (a d) -> p a d", a=halves)
        wo_ps, v_ps = bank[7][:, 0:C], bank[7][:, C:2 * C]
        x1T_ps = wo_ps.rearrange("p (a t) -> p a t", a=halves)
        logitT_ps = bank[7][0:E, C:C + P]
        logits_ps, rank_ps, total_ps = bank[5][:, 0:TE], bank[6][:, 0:TE], bank[7][:, 0:TE]
        gate_ps, up_ps = bank[0], bank[1]
        inT_ps = bank[2][:, 0:C].rearrange("p (a t) -> p a t", a=halves)
        hT_ps = bank[3].rearrange("p (m t) -> p m t", m=inner)
        y_ps = bank[4][:, 0:C]

        ident = sb("ident", [P])
        ones = sb("ones", [P])
        before = sb("before", [P])
        eps_ln = sb("eps_ln", [1])
        eps_attn = sb("eps_attn", [1])
        countdown = sb("countdown", [E])
        slot_number = sb("slot_number", [slot_tiles])
        router_bias_sb = sb("router_bias_sb", [1], partitions=E)
        weight = sb("weight", [TOP_K, tiles])
        position_i = sb("position_i", [TOP_K, tiles], I32)
        expert_i = sb("expert_i", [slot_tiles], I32, partitions=1)
        index_sb = sb("index_sb", [2, TOP_K, 4], I32)
        weight_sb = sb("weight_sb", [2, TOP_K, 4])
        turn = sb("turn", [1])
        carried = sb("carried", [2])
        f_stats = sb("f_stats", [4, 6])
        f_moments = sb("f_moments", [2, 4, 2])
        f_std = sb("f_std", [2, 4])
        f_inv = sb("f_inv", [2, 4])
        f_shift = sb("f_shift", [2, 4])
        down_sb = sb("down_sb", [E + 1, DN])
        send_sb = sb("send_sb", [2, 2, C])
        with ExitStack() as place:
            ZERO_TILES = 12
            zero_rows = sb("zero_rows", [ZERO_TILES * C], stack=place)
        in_sb = sb("in_sb", [2, C])
        in_hi = sb("in_hi", [2, halves, P], F32R)
        in_lo = sb("in_lo", [2, halves, P], F32R)
        h_sb = sb("h_sb", [I])
        hT_sb = sb("hT_sb", [inner, P])
        y_sb = sb("y_sb", [2, C])
        add_sb = sb("add_sb", [2, C])
        with ExitStack() as place:
            shared_raw = sb("shared_raw", [2, CHUNK], stack=place)
        shared_lo = sb("shared_lo", [2, CHUNK], F32R)
        shared_hi = sb("shared_hi", [2, CHUNK], F32R)
        with ExitStack() as place:
            def at(name, shape, dt=F32, partitions=P):
                return sb(name, shape, dt, place, partitions)

            wqkv_sb = at("wqkv_sb", [halves, 3 * C])
            wo_sb = at("wo_sb", [halves, C])
            router_sb = at("router_sb", [halves, E])
            bqkv_sb = at("bqkv_sb", [3 * C])
            bo_sb = at("bo_sb", [C])
            gk_sb = at("gk_sb", [C])
            bk_sb = at("bk_sb", [C])
            gb_sb = at("gb_sb", [2, 2 * halves])
            head_block = at("head_block", [P])
            head_of_pair = at("head_of_pair", [2])
            causal = at("causal", [P])
            xT_sb = at("xT_sb", [2, halves, P])
            x_sb = at("x_sb", [2, C])
            xb_sb = at("xb_sb", [2, C])
            qk_sb = at("qk_sb", [2 * C])
            stats = at("stats", [2, 6])
            moments = at("moments", [2, 2])
            std = at("std", [2])
            std_eps = at("std_eps", [2])
            inv_std = at("inv_std", [2])
            shift = at("shift", [2])
            qkn = at("qkn", [2, 2 * C])
            kerT = at("kerT", [2, 2 * halves, P])
            ksumT = at("ksumT", [2, halves, P])
            prod = at("prod", [2, halves, P])
            k_affine = at("k_affine", [2, C])
            ktok = at("ktok", [2, C])
            q_pair = at("q_pair", [2, halves, 2, P])
            v_raw = at("v_raw", [C])
            v_pair = at("v_pair", [2, HEADS // 2, VB])
            scores = at("scores", [2, HEADS, P])
            state = at("state", [halves, VH])
            den = at("den", [halves, P])
            inv_den = at("inv_den", [halves, P])
            attnT = at("attnT", [2, halves, P])
            res = at("res", [C])
            ln_stats = at("ln_stats", [6])
            ln_moments = at("ln_moments", [2])
            ln_std = at("ln_std", [1])
            ln_inv = at("ln_inv", [1])
            x1_sb = at("x1_sb", [2, C])
            x1T_sb = at("x1T_sb", [halves, P])
        with ExitStack() as place:
            sb("weights_place", [3 * E * CHUNK], stack=place)
            logitsT = sb("logitsT", [tiles * P], stack=place, partitions=E)
            routing = sb("routing", [E * CHUNK - tiles * P], stack=place)
        assert tiles * P <= 4 * CHUNK
        used = [0]

        def room(*shape):
            n, start = 1, used[0]
            for x in shape:
                n *= x
            used[0] += n
            flat_room = routing[:, start:start + n]
            return flat_room.rearrange("p (a b) -> p a b", b=shape[1]) if len(shape) > 1 else flat_room

        def flat(ap):
            return ap.rearrange("p a b -> p (a b)")

        probs, is_top, rest, onehot1, onehot2, member, position, picked = (room(tiles, E) for _ in range(8))
        totals_by_expert, running_by_expert, reset_by_expert = (room(E, tiles) for _ in range(3))
        max1, max2, first, p_sum, p_inv = (room(tiles) for _ in range(5))
        position_f = room(TOP_K, tiles)
        tile_n = room(E).bitcast(I32)
        tile_f, tile_end, slot_base = (room(E) for _ in range(3))
        expert_cmp = room(slot_tiles, E)[0:1]
        expert_f = room(slot_tiles)[0:1]
        with ExitStack() as place:
            own_sb = sb("own_sb", [2, 4, C], stack=place)
            got_sb = sb("got_sb", [2, TOP_K, 4, C], stack=place)
            out_sb = sb("out_sb", [2, 4, C], stack=place)
        with ExitStack() as place:
            raw = []
            for what in ("gate", "up"):
                sb(what + "_hi_place", [E * CHUNK], stack=place)
                raw.append(sb(what + "_raw", [E, CHUNK], stack=place))
        gate_hi, gate_lo, up_hi, up_lo = (sb(name, [E, CHUNK], F32R) for name in ("gate_hi", "gate_lo", "up_hi", "up_lo"))
        high, low = (gate_hi, up_hi), (gate_lo, up_lo)
        GATE, UP = 0, 1

        names = """consts_set masks_set wqkv_loaded params_loaded gu_loaded zero_set zero_filled down_loaded hi_done lo_done
            qk_mm v_mm qk_biased v_copied v_ready stats_done qk_carry_done aggr_done std_done std_eps_done inv_std_done shift_done norm_done
            qkT_mm ker_done qexp_done scan_done prod_done affine_done ktok_done score_mm mask_done num_mm av_done
            den_done inv_den_done attn_done state_ready wo_mm xb_done res_done ln_stats_done ln_carry_done ln_aggr_done
            ln_std_done ln_inv_done x1_done x1T_mm x1T_done logit_mm logit_done
            eps_set sums_zeroed logitsT_mm probs_done route member_done rank_mm total_mm position_done experts_done
            index_set turn_done inT_mm in_hi_done in_lo_done gu_mm silu_done h_done hT_mm hT_done y_mm y_done
            gather_set f_turn_done mix_done f_stats_done f_aggr_done f_std_done f_inv_done f_shift_done out_done"""
        s = {n: sem(n) for n in names.split()}
        (consts_set, masks_set, wqkv_loaded, params_loaded, gu_loaded, zero_set, zero_filled, down_loaded, hi_done, lo_done,
         qk_mm, v_mm, qk_biased, v_copied, v_ready, stats_done, qk_carry_done, aggr_done, std_done, std_eps_done, inv_std_done, shift_done,
         norm_done,
         qkT_mm, ker_done, qexp_done, scan_done, prod_done, affine_done, ktok_done, score_mm, mask_done, num_mm,
         av_done,
         den_done, inv_den_done, attn_done, state_ready, wo_mm, xb_done, res_done, ln_stats_done, ln_carry_done, ln_aggr_done,
         ln_std_done, ln_inv_done, x1_done, x1T_mm, x1T_done, logit_mm, logit_done,
         eps_set, sums_zeroed, logitsT_mm, probs_done, route, member_done, rank_mm, total_mm, position_done,
         experts_done,
         index_set, turn_done, inT_mm, in_hi_done, in_lo_done, gu_mm, silu_done, h_done, hT_mm, hT_done, y_mm, y_done,
         gather_set, f_turn_done, mix_done, f_stats_done, f_aggr_done, f_std_done, f_inv_done, f_shift_done, out_done) = s.values()
        xT_loaded = [sem(f"xT_loaded{b}") for b in range(2)]
        x_loaded = [sem(f"x_loaded{b}") for b in range(2)]
        x1_stored = [sem(f"x1_stored{b}") for b in range(2)]
        send_loaded = [sem(f"send_loaded{b}") for b in range(2)]
        sent = [sem(f"sent{b}") for b in range(2)]
        in_loaded = [sem(f"in_loaded{b}") for b in range(2)]
        add_loaded = [sem(f"add_loaded{b}") for b in range(2)]
        y_stored = [sem(f"y_stored{b}") for b in range(2)]
        own_loaded = [sem(f"own_loaded{b}") for b in range(2)]
        gathered = [sem(f"gathered{b}") for b in range(2)]
        out_stored = [sem(f"out_stored{b}") for b in range(2)]

        params = [(gb_sb[:, :, :], gb_cols), (bqkv_sb[:, :], bqkv.partition_broadcast(P)),
                  (gk_sb[:, :], gk_row.partition_broadcast(P)), (bk_sb[:, :], bk_row.partition_broadcast(P)),
                  (bo_sb[:, :], bo.partition_broadcast(P)), (wo_sb[:, :, :], wo), (router_sb[:, :, :], router),
                  (router_bias_sb[:, :], router_bias.rearrange("(e n) -> e n", n=1))]
        ALL_PARAMS = 16 * len(params)
        ZERO_FILLS = slot_tiles // ZERO_TILES
        assert ZERO_FILLS * ZERO_TILES == slot_tiles
        MASKS = 11
        GOT = 16 * 4 * TOP_K
        SENT = 16 * 2 * TOP_K

        def v_view(ap):
            return ap.rearrange("p j (r c) -> p j r c", r=2)[:, :, :, 0:D]

        def row_tiles(dram, n, count):
            return dram.rearrange("(n j p) c -> n p j c", p=P, j=count)[bass.ds(n, 1)].rearrange("n p j c -> p (n j) c")

        def row_tile(dram, n):
            return dram.rearrange("(n p) c -> n p c", p=P)[bass.ds(n, 1), :, :].rearrange("n p c -> p (n c)")

        block = ctx.enter_context(nc.Block())

        @block.sync
        def _(sp):
            def load_xT(t, wait_free=True):
                if wait_free:
                    sp.wait_ge(v_mm, t.index - 1)
                sp.dma_start(xT_sb[:, t.parity, :, :], xT[bass.ds(t.index, 1)].rearrange("n p a t -> p (n a) t")
                             ).then_inc(xT_loaded[t.parity], 16)

            def load_x(t, wait_free=True):
                if wait_free:
                    sp.wait_ge(xb_done, t.index - 1)
                sp.dma_start(x_sb[:, t.parity, :], x[bass.ds(t.index, 1)].rearrange("n p c -> p (n c)")
                             ).then_inc(x_loaded[t.parity], 16)

            load_xT(Tile(0, 0), False)
            sp.dma_start(wqkv_sb[:, :, :], wqkv).then_inc(wqkv_loaded, 16)
            load_xT(Tile(0, 1), False)
            for dst, src in params:
                sp.dma_start(dst, src).then_inc(params_loaded, 16)
            load_x(Tile(0, 0), False)
            load_x(Tile(0, 1), False)
            with sp.Fori(1, tiles // 2) as it:
                for d in range(2):
                    load_xT(Tile(it, d))
                    load_x(Tile(it, d))

            def load_in(t, rows, n, wait_free=True):
                if wait_free:
                    sp.wait_ge(inT_mm, t.index - 1)
                sp.dma_start(in_sb[:, t.parity, :], row_tile(rows, n)).then_inc(in_loaded[t.parity], 16)

            def load_add(t, n, wait_free=True):
                if wait_free:
                    sp.wait_ge(y_done, t.index - 1)
                sp.dma_start(add_sb[:, t.parity, :], row_tile(x1_rows, n)).then_inc(add_loaded[t.parity], 16)

            def load_send(u):
                wait(sp, sent[u.parity], u.round * SENT)
                sp.dma_start(send_sb[:, u.parity, :, :], row_tiles(x1_rows, u.index, 2)).then_inc(send_loaded[u.parity], 16)

            for b in range(2):
                sp.wait_ge(x1_stored[b], 16 * (tiles // 2))
            sp.wait_ge(zero_filled, 16 * ZERO_FILLS)
            for n in range(2):
                load_in(Tile(0, n), x1_rows, n, False)
            for n in range(2):
                load_send(Tile(0, n))
                load_add(Tile(0, n), n, False)
                load_in(Tile(0, n + 2), x1_rows, n + 2)
            with sp.Fori(1, pairs // 2) as it:
                for d in range(2):
                    load_send(Tile(it, d))
                    load_add(Tile(it, d), Tile(it, d).index)
                    load_in(Tile(it, d + 2), x1_rows, Tile(it, d + 2).index)
            assert early == pairs + 2
            for n in range(pairs, early):
                load_add(Tile(0, n), n)
            for b in range(2):
                sp.wait_ge(sent[b], SENT * (pairs // 2))
            with sp.Fori(early // 2, routed_end // 2) as it:
                for d in range(2):
                    t = Tile(it, d)
                    load_in(t, slot_rows, t.index - early)

            def load_own(q):
                wait(sp, out_done, q * 4 - 4)
                for b in range(2):
                    sp.wait_ge(y_stored[b], (q * 2 + 2 + slot_tiles // 2) * 16)
                sp.dma_start(own_sb[:, q % 2, :, :], row_tiles(sum_rows, q, 4)).then_inc(own_loaded[q % 2], 16)

            for n in range(routed_end, routed_end + 2):
                load_in(Tile(0, n), x1_rows, n - slot_tiles)
            for n in range(routed_end, ffn_tiles):
                ahead, half = divmod(n - routed_end, 2)
                if ahead >= 1 and half == 0:
                    load_own(ahead - 1)
                load_add(Tile(0, n), n - slot_tiles)
                if n + 2 < ffn_tiles:
                    load_in(Tile(0, n + 2), x1_rows, n + 2 - slot_tiles)
            for q in range((tiles - early) // 2 - 1, quads):
                load_own(q)

        @block.gpsimd
        def _(pool):
            fills = [(ident, 0.0), (head_block, 1.0), (head_of_pair, 1.0), (causal, 1.0), (before, 1.0), (ones, 1.0)]
            for dst, value in fills:
                pool.memset(dst[:, :], value).then_inc(consts_set, 1)
            pool.wait_ge(consts_set, len(fills))
            blocks = head_block[:, :].rearrange("p (h d) -> p h d", d=D)

            def select(m, op, fill, base, pattern, by_row):
                pool.affine_select(out=m, in_=m, compare_op=op, fill=fill, base=base, pattern=pattern,
                                   channel_multiplier=by_row).then_inc(masks_set, 1)

            select(ident[:, :], ALU.not_equal, 1.0, 0, [[-1, P]], 1)
            select(causal[:, :], ALU.is_ge, 0.0, 0, [[1, P]], -1)
            select(before[:, :], ALU.is_ge, 0.0, -1, [[1, P]], -1)
            select(blocks, ALU.is_ge, 0.0, 0, [[-D, hpg], [0, D]], 1)
            pool.memset(v_pair[:, :, :, :], 0.0).then_inc(masks_set, 1)
            pool.wait_ge(masks_set, 5)
            select(blocks, ALU.is_ge, 0.0, D - 1, [[D, hpg], [0, D]], -1)
            pool.wait_ge(masks_set, 6)
            by_pair = head_block[:, :].rearrange("p (j r d) -> p r j d", r=2, d=D)
            pool.tensor_tensor(head_of_pair[:, :], by_pair[:, :, 0, 0], by_pair[:, :, 1, 0], ALU.add).then_inc(masks_set, 1)
            for j in range(2, hpg // 2):
                pool.wait_ge(masks_set, 5 + j)
                pool.tensor_tensor(head_of_pair[:, :], head_of_pair[:, :], by_pair[:, :, j, 0], ALU.add).then_inc(masks_set, 1)
            pool.iota(countdown[:, :], pattern=[[-1, E]], base=E, channel_multiplier=0,
                      allow_small_or_imprecise_dtypes=True).then_inc(masks_set, 1)
            pool.iota(slot_number[:, :], pattern=[[1, slot_tiles]], base=0, channel_multiplier=0,
                      allow_small_or_imprecise_dtypes=True).then_inc(masks_set, 1)
            pool.wait_ge(masks_set, MASKS)
            pool.wait_ge(params_loaded, ALL_PARAMS)

            def tile_side(t):
                i, b = t.index, t.parity
                pool.wait_ge(v_copied, i + 1)
                wait(pool, av_done, i - 1)
                pool.tensor_tensor(v_view(v_pair[:, b, :, :]), v_raw[:, :].rearrange("p (j r d) -> p j r d", r=2, d=D),
                                   bqkv_sb[:, 2 * C:3 * C].rearrange("p (j r d) -> p j r d", r=2, d=D),
                                   ALU.add).then_inc(v_ready, 1)
                for a in range(halves):
                    pool.wait_ge(ker_done, i * 4 + a + 1)
                    wait(pool, score_mm, i * 4 - 4)
                    pool.tensor_tensor(q_pair[:, b, a, :, :],
                                       kerT[:, b, a, :].unsqueeze(1).broadcast_to([P, 2, P]),
                                       head_of_pair[:, :].unsqueeze(2).broadcast_to([P, 2, P]),
                                       ALU.mult).then_inc(qexp_done, 1)
                pool.wait_ge(norm_done, i * 2 + 2)
                wait(pool, ktok_done, i - 1)
                pool.tensor_tensor(k_affine[:, b, :], qkn[:, b, C:2 * C], gk_sb[:, :], ALU.mult).then_inc(affine_done, 1)
                pool.wait_ge(affine_done, i * 2 + 1)
                pool.tensor_tensor(k_affine[:, b, :], k_affine[:, b, :], bk_sb[:, :], ALU.add).then_inc(affine_done, 1)
                pool.wait_ge(scan_done, i * 2 + 2)
                wait(pool, av_done, i - 1)
                pool.tensor_tensor(prod[:, b, :, :], kerT[:, b, 0:halves, :], ksumT[:, b, :, :],
                                   ALU.mult).then_inc(prod_done, 1)
                pool.wait_ge(x_loaded[b], t.round * 16 + 16)
                wait(pool, res_done, i - 1)
                pool.tensor_tensor(xb_sb[:, b, :], x_sb[:, b, :], bo_sb[:, :], ALU.add).then_inc(xb_done, 1)

            tile_side(Tile(0, 0))
            tile_side(Tile(0, 1))
            with pool.Fori(1, tiles // 2) as it:
                tile_side(Tile(it, 0))
                tile_side(Tile(it, 1))

            def carry(done, count):
                wait(pool, done, count)
                pool.tensor_tensor(turn[:, :], ones[:, 0:1], ones[:, 0:1], ALU.mult).then_inc(done, 1)

            def columns(x, u, count):
                return x[:, :, bass.ds(u.index * count, count)]

            def send(u):
                i, b = u.index, u.parity
                wait(pool, sent[b], u.round * SENT)
                pool.tensor_copy(index_sb[:, b, :, 0:2], columns(position_i, u, 2)).then_inc(index_set, 1)
                pool.wait_ge(index_set, i + 1)
                pool.wait_ge(send_loaded[b], u.round * 16 + 16)
                carry(turn_done, i)
                for j in range(2):
                    for k in range(TOP_K):
                        pool.indirect_dma_start(
                            out=slot_rows, in_=send_sb[:, b, j, :], in_offset=None,
                            out_offset=bass.IndirectOffsetOnAxis(ap=index_sb[:, b, k, j:j + 1], axis=0)
                        ).then_inc(sent[b], 16)

            pool.wait_ge(zero_filled, 16 * ZERO_FILLS)
            pool.wait_ge(position_done, 1)
            for n in range(2):
                send(Tile(0, n))
            with pool.Fori(1, pairs // 2) as it:
                for d in range(2):
                    send(Tile(it, d))

            def fetch(u):
                i, b = u.index, u.parity
                wait(pool, mix_done, i * 8 - 8)
                pool.tensor_copy(index_sb[:, b, :, :], columns(position_i, u, 4)).then_inc(gather_set, 1)
                pool.tensor_copy(weight_sb[:, b, :, :], columns(weight, u, 4)).then_inc(gather_set, 1)
                pool.wait_ge(gather_set, i * 2 + 2)
                carry(f_turn_done, i)
                for j in range(4):
                    for k in range(TOP_K):
                        pool.indirect_dma_start(
                            out=got_sb[:, b, k, j, :], out_offset=None, in_=slot_y,
                            in_offset=bass.IndirectOffsetOnAxis(ap=index_sb[:, b, k, j:j + 1], axis=0)
                        ).then_inc(gathered[b], 16)

            for b in range(2):
                pool.wait_ge(sent[b], SENT * (pairs // 2))
            for b in range(2):
                pool.wait_ge(y_stored[b], 16 * (routed_end // 2))
            for n in range(2):
                fetch(Tile(0, n))
            with pool.Fori(1, quads // 2) as it:
                for d in range(2):
                    fetch(Tile(it, d))

        @block.tensor
        def _(pe):
            def qk(t):
                i, b = t.index, t.parity
                pe.wait_ge(xT_loaded[b], t.round * 16 + 16)
                wait(pe, ker_done, i * 4)
                for a in range(halves):
                    mm = pe.matmul(qk_ps, xT_sb[:, b, a, :], wqkv_sb[:, a, 0:2 * C], start=a == 0, stop=a == halves - 1)
                mm.then_inc(qk_mm, 1)

            def values(t):
                i, b = t.index, t.parity
                wait(pe, v_copied, i)
                wait(pe, logit_done, i - 2)
                for a in range(halves):
                    mm = pe.matmul(v_ps, xT_sb[:, b, a, :], wqkv_sb[:, a, 2 * C:3 * C], start=a == 0, stop=a == halves - 1)
                mm.then_inc(v_mm, 1)

            def turn_qk(t):
                i, b = t.index, t.parity
                pe.wait_ge(norm_done, i * 2 + 2)
                for n in range(2 * halves):
                    mm = pe.transpose(qkT_ps[:, n * P:(n + 1) * P], qkn[:, b, n * P:(n + 1) * P], ident[:, :])
                mm.then_inc(qkT_mm, 1)

            def score(t):
                i, b = t.index, t.parity
                pe.wait_ge(ker_done, i * 4 + 4)
                for a in range(halves):
                    pe.wait_ge(qexp_done, i * 2 + a + 1)
                    if a == 0:
                        wait(pe, mask_done, i * 4)
                    for j in range(hpg // 2):
                        rows = slice(j * VH, (j + 1) * VH)
                        mm = pe.matmul(score_ps[:, j, a * 2 * P:(a + 1) * 2 * P], kerT[rows, b, halves + a, :],
                                       q_pair[rows, b, a, :, :].rearrange("p r t -> p (r t)"), start=True, stop=True,
                                       skip_group_check=True)
                        if a == halves - 1:
                            mm.then_inc(score_mm, 1)

            def attend(t):
                i, b = t.index, t.parity
                pe.wait_ge(mask_done, i * 4 + 4)
                pe.wait_ge(v_ready, i + 1)
                pe.wait_ge(state_ready, i + 1)
                wait(pe, attn_done, i)
                for a in range(halves):
                    for r in range(2):
                        for j in range(hpg // 2):
                            pair = a * (hpg // 2) + j
                            pe.matmul(num_ps[j * VH:(j + 1) * VH, a, :], v_pair[:, b, pair, r * VH:(r + 1) * VH],
                                      scores[:, b, pair * 2 + r, :], start=r == 0, stop=False, skip_group_check=True)
                    for j in range(hpg // 2):
                        rows = slice(j * VH, (j + 1) * VH)
                        pe.matmul(num_ps[rows, a, :], state[rows, a, :], kerT[rows, b, a, :], start=False, stop=True,
                                  skip_group_check=True)

            def denominators_and_sums(t):
                i, b = t.index, t.parity
                pe.wait_ge(prod_done, i + 1)
                for a in range(halves):
                    mm = pe.matmul(den_ps[:, a, :], head_block[:, :], prod[:, b, a, :], start=True, stop=True,
                                   skip_group_check=True)
                mm.then_inc(num_mm, 1)
                pe.wait_ge(ktok_done, i + 1)
                for a in range(halves):
                    for j in range(hpg // 2):
                        pair = a * (hpg // 2) + j
                        mm = pe.matmul(state_ps[j * VH:(j + 1) * VH, a, :], ktok[:, b, pair * VH:(pair + 1) * VH],
                                       v_view(v_pair[:, b, pair:pair + 1, :]).rearrange("p j r d -> p (j r) d"),
                                       start=False, stop=False, skip_group_check=True)
                mm.then_inc(av_done, 1)

            def project(t, after=None):
                i, b = t.index, t.parity
                if after:
                    pe.wait_ge(v_copied, after.index + 1)
                else:
                    pe.wait_ge(logit_done, i)
                pe.wait_ge(attn_done, i + 1)
                for a in range(halves):
                    mm = pe.matmul(wo_ps, attnT[:, b, a, :], wo_sb[:, a, :], start=a == 0, stop=a == halves - 1)
                mm.then_inc(wo_mm, 1)

            def turn_x1(t):
                i, b = t.index, t.parity
                pe.wait_ge(x1_done, i + 1)
                for a in range(halves):
                    mm = pe.transpose(x1T_ps[:, a, :], x1_sb[:, b, a * P:(a + 1) * P], ident[:, :])
                mm.then_inc(x1T_mm, 1)

            def logit(t):
                pe.wait_ge(x1T_done, t.index + 1)
                for a in range(halves):
                    mm = pe.matmul(logitT_ps, router_sb[:, a, :], x1T_sb[:, a, :], start=a == 0, stop=a == halves - 1)
                mm.then_inc(logit_mm, 1)

            def step(after, now, last):
                if after:
                    qk(after)
                    values(after)
                score(now)
                if last:
                    project(last, after)
                if after:
                    turn_qk(after)
                attend(now)
                if last:
                    turn_x1(last)
                denominators_and_sums(now)
                if last:
                    logit(last)

            pe.wait_ge(zero_set, 1)
            pe.matmul(bank[6][:, 0:halves * VH], zero_rows[:, 0:P], zero_rows[:, 0:halves * VH], start=True, stop=False,
                      skip_group_check=True)
            pe.wait_ge(wqkv_loaded, 16)
            qk(Tile(0, 0))
            values(Tile(0, 0))
            pe.wait_ge(masks_set, MASKS)
            pe.wait_ge(params_loaded, ALL_PARAMS)
            turn_qk(Tile(0, 0))
            step(Tile(0, 1), Tile(0, 0), None)
            step(Tile(0, 2), Tile(0, 1), Tile(0, 0))
            step(Tile(0, 3), Tile(0, 2), Tile(0, 1))
            with pe.Fori(1, tiles // 2 - 1) as it:
                step(Tile(it, 2), Tile(it, 1), Tile(it, 0))
                step(Tile(it, 3), Tile(it, 2), Tile(it, 1))
            last = Tile(0, tiles - 1)
            step(None, last, Tile(0, tiles - 2))
            project(last)
            turn_x1(last)
            logit(last)

            pe.wait_ge(logit_done, tiles)
            for n in range(tiles):
                mm = pe.transpose(logits_ps[:, n * E:(n + 1) * E], logitsT[:, n * P:(n + 1) * P], ident[0:E, 0:E])
            mm.then_inc(logitsT_mm, 1)

            def turn_in(t):
                i, b = t.index, t.parity
                pe.wait_ge(in_loaded[b], t.round * 16 + 16)
                wait(pe, in_lo_done, i)
                for a in range(halves):
                    mm = pe.transpose(inT_ps[:, a, :], in_sb[:, b, a * P:(a + 1) * P], ident[:, :])
                mm.then_inc(inT_mm, 1)

            def gate_up(t, e):
                i, b = t.index, t.parity
                pe.wait_ge(in_lo_done, i + 1)
                wait(pe, h_done, i)
                for which, dst in ((GATE, gate_ps), (UP, up_ps)):
                    if e is None:
                        w_hi, w_lo = shared_hi[:, which, :], shared_lo[:, which, :]
                    else:
                        w_hi, w_lo = (w[which][:, bass.ds(e, 1), :].rearrange("p e n -> p (e n)") for w in (high, low))
                    for a in range(halves):
                        words = slice(a * I, (a + 1) * I)
                        for n, (x_part, w) in enumerate(((in_hi, w_hi), (in_hi, w_lo), (in_lo, w_hi))):
                            mm = pe.matmul(dst, x_part[:, b, a, :], w[:, words], start=a == 0 and n == 0,
                                           stop=a == halves - 1 and n == 2)
                    mm.then_inc(gu_mm, 1)

            def turn_h(t):
                i = t.index
                pe.wait_ge(h_done, i + 1)
                wait(pe, hT_done, i)
                for m in range(inner):
                    mm = pe.transpose(hT_ps[:, m, :], h_sb[:, m * P:(m + 1) * P], ident[:, :])
                mm.then_inc(hT_mm, 1)

            def down(t, e):
                i = t.index
                pe.wait_ge(hT_done, i + 1)
                wait(pe, y_done, i)
                e = E if e is None else e
                for m in range(inner):
                    w = down_sb[:, bass.ds(e, 1), m * C:(m + 1) * C].rearrange("p e n -> p (e n)")
                    mm = pe.matmul(y_ps, hT_sb[:, m, :], w, start=m == 0, stop=m == inner - 1)
                mm.then_inc(y_mm, 1)

            def ffn_step(now, e=None, last=None, e_last=None, after=None):
                gate_up(now, e)
                if after:
                    turn_in(after)
                if last:
                    down(last, e_last() if callable(e_last) else e_last)
                turn_h(now)

            def own_step(it, d):
                ffn_step(Tile(it, d), None, Tile(it, d - 1), None, Tile(it, d + 1))

            pe.wait_ge(down_loaded, 16)
            pe.wait_ge(lo_done, 2)
            turn_in(Tile(0, 0))
            ffn_step(Tile(0, 0), after=Tile(0, 1))
            pe.wait_ge(member_done, 1)
            pe.matmul(rank_ps, before[:, :], flat(member), start=True, stop=True).then_inc(rank_mm, 1)
            pe.matmul(total_ps, ones[:, :], flat(member), start=True, stop=True).then_inc(total_mm, 1)
            own_step(0, 1)
            own_step(0, 2)
            with pe.Fori(1, early // 2 - 1) as it:
                own_step(it, 1)
                own_step(it, 2)
            own_step(0, early - 1)
            pe.wait_ge(experts_done, 1)
            pe.wait_ge(lo_done, 2 * E + 2)

            def expert(n):
                return pe.value_load(expert_i[0:1, bass.ds(n, 1)], min_val=0, max_val=E - 1)

            ffn_step(Tile(0, early), expert(0), Tile(0, early - 1), None, Tile(0, early + 1))
            with pe.Fori(0, (slot_tiles - 2) // 2) as it:
                e_last = lambda: expert(it * 2)
                for d in range(1, 3):
                    e = expert(it * 2 + d)
                    ffn_step(Tile(it * 1, early + d), e, Tile(it * 1, early + d - 1), e_last, Tile(it * 1, early + d + 1))
                    e_last = e
            e_last = expert(slot_tiles - 1)
            e_before = expert(slot_tiles - 2)
            n = routed_end - 1
            ffn_step(Tile(0, n), e_last, Tile(0, n - 1), e_before, Tile(0, n + 1))
            ffn_step(Tile(0, n + 1), None, Tile(0, n), e_last, Tile(0, n + 2))
            with pe.Fori(routed_end // 2, ffn_tiles // 2 - 1) as it:
                own_step(it, 1)
                own_step(it, 2)
            n = ffn_tiles - 1
            ffn_step(Tile(0, n), None, Tile(0, n - 1), None)
            down(Tile(0, n), None)

        @block.scalar
        def _(act):
            act.dma_start(shared_raw[:, :, :], ffn_w[E, :, 0:GU].rearrange("p (w n) -> p w n", w=2)).then_inc(gu_loaded, 16)

            def split_hi(e, which):
                dst, src = (w[which][:, bass.ds(e, 1), :].rearrange("p e n -> p (e n)") for w in (high, raw))
                act.activation(dst, src, ACT.Copy).then_inc(hi_done, 1)

            def qk_std(t):
                act.wait_ge(aggr_done, t.index * 2 + 2)
                wait(act, std_eps_done, t.index)
                act.activation(std[:, :], moments[:, :, 1], ACT.Sqrt, scale=C / (C - 1)).then_inc(std_done, 1)

            def normalise(t):
                i, b = t.index, t.parity
                act.wait_ge(shift_done, i + 1)
                wait(act, qkT_mm, i - 1)
                wait(act, affine_done, i * 2 - 2)
                for n in range(2):
                    act.activation(qkn[:, b, n * C:(n + 1) * C], qk_sb[:, n * C:(n + 1) * C], ACT.Identity,
                                   scale=inv_std[:, n:n + 1], bias=shift[:, n:n + 1]).then_inc(norm_done, 1)

            def copy_v(t):
                act.wait_ge(v_mm, t.index + 1)
                wait(act, v_ready, t.index)
                act.activation(v_raw[:, :], v_ps, ACT.Copy).then_inc(v_copied, 1)

            def features(t):
                i, b = t.index, t.parity
                act.wait_ge(qkT_mm, i + 1)
                wait(act, av_done, i - 1)
                for n in range(2 * halves):
                    act.activation(kerT[:, b, n, :], qkT_ps[:, n * P:(n + 1) * P], ACT.Square,
                                   scale=gb_sb[:, 0, n:n + 1], bias=gb_sb[:, 1, n:n + 1]).then_inc(ker_done, 1)

            def key_rows(t):
                i, b = t.index, t.parity
                act.wait_ge(affine_done, i * 2 + 2)
                wait(act, av_done, i - 1)
                act.activation(ktok[:, b, :], k_affine[:, b, :], ACT.Square).then_inc(ktok_done, 1)

            def denominators(t):
                i = t.index
                act.wait_ge(num_mm, i + 1)
                wait(act, inv_den_done, i)
                act.activation(den[:, :, :], den_ps, ACT.Identity, bias=eps_attn[:, :]).then_inc(den_done, 1)

            def x1_std(t):
                act.wait_ge(ln_aggr_done, t.index + 1)
                wait(act, ln_inv_done, t.index)
                act.activation(ln_std[:, :], ln_moments[:, 1:2], ACT.Sqrt, bias=eps_ln[:, :]).then_inc(ln_std_done, 1)

            def x1_out(t):
                i, b = t.index, t.parity
                act.wait_ge(x1_done, i + 1)
                act.dma_start(row_tile(x1_rows, i), x1_sb[:, b, :]).then_inc(x1_stored[b], 16)
                act.wait_ge(x1T_mm, i + 1)
                wait(act, logit_mm, i)
                act.activation(x1T_sb[:, :, :], x1T_ps, ACT.Copy).then_inc(x1T_done, 1)

            def logit_out(t):
                act.wait_ge(logit_mm, t.index + 1)
                act.activation(logitsT[:, bass.ds(t.index * P, P)], logitT_ps, ACT.Identity,
                               bias=router_bias_sb[:, :]).then_inc(logit_done, 1)

            def step(after, now, last):
                key_rows(now)
                if after:
                    copy_v(after)
                    qk_std(after)
                    normalise(after)
                if last:
                    x1_std(last)
                if after:
                    features(after)
                if last:
                    x1_out(last)
                denominators(now)
                if last:
                    logit_out(last)

            act.wait_ge(eps_set, 2)
            act.wait_ge(params_loaded, ALL_PARAMS)
            qk_std(Tile(0, 0))
            normalise(Tile(0, 0))
            copy_v(Tile(0, 0))
            features(Tile(0, 0))
            step(Tile(0, 1), Tile(0, 0), None)
            step(Tile(0, 2), Tile(0, 1), Tile(0, 0))
            act.wait_ge(gu_loaded, 16)
            for which in (GATE, UP):
                act.activation(shared_hi[:, which, :], shared_raw[:, which, :], ACT.Copy).then_inc(hi_done, 1)
            fill = slot_rows.rearrange("(n p r) c -> n p (r c)", p=P, r=ZERO_TILES)
            for n in range(ZERO_FILLS):
                act.dma_start(fill[n], zero_rows[:, :]).then_inc(zero_filled, 16)
            act.dma_start(down_sb[:, :, :], ffn_w[:, :, GU:].rearrange("e p n -> p e n")).then_inc(down_loaded, 16)
            step(Tile(0, 3), Tile(0, 2), Tile(0, 1))
            with act.Fori(1, tiles // 2 - 1) as it:
                step(Tile(it, 2), Tile(it, 1), Tile(it, 0))
                step(Tile(it, 3), Tile(it, 2), Tile(it, 1))
            last = Tile(0, tiles - 1)
            step(None, last, Tile(0, tiles - 2))
            x1_std(last)
            x1_out(last)
            logit_out(last)

            act.wait_ge(logitsT_mm, 1)
            for b in range(2):
                act.wait_ge(x1_stored[b], 16 * (tiles // 2))
            act.activation(flat(probs), logits_ps, ACT.Sigmoid).then_inc(probs_done, 1)

            def load_expert(e):
                for which in (GATE, UP):
                    act.dma_start(raw[which][:, bass.ds(e, 1), :].rearrange("p e n -> p (e n)"),
                                  ffn_w[bass.ds(e, 1), :, which * CHUNK:(which + 1) * CHUNK].rearrange("e p n -> p (e n)")
                                  ).then_inc(gu_loaded, 16)

            act.wait_ge(state_ready, tiles + 1)
            load_expert(0)

            def copy_in(t):
                i, b = t.index, t.parity
                act.wait_ge(inT_mm, i + 1)
                wait(act, gu_mm, i * 2 - 2)
                act.activation(in_hi[:, b, :, :], inT_ps, ACT.Copy).then_inc(in_hi_done, 1)

            def silu(t):
                i = t.index
                act.wait_ge(gu_mm, i * 2 + 1)
                wait(act, hT_mm, i)
                act.activation(h_sb[:, :], gate_ps, ACT.Silu).then_inc(silu_done, 1)

            def copy_h(t):
                i = t.index
                act.wait_ge(hT_mm, i + 1)
                wait(act, y_mm, i)
                act.activation(hT_sb[:, :, :], hT_ps, ACT.Copy).then_inc(hT_done, 1)

            def copy_y(t):
                i, b = t.index, t.parity
                act.wait_ge(y_mm, i + 1)
                act.wait_ge(y_stored[b], t.round * 16)
                act.activation(y_sb[:, b, :], y_ps, ACT.Copy).then_inc(y_done, 1)

            def store_y(t, rows, n):
                i, b = t.index, t.parity
                act.wait_ge(y_done, i + 1)
                act.dma_start(row_tile(rows, n), y_sb[:, b, :]).then_inc(y_stored[b], 16)

            def split_hi_chunk(t, load=True):
                if t.parity == 0:
                    act.wait_ge(gu_loaded, t.round * 32 + 48)
                    if load:
                        load_expert(t.round + 1)
                split_hi(t.round, t.parity)

            def ffn_step(now, after=None, last=None, n=None, routed=False, chunk=False, load=True, between=None):
                silu(now)
                if after:
                    copy_in(after)
                if between:
                    between()
                if last and routed:
                    copy_y(last)
                copy_h(now)
                if last:
                    store_y(last, slot_y if routed else sum_rows, n)
                if chunk:
                    split_hi_chunk(now, load)

            def deviations(q):
                act.wait_ge(f_aggr_done, q * 4 + 4)
                wait(act, f_inv_done, q - 1)
                act.activation(f_std[:, q % 2, :], f_moments[:, q % 2, :, 1], ACT.Sqrt,
                               bias=eps_ln[:, :]).then_inc(f_std_done, 1)

            def normalise_quad(q):
                b = q % 2
                act.wait_ge(f_shift_done, q + 1)
                wait(act, out_stored[b], q // 2 * 16)
                for j in range(4):
                    act.activation(out_sb[:, b, j, :], own_sb[:, b, j, :], ACT.Identity, scale=f_inv[:, b, j:j + 1],
                                   bias=f_shift[:, b, j:j + 1]).then_inc(out_done, 1)

            def store_quad(q):
                act.wait_ge(out_done, q * 4 + 4)
                act.dma_start(row_tiles(out, q, 4), out_sb[:, q % 2, :, :]).then_inc(out_stored[q % 2], 16)

            copy_in(Tile(0, 0))
            ffn_step(Tile(0, 0), Tile(0, 1), chunk=True)
            act.wait_ge(experts_done, 1)
            ffn_step(Tile(0, 1), Tile(0, 2), Tile(0, 0), 0, chunk=True)
            ffn_step(Tile(0, 2), Tile(0, 3), Tile(0, 1), 1, chunk=True)
            with act.Fori(1, E - 2) as it:
                for d in (1, 2):
                    ffn_step(Tile(it, d), Tile(it, d + 1), Tile(it, d - 1), it * 2 + d - 1, chunk=True)
            for n in range(2 * E - 3, 2 * E):
                ffn_step(Tile(0, n), Tile(0, n + 1), Tile(0, n - 1), n - 1, chunk=True, load=False)
            for n in range(2 * E, early + 1):
                ffn_step(Tile(0, n), Tile(0, n + 1), Tile(0, n - 1), n - 1)
            with act.Fori(early // 2, routed_end // 2) as it:
                for d in (1, 2):
                    ffn_step(Tile(it, d), Tile(it, d + 1), Tile(it, d - 1), it * 2 + d - 1 - early, routed=True)
            for n in range(routed_end + 1, ffn_tiles):
                t = Tile(0, n)
                q, half = (n - routed_end) // 2 - 2, (n - routed_end) % 2
                between = None if q < 0 else (lambda: normalise_quad(q)) if half else (lambda: deviations(q))
                ffn_step(t, Tile(0, n + 1) if n + 1 < ffn_tiles else None, Tile(0, n - 1), n - 1 - slot_tiles,
                         between=between)
                if q >= 0 and half:
                    store_quad(q)
            store_y(Tile(0, n), sum_rows, n - slot_tiles)
            for q in range((tiles - early) // 2 - 2, quads):
                deviations(q)
                normalise_quad(q)
                store_quad(q)
            for b in range(2):
                act.wait_ge(out_stored[b], 16 * (quads // 2))

        @block.vector
        def _(dve):
            def split_lo(t):
                part_hi, part_lo, part_raw = (w[t.parity][:, bass.ds(t.round, 1), :].rearrange("p e n -> p (e n)")
                                              for w in (high, low, raw))
                dve.wait_ge(hi_done, t.index + 3)
                dve.tensor_tensor(part_lo, part_raw, part_hi.bitcast(F32), ALU.subtract).then_inc(lo_done, 1)

            def bias_qk(t):
                i, b = t.index, t.parity
                dve.wait_ge(qk_mm, i + 1)
                wait(dve, norm_done, i * 2)
                dve.tensor_tensor(qk_sb[:, :], qk_ps, bqkv_sb[:, 0:2 * C], ALU.add).then_inc(qk_biased, 1)
                wait(dve, aggr_done, i * 2)
                dve.wait_ge(qk_biased, i + 1)
                for n in range(2):
                    dve.bn_stats(stats[:, n, :], qk_sb[:, n * C:(n + 1) * C]).then_inc(stats_done, 1)

            def qk_moments(t):
                dve.wait_ge(stats_done, t.index * 2 + 2)
                wait(dve, qk_carry_done, t.index)
                dve.tensor_tensor(carried[:, 0:1], ones[:, 0:1], ones[:, 0:1], ALU.mult).then_inc(qk_carry_done, 1)
                for n in range(2):
                    dve.bn_aggr(moments[:, n, :], stats[:, n, :]).then_inc(aggr_done, 1)

            def qk_scales(t):
                i = t.index
                dve.wait_ge(std_done, i + 1)
                dve.tensor_scalar(std_eps[:, :], std[:, :], EPS_ATTN, None, ALU.add).then_inc(std_eps_done, 1)
                dve.wait_ge(std_eps_done, i + 1)
                dve.reciprocal(inv_std[:, :], std_eps[:, :]).then_inc(inv_std_done, 1)
                dve.wait_ge(inv_std_done, i + 1)
                dve.scalar_tensor_tensor(out=shift[:, :], in0=moments[:, :, 0], scalar=-1.0, in1=inv_std[:, :],
                                         op0=ALU.mult, op1=ALU.mult).then_inc(shift_done, 1)

            def mask(t, j):
                i, b = t.index, t.parity
                dve.wait_ge(score_mm, i * 4 + j + 1)
                wait(dve, av_done, i - 1)
                dve.tensor_tensor(
                    scores[:, b, :, :].rearrange("p (a j r) t -> p j a r t", a=halves, r=2)[:, j],
                    score_ps[:, j, :].rearrange("p (a r t) -> p a r t", a=halves, r=2),
                    causal[:, :].unsqueeze(1).unsqueeze(1).broadcast_to([P, halves, 2, P]), ALU.mult).then_inc(mask_done, 1)

            def key_sums(t):
                i, b = t.index, t.parity
                dve.wait_ge(ker_done, i * 4 + 4)
                wait(dve, prod_done, i - 1)
                wait(dve, scan_done, i * 2)
                for a in range(halves):
                    dve.tensor_tensor_scan(ksumT[:, b, a, :], ones[:, :], kerT[:, b, halves + a, :],
                                           ksumT[:, 1 - b, a, P - 1:P], ALU.mult, ALU.add).then_inc(scan_done, 1)

            def attn_out(t):
                i, b = t.index, t.parity
                dve.wait_ge(den_done, i + 1)
                wait(dve, attn_done, i)
                dve.reciprocal(inv_den[:, :, :], den[:, :, :]).then_inc(inv_den_done, 1)
                dve.wait_ge(inv_den_done, i + 1)
                wait(dve, wo_mm, i - 1)
                dve.tensor_tensor(attnT[:, b, :, :], num_ps, inv_den[:, :, :], ALU.mult).then_inc(attn_done, 1)

            def add_state(t):
                i = t.index
                dve.wait_ge(av_done, i + 1)
                dve.tensor_tensor(state[:, :, :].rearrange("p a (r d) -> p a r d", d=D),
                                  state_ps.rearrange("p a (r d) -> p a r d", d=D),
                                  head_of_pair[:, :].unsqueeze(1).unsqueeze(3).broadcast_to([P, halves, 2, D]),
                                  ALU.mult).then_inc(state_ready, 1)

            def residual(t):
                i, b = t.index, t.parity
                dve.wait_ge(wo_mm, i + 1)
                dve.wait_ge(xb_done, i + 1)
                wait(dve, x1_done, i)
                dve.tensor_tensor(res[:, :], wo_ps, xb_sb[:, b, :], ALU.add).then_inc(res_done, 1)
                dve.wait_ge(res_done, i + 1)
                wait(dve, ln_aggr_done, i)
                dve.bn_stats(ln_stats[:, :], res[:, :]).then_inc(ln_stats_done, 1)

            def x1_moments(t):
                dve.wait_ge(ln_stats_done, t.index + 1)
                wait(dve, ln_carry_done, t.index)
                dve.tensor_tensor(carried[:, 1:2], ones[:, 0:1], ones[:, 0:1], ALU.mult).then_inc(ln_carry_done, 1)
                dve.bn_aggr(ln_moments[:, :], ln_stats[:, :]).then_inc(ln_aggr_done, 1)

            def make_x1(t):
                i, b = t.index, t.parity
                dve.wait_ge(ln_std_done, i + 1)
                dve.reciprocal(ln_inv[:, :], ln_std[:, :]).then_inc(ln_inv_done, 1)
                dve.wait_ge(ln_inv_done, i + 1)
                if not isinstance(t.round, int) or t.round > 0:
                    dve.wait_ge(x1_stored[b], t.round * 16)
                    dve.wait_ge(x1T_mm, i - 1)
                dve.tensor_scalar(x1_sb[:, b, :], res[:, :], ln_moments[:, 0:1], ln_inv[:, 0:1],
                                  ALU.subtract, ALU.mult).then_inc(x1_done, 1)

            def step(after, now, last):
                if after:
                    bias_qk(after)
                    qk_moments(after)
                mask(now, 0)
                if after:
                    qk_scales(after)
                for j in range(1, hpg // 2):
                    mask(now, j)
                if last:
                    residual(last)
                    x1_moments(last)
                    make_x1(last)
                if after:
                    key_sums(after)
                attn_out(now)
                add_state(now)

            dve.memset(zero_rows[:, :], 0.0).then_inc(zero_set, 1)
            dve.memset(eps_ln[:, :], EPS_LN).then_inc(eps_set, 1)
            dve.memset(eps_attn[:, :], EPS_ATTN).then_inc(eps_set, 1)
            dve.memset(state[:, :, :], 0.0).then_inc(state_ready, 1)
            dve.memset(ksumT[:, 1, :, :], 0.0).then_inc(sums_zeroed, 1)
            dve.wait_ge(sums_zeroed, 1)
            dve.wait_ge(masks_set, MASKS)
            dve.wait_ge(params_loaded, ALL_PARAMS)
            bias_qk(Tile(0, 0))
            qk_moments(Tile(0, 0))
            qk_scales(Tile(0, 0))
            key_sums(Tile(0, 0))
            step(Tile(0, 1), Tile(0, 0), None)
            step(Tile(0, 2), Tile(0, 1), Tile(0, 0))
            for which in (GATE, UP):
                dve.wait_ge(hi_done, which + 1)
                dve.tensor_tensor(shared_lo[:, which, :], shared_raw[:, which, :], shared_hi[:, which, :].bitcast(F32),
                                  ALU.subtract).then_inc(lo_done, 1)
            step(Tile(0, 3), Tile(0, 2), Tile(0, 1))
            with dve.Fori(1, tiles // 2 - 1) as it:
                step(Tile(it, 2), Tile(it, 1), Tile(it, 0))
                step(Tile(it, 3), Tile(it, 2), Tile(it, 1))
            last = Tile(0, tiles - 1)
            step(None, last, Tile(0, tiles - 2))
            residual(last)
            x1_moments(last)
            make_x1(last)

            chained = [0]

            def link(ins):
                chained[0] += 1
                ins.then_inc(route, 1)
                dve.wait_ge(route, chained[0])

            def over_experts(x):
                return x.unsqueeze(2).broadcast_to([P, tiles, E])

            def over_tiles(x):
                return x.unsqueeze(1).broadcast_to([P, tiles, E])

            def pick(onehot, values, best):
                link(dve.tensor_reduce(best, values, AX_X, ALU.max))
                link(dve.tensor_tensor(is_top, values, over_experts(best), ALU.is_equal))
                link(dve.tensor_tensor(picked, is_top, over_tiles(countdown[:, :]), ALU.mult))
                link(dve.tensor_reduce(first, picked, AX_X, ALU.max))
                link(dve.tensor_tensor(onehot, over_tiles(countdown[:, :]), over_experts(first), ALU.is_equal))

            dve.wait_ge(probs_done, 1)
            pick(onehot1, probs, max1)
            link(dve.scalar_tensor_tensor(out=rest, in0=onehot1, scalar=-4.0, in1=probs, op0=ALU.mult, op1=ALU.add))
            pick(onehot2, rest, max2)
            dve.tensor_tensor(member, onehot1, onehot2, ALU.add).then_inc(member_done, 1)

            def low_in(t):
                i, b = t.index, t.parity
                dve.wait_ge(in_hi_done, i + 1)
                dve.tensor_tensor(in_lo[:, b, :, :], inT_ps, in_hi[:, b, :, :].bitcast(F32),
                                  ALU.subtract).then_inc(in_lo_done, 1)

            def hidden(t):
                i = t.index
                dve.wait_ge(silu_done, i + 1)
                dve.wait_ge(gu_mm, i * 2 + 2)
                dve.tensor_tensor(h_sb[:, :], up_ps, h_sb[:, :], ALU.mult).then_inc(h_done, 1)

            def sum_y(t, late):
                i, b = t.index, t.parity
                dve.wait_ge(y_mm, i + 1)
                dve.wait_ge(add_loaded[b], t.round * 16 + 16 - (slot_tiles // 2 * 16 if late else 0))
                if not isinstance(t.round, int) or t.round > 0:
                    dve.wait_ge(y_stored[b], t.round * 16)
                dve.tensor_tensor(y_sb[:, b, :], y_ps, add_sb[:, b, :], ALU.add).then_inc(y_done, 1)

            EARLY, ROUTED, LATE = range(3)

            def ffn_step(now, after=None, last=None, last_in=ROUTED, chunk=False):
                hidden(now)
                if after:
                    low_in(after)
                if last and last_in != ROUTED:
                    sum_y(last, last_in == LATE)
                if chunk:
                    split_lo(now)

            low_in(Tile(0, 0))
            ffn_step(Tile(0, 0), Tile(0, 1), chunk=True)

            link(dve.tensor_tensor(p_sum, max1, max2, ALU.add))
            link(dve.reciprocal(p_inv, p_sum))
            link(dve.tensor_tensor(weight[:, 0, :], max1, p_inv, ALU.mult))
            link(dve.tensor_tensor(weight[:, 1, :], max2, p_inv, ALU.mult))
            link(dve.memset(reset_by_expert, 1.0))
            link(dve.memset(reset_by_expert[:, :, 0:1], 0.0))
            dve.wait_ge(total_mm, 1)
            link(dve.tensor_copy(totals_by_expert, total_ps.rearrange("p (i e) -> p e i", e=E)))
            link(dve.tensor_tensor_scan(flat(running_by_expert), flat(reset_by_expert), flat(totals_by_expert), 0.0,
                                        ALU.mult, ALU.add))
            link(dve.tensor_scalar(tile_n, running_by_expert[:, :, tiles - 1], float(P - 1), None, ALU.add))
            link(dve.tensor_scalar(tile_n, tile_n, P.bit_length() - 1, None, ALU.arith_shift_right))
            link(dve.tensor_copy(tile_f, tile_n))
            link(dve.tensor_tensor_scan(tile_end, ones[:, 0:E], tile_f, 0.0, ALU.mult, ALU.add))
            link(dve.tensor_tensor(slot_base, tile_end, tile_f, ALU.subtract))
            link(dve.tensor_scalar(slot_base, slot_base, float(P), None, ALU.mult))
            link(dve.tensor_tensor(position, running_by_expert.rearrange("p e i -> p i e"),
                                   totals_by_expert.rearrange("p e i -> p i e"), ALU.subtract))
            link(dve.tensor_tensor(position, position, over_tiles(slot_base), ALU.add))
            link(dve.tensor_tensor(position, rank_ps.rearrange("p (i e) -> p i e", e=E), position, ALU.add))
            for k, onehot in enumerate((onehot1, onehot2)):
                link(dve.tensor_tensor(picked, position, onehot, ALU.mult))
                link(dve.tensor_reduce(position_f[:, k, :], picked, AX_X, ALU.add))
            dve.tensor_copy(position_i[:, :, :], position_f).then_inc(position_done, 1)
            link(dve.tensor_tensor(expert_cmp,
                                   slot_number[0:1, :].unsqueeze(2).broadcast_to([1, slot_tiles, E]),
                                   tile_end[0:1, :].unsqueeze(1).broadcast_to([1, slot_tiles, E]), ALU.is_ge))
            link(dve.tensor_reduce(expert_f, expert_cmp, AX_X, ALU.add))
            dve.tensor_scalar(expert_i[:, :], expert_f, float(E - 1), None, ALU.min).then_inc(experts_done, 1)

            ffn_step(Tile(0, 1), Tile(0, 2), Tile(0, 0), EARLY, chunk=True)
            ffn_step(Tile(0, 2), Tile(0, 3), Tile(0, 1), EARLY, chunk=True)
            with dve.Fori(1, E - 1) as it:
                for d in (1, 2):
                    ffn_step(Tile(it, d), Tile(it, d + 1), Tile(it, d - 1), EARLY, chunk=True)
            n = 2 * E - 1
            ffn_step(Tile(0, n), Tile(0, n + 1), Tile(0, n - 1), EARLY, chunk=True)
            for n in range(2 * E, early + 1):
                ffn_step(Tile(0, n), Tile(0, n + 1), Tile(0, n - 1), EARLY)
            with dve.Fori(early // 2, routed_end // 2) as it:
                for d in (1, 2):
                    ffn_step(Tile(it, d), Tile(it, d + 1), Tile(it, d - 1), ROUTED)
            def mix(q, half):
                b = q % 2
                dve.wait_ge(gathered[b], q // 2 * GOT + GOT)
                dve.wait_ge(own_loaded[b], q // 2 * 16 + 16)
                dve.wait_ge(gather_set, q * 2 + 2)
                for k in range(TOP_K):
                    for j in (2 * half, 2 * half + 1):
                        if k:
                            dve.wait_ge(mix_done, q * 8 + half * 4 + j % 2 + 1)
                        dve.scalar_tensor_tensor(out=own_sb[:, b, j, :], in0=got_sb[:, b, k, j, :],
                                                 scalar=weight_sb[:, b, k, j:j + 1], in1=own_sb[:, b, j, :],
                                                 op0=ALU.mult, op1=ALU.add).then_inc(mix_done, 1)
                wait(dve, f_aggr_done, q * 4)
                for j in (2 * half, 2 * half + 1):
                    dve.wait_ge(mix_done, q * 8 + half * 4 + 3 + j % 2)
                    dve.bn_stats(f_stats[:, j, :], own_sb[:, b, j, :]).then_inc(f_stats_done, 1)

            def quad_moments(q):
                dve.wait_ge(f_stats_done, q * 4 + 4)
                wait(dve, f_shift_done, q - 1)
                for j in range(4):
                    dve.bn_aggr(f_moments[:, q % 2, j, :], f_stats[:, j, :]).then_inc(f_aggr_done, 1)

            def quad_scales(q):
                b = q % 2
                dve.wait_ge(f_std_done, q + 1)
                wait(dve, out_done, q * 4 - 4)
                dve.reciprocal(f_inv[:, b, :], f_std[:, b, :]).then_inc(f_inv_done, 1)
                dve.wait_ge(f_inv_done, q + 1)
                dve.scalar_tensor_tensor(out=f_shift[:, b, :], in0=f_moments[:, b, :, 0], scalar=-1.0,
                                         in1=f_inv[:, b, :], op0=ALU.mult, op1=ALU.mult).then_inc(f_shift_done, 1)

            def finish(q, half):
                mix(q, half)
                if half:
                    quad_moments(q)
                elif q:
                    quad_scales(q - 1)

            for n in range(routed_end + 1, ffn_tiles):
                ffn_step(Tile(0, n), Tile(0, n + 1) if n + 1 < ffn_tiles else None, Tile(0, n - 1), LATE)
                if n >= routed_end + 2:
                    finish((n - routed_end) // 2 - 1, (n - routed_end) % 2)
            sum_y(Tile(0, n), True)
            for q in range((tiles - early) // 2 - 1, quads):
                finish(q, 0)
                finish(q, 1)
            quad_scales(quads - 1)


def kernel(L0_attn_x, L0_attn_Wqkv, L0_attn_bqkv, L0_attn_gamma_q, L0_attn_beta_q, L0_attn_gamma_k,
           L0_attn_beta_k, L0_attn_Wo, L0_attn_bo, L0_ffn_sg_w, L0_ffn_su_w, L0_ffn_sd_w, L0_ffn_router_w,
           L0_ffn_routing_bias, L0_ffn_wg, L0_ffn_wu, L0_ffn_wd):
    import numpy as np
    import concourse.bacc as bacc
    from concourse.bass_utils import run_bass_kernel_spmd

    x = np.asarray(L0_attn_x)
    B, T, C = x.shape
    tiles, halves = B * T // P, C // P
    E = L0_ffn_wg.shape[0]
    slot_tiles = tiles * TOP_K + E

    def by_feature(w):
        return np.asarray(w).reshape(-1, P, w.shape[1]).transpose(1, 0, 2)

    def expert_rows(gate, up, down):
        return np.concatenate([by_feature(np.asarray(w).T).reshape(P, -1) for w in (gate, up, down)], axis=1)

    rows = x.reshape(tiles, P, C)
    columns = [np.asarray(v).reshape(halves, P).T
               for v in (L0_attn_gamma_q, L0_attn_gamma_k, L0_attn_beta_q, L0_attn_beta_k)]
    arrays = {
        "xT": rows.reshape(tiles, P, halves, P).transpose(0, 3, 2, 1),
        "x": rows,
        "wqkv": by_feature(L0_attn_Wqkv),
        "bqkv": L0_attn_bqkv,
        "gb_cols": np.stack(columns, axis=1).reshape(P, 2, 2 * halves),
        "gk_row": L0_attn_gamma_k,
        "bk_row": L0_attn_beta_k,
        "wo": by_feature(L0_attn_Wo),
        "bo": L0_attn_bo,
        "router": by_feature(np.asarray(L0_ffn_router_w).T),
        "router_bias": L0_ffn_routing_bias,
        "ffn_w": np.stack([expert_rows(L0_ffn_wg[e], L0_ffn_wu[e], L0_ffn_wd[e]) for e in range(E)]
                          + [expert_rows(L0_ffn_sg_w, L0_ffn_su_w, L0_ffn_sd_w)]),
    }
    arrays = {name: np.ascontiguousarray(a) for name, a in arrays.items()}
    nc = bacc.Bacc("TRN2", target_bir_lowering=False, num_devices=1)
    ins = {name: nc.dram_tensor(name, a.shape, F32, kind="ExternalInput").ap() for name, a in arrays.items()}
    out = nc.dram_tensor("out", (tiles * P, C), F32, kind="ExternalOutput").ap()
    inner = {name: nc.dram_tensor(name, (n * P, C), F32, kind="Internal").ap()
             for name, n in (("x1_rows", tiles), ("sum_rows", tiles), ("slot_rows", slot_tiles), ("slot_y", slot_tiles))}
    post_ln_block(nc, **ins, out=out, **inner)
    got = run_bass_kernel_spmd(nc, [arrays], core_ids=[0])
    return got.results[0]["out"].reshape(B, T, C)
```

```python
from contextlib import ExitStack

import concourse.bass as bass
from concourse import mybir

ALU = mybir.AluOpType
ACT = mybir.ActivationFunctionType
AX_X = mybir.AxisListType.X
F32 = mybir.dt.float32
F32R = mybir.dt.float32r
I32 = mybir.dt.int32

P = 128
HEADS = 16
D = 16
EPS_LN = 1e-5
EPS_ATTN = 1e-6
TOP_K = 2
EARLY_MORE = 8


class Tile:

    def __init__(self, it, d, buffers=2):
        self.index = it * buffers + d
        self.round = it + d // buffers
        self.parity = d % buffers
        self.later = not isinstance(self.round, int) or self.round > 0


def wait(eng, sem, value):
    if not isinstance(value, int) or value > 0:
        eng.wait_ge(sem, value)


def post_ln_block(nc, xT, x, wqkv, bqkv, gb_cols, gk_row, bk_row, wo, bo, router, router_bias, ffn_w,
                  out, x1_rows, sum_rows, slot_rows, routed_y):
    tiles, _, C = x.shape
    halves = C // P
    hpg = P // D
    E = ffn_w.shape[0] - 1
    I = ffn_w.shape[2] // (3 * halves)
    inner = I // P
    GU, DN = 2 * halves * I, inner * C
    CHUNK = GU // 2
    slot_tiles = slot_rows.shape[0] // P
    ffn_tiles = tiles + slot_tiles
    early = tiles // 2 + EARLY_MORE
    routed_end = early + slot_tiles
    pairs = tiles // 2
    quads = tiles // 4
    assert slot_tiles >= tiles * TOP_K + E - 1 and slot_tiles % 2 == 0 and tiles % 4 == 0
    assert 2 * E + 2 <= early and early % 2 == 0
    TE = tiles * E
    VH = 2 * D
    VB = 3 * VH

    ROW = C + 2
    FIRST_RESULT = slot_tiles * P + 1

    AHEAD = 4

    with ExitStack() as ctx:
        def sb(name, shape, dt=F32, stack=ctx, partitions=P):
            return stack.enter_context(nc.sbuf_tensor(name, [partitions, *shape], dt))

        def sem(name):
            return ctx.enter_context(nc.semaphore(name))

        psum = ctx.enter_context(nc.psum_tensor("psum", [P, 8, 512], F32))
        bank = [psum[:, n, :] for n in range(8)]
        qk_ps = qkT_ps = bank[0]
        score_ps = psum[:, 1:5, :]
        num_ps = bank[5][:, 0:C].rearrange("p (a t) -> p a t", a=halves)
        den_ps = bank[5][:, C:2 * C].rearrange("p (a t) -> p a t", a=halves)
        state_ps = bank[6][:, 0:halves * VH].rearrange("p (a d) -> p a d", a=halves)
        wo_ps, v_ps = bank[7][:, 0:C], bank[7][:, C:2 * C]
        x1T_ps = wo_ps.rearrange("p (a t) -> p a t", a=halves)
        logitT_ps = bank[7][0:E, C:C + P]
        logits_ps, rank_ps, total_ps = bank[5][:, 0:TE], bank[6][:, 0:TE], bank[7][:, 0:TE]
        gate_ps, up_ps = bank[0], bank[1]
        inT_ps = bank[2][:, 0:C].rearrange("p (a t) -> p a t", a=halves)
        hT_ps = bank[3].rearrange("p (m t) -> p m t", m=inner)
        y_ps = bank[4][:, 0:C]

        ident = sb("ident", [P])
        ones = sb("ones", [P])
        eps_ln = sb("eps_ln", [1])
        eps_attn = sb("eps_attn", [1])
        countdown = sb("countdown", [E])
        words = sb("words", [2, tiles])
        slot_values = sb("slot_values", [3, slot_tiles])
        value_if, expected = slot_values[:, 0:2, :], slot_values[:, 1:3, :]
        router_bias_sb = sb("router_bias_sb", [1], partitions=E)
        weight = sb("weight", [TOP_K, tiles])
        position_i = sb("position_i", [TOP_K, tiles], I32)
        expert_i = sb("expert_i", [slot_tiles], I32, partitions=1)
        index_sb = sb("index_sb", [2, TOP_K, 2], I32)
        back_eq = sb("back_eq", [2])
        back_add = sb("back_add", [2])
        back_row = sb("back_row", [2])
        back_index = sb("back_index", [2], I32)
        turn = sb("turn", [3])
        carried = sb("carried", [2])
        f_stats = sb("f_stats", [4, 6])
        f_moments = sb("f_moments", [2, 4, 2])
        f_std = sb("f_std", [2, 4])
        f_inv = sb("f_inv", [2, 4])
        f_shift = sb("f_shift", [2, 4])
        down_sb = sb("down_sb", [E, DN])
        with ExitStack() as place:
            down_raw = sb("down_raw", [DN], stack=place)
        down_lo = sb("down_lo", [DN], F32R)
        down_hi = sb("down_hi", [DN], F32R)
        send_sb = sb("send_sb", [2, 2, ROW])
        with ExitStack() as place:
            ZERO_TILES = 9
            zero_rows = sb("zero_rows", [ZERO_TILES * ROW], stack=place)
        in_sb = sb("in_sb", [2, ROW])
        in_hi = sb("in_hi", [2, halves, P], F32R)
        in_lo = sb("in_lo", [2, halves, P], F32R)
        h_sb = sb("h_sb", [I])
        with ExitStack() as place:
            hT_sb = sb("hT_sb", [inner, P], stack=place)
        hT_hi = sb("hT_hi", [inner, P], F32R)
        hT_lo = sb("hT_lo", [inner, P], F32R)
        y_sb = sb("y_sb", [2, C])
        add_sb = sb("add_sb", [2, C])
        with ExitStack() as place:
            shared_raw = sb("shared_raw", [2, CHUNK], stack=place)
        shared_lo = sb("shared_lo", [2, CHUNK], F32R)
        shared_hi = sb("shared_hi", [2, CHUNK], F32R)
        with ExitStack() as place:
            def at(name, shape, dt=F32, partitions=P):
                return sb(name, shape, dt, place, partitions)

            wqkv_sb = at("wqkv_sb", [halves, 3 * C])
            wo_sb = at("wo_sb", [halves, C])
            router_sb = at("router_sb", [halves, E])
            bqkv_sb = at("bqkv_sb", [3 * C])
            bo_sb = at("bo_sb", [C])
            gk_sb = at("gk_sb", [C])
            bk_sb = at("bk_sb", [C])
            gb_sb = at("gb_sb", [2, 2 * halves])
            head_block = at("head_block", [P])
            head_of_pair = at("head_of_pair", [2])
            causal = at("causal", [P])
            wqkv_hi = at("wqkv_hi", [halves, 3 * C], F32R)
            wqkv_lo = at("wqkv_lo", [halves, 3 * C], F32R)
            xT_sb = at("xT_sb", [2, halves, P])
            xT_hi = at("xT_hi", [2, halves, P], F32R)
            xT_lo = at("xT_lo", [2, halves, P], F32R)
            x_sb = at("x_sb", [2, C])
            xb_sb = at("xb_sb", [2, C])
            qk_sb = at("qk_sb", [2 * C])
            stats = at("stats", [2, 6])
            moments = at("moments", [2, 2])
            std = at("std", [2])
            std_eps = at("std_eps", [2])
            inv_std = at("inv_std", [2])
            shift = at("shift", [2])
            qkn = at("qkn", [2, 2 * C])
            kerT = at("kerT", [2, 2 * halves, P])
            ksumT = at("ksumT", [2, halves, P])
            prod = at("prod", [2, halves, P])
            k_affine = at("k_affine", [2, C])
            ktok = at("ktok", [2, C])
            q_pair = at("q_pair", [2, halves, 2, P])
            v_raw = at("v_raw", [C])
            v_pair = at("v_pair", [2, HEADS // 2, VB])
            scores = at("scores", [2, HEADS, P])
            state = at("state", [halves, VH])
            den = at("den", [halves, P])
            inv_den = at("inv_den", [halves, P])
            attnT = at("attnT", [2, halves, P])
            res = at("res", [C])
            ln_stats = at("ln_stats", [6])
            ln_moments = at("ln_moments", [2])
            ln_std = at("ln_std", [1])
            ln_inv = at("ln_inv", [1])
            x1_sb = at("x1_sb", [2, C])
            x1T_sb = at("x1T_sb", [halves, P])
        with ExitStack() as place:
            sb("weights_place", [3 * E * CHUNK], stack=place)
            logitsT = sb("logitsT", [tiles * P], stack=place, partitions=E)
            routing = sb("routing", [E * CHUNK - tiles * P], stack=place)
        assert tiles * P <= 4 * CHUNK
        used = [0]

        def room(*shape):
            n, start = 1, used[0]
            for x in shape:
                n *= x
            used[0] += n
            flat_room = routing[:, start:start + n]
            return flat_room.rearrange("p (a b) -> p a b", b=shape[1]) if len(shape) > 1 else flat_room

        def flat(ap):
            return ap.rearrange("p a b -> p (a b)")

        probs, is_top, rest, onehot1, onehot2, member, position, picked = (room(tiles, E) for _ in range(8))
        totals_by_expert, running_by_expert, reset_by_expert = (room(E, tiles) for _ in range(3))
        max1, max2, first, p_sum, p_inv = (room(tiles) for _ in range(5))
        position_f = room(TOP_K, tiles)
        tile_n = room(E).bitcast(I32)
        tile_f, tile_end, slot_base = (room(E) for _ in range(3))
        expert_cmp = room(slot_tiles, E)[0:1]
        expert_f = room(slot_tiles)[0:1]
        before = room(P)
        slot_number = room(slot_tiles)
        with ExitStack() as place:
            own_sb = sb("own_sb", [AHEAD, 4, C], stack=place)
            got_sb = sb("got_sb", [AHEAD, TOP_K, 4, C], stack=place)
            out_sb = sb("out_sb", [2, 4, C], stack=place)
        with ExitStack() as place:
            raw = []
            for what in ("gate", "up"):
                sb(what + "_hi_place", [E * CHUNK], stack=place)
                raw.append(sb(what + "_raw", [E, CHUNK], stack=place))
        gate_hi, gate_lo, up_hi, up_lo = (sb(name, [E, CHUNK], F32R) for name in ("gate_hi", "gate_lo", "up_hi", "up_lo"))
        high, low = (gate_hi, up_hi), (gate_lo, up_lo)
        GATE, UP = 0, 1

        names = """down_hi_done down_lo_done hT_lo_done w_hi_done w_lo_done x_hi_done x_lo_done consts_set masks_set tables_set wqkv_loaded params_loaded gu_loaded zero_set zero_filled down_loaded hi_done lo_done
            qk_mm v_mm qk_biased v_copied v_ready stats_done qk_carry_done aggr_done std_done std_eps_done inv_std_done shift_done norm_done
            qkT_mm ker_done qexp_done scan_done prod_done affine_done ktok_done score_mm mask_done num_mm av_done
            den_done inv_den_done attn_done state_ready wo_mm xb_done res_done ln_stats_done ln_carry_done ln_aggr_done
            ln_std_done ln_inv_done x1_done x1T_mm x1T_done logit_mm logit_done
            eps_set sums_zeroed logitsT_mm probs_done route member_done rank_mm total_mm position_done experts_done
            index_set words_set turn_done back_cmp_done back_add_done back_row_done back_turn_done back_set y_turn_done inT_mm in_hi_done in_lo_done gu_mm silu_done h_done hT_mm hT_done y_mm y_done
            mix_done f_stats_done f_aggr_done f_std_done f_inv_done f_shift_done out_done"""
        s = {n: sem(n) for n in names.split()}
        (down_hi_done, down_lo_done, hT_lo_done, w_hi_done, w_lo_done, x_hi_done, x_lo_done, consts_set, masks_set, tables_set, wqkv_loaded, params_loaded, gu_loaded, zero_set, zero_filled, down_loaded, hi_done, lo_done,
         qk_mm, v_mm, qk_biased, v_copied, v_ready, stats_done, qk_carry_done, aggr_done, std_done, std_eps_done, inv_std_done, shift_done,
         norm_done,
         qkT_mm, ker_done, qexp_done, scan_done, prod_done, affine_done, ktok_done, score_mm, mask_done, num_mm,
         av_done,
         den_done, inv_den_done, attn_done, state_ready, wo_mm, xb_done, res_done, ln_stats_done, ln_carry_done, ln_aggr_done,
         ln_std_done, ln_inv_done, x1_done, x1T_mm, x1T_done, logit_mm, logit_done,
         eps_set, sums_zeroed, logitsT_mm, probs_done, route, member_done, rank_mm, total_mm, position_done,
         experts_done,
         index_set, words_set, turn_done, back_cmp_done, back_add_done, back_row_done, back_turn_done, back_set, y_turn_done, inT_mm, in_hi_done, in_lo_done, gu_mm, silu_done, h_done, hT_mm, hT_done, y_mm, y_done,
         mix_done, f_stats_done, f_aggr_done, f_std_done, f_inv_done, f_shift_done, out_done) = s.values()
        xT_loaded = [sem(f"xT_loaded{b}") for b in range(2)]
        x_loaded = [sem(f"x_loaded{b}") for b in range(2)]
        x1_stored = [sem(f"x1_stored{b}") for b in range(2)]
        send_loaded = [sem(f"send_loaded{b}") for b in range(2)]
        sent = [sem(f"sent{b}") for b in range(2)]
        in_loaded = [sem(f"in_loaded{b}") for b in range(2)]
        add_loaded = [sem(f"add_loaded{b}") for b in range(2)]
        y_stored = [sem(f"y_stored{b}") for b in range(2)]
        y_sent = [sem(f"y_sent{b}") for b in range(2)]
        own_loaded = [sem(f"own_loaded{b}") for b in range(AHEAD)]
        out_stored = [sem(f"out_stored{b}") for b in range(2)]

        params = [(gb_sb[:, :, :], gb_cols), (bqkv_sb[:, :], bqkv.partition_broadcast(P)),
                  (gk_sb[:, :], gk_row.partition_broadcast(P)), (bk_sb[:, :], bk_row.partition_broadcast(P)),
                  (bo_sb[:, :], bo.partition_broadcast(P)), (wo_sb[:, :, :], wo), (router_sb[:, :, :], router),
                  (router_bias_sb[:, :], router_bias.rearrange("(e n) -> e n", n=1))]
        ALL_PARAMS = 16 * len(params)
        ZERO_FILLS = slot_tiles // ZERO_TILES
        assert ZERO_FILLS * ZERO_TILES == slot_tiles
        MASKS = 12
        GOT = 16 * (1 + TOP_K)
        TABLES = 3
        SENT = 16 * 2 * TOP_K

        def v_view(ap):
            return ap.rearrange("p j (r c) -> p j r c", r=2)[:, :, :, 0:D]

        def row_tiles(dram, n, count):
            return dram.rearrange("(n j p) c -> n p j c", p=P, j=count)[bass.ds(n, 1)].rearrange("n p j c -> p (n j) c")

        def row_tile(dram, n):
            return dram.rearrange("(n p) c -> n p c", p=P)[bass.ds(n, 1), :, :].rearrange("n p c -> p (n c)")

        WHOLE = 2

        def whole(t):
            return isinstance(t.index, int) and t.index < WHOLE

        block = ctx.enter_context(nc.Block())

        @block.sync
        def _(sp):
            def load_xT(t, wait_free=True):
                if wait_free and isinstance(t.index, int) and t.index - 2 < WHOLE:
                    sp.wait_ge(v_mm, t.index - 1)
                elif wait_free:
                    sp.wait_ge(x_lo_done, t.index - 1 - WHOLE)
                sp.dma_start(xT_sb[:, t.parity, :, :], xT[bass.ds(t.index, 1)].rearrange("n p a t -> p (n a) t")
                             ).then_inc(xT_loaded[t.parity], 16)

            def load_x(t, wait_free=True):
                if wait_free:
                    sp.wait_ge(xb_done, t.index - 1)
                sp.dma_start(x_sb[:, t.parity, :], x[bass.ds(t.index, 1)].rearrange("n p c -> p (n c)")
                             ).then_inc(x_loaded[t.parity], 16)

            load_xT(Tile(0, 0), False)
            sp.dma_start(wqkv_sb[:, :, :], wqkv).then_inc(wqkv_loaded, 16)
            load_xT(Tile(0, 1), False)
            for dst, src in params:
                sp.dma_start(dst, src).then_inc(params_loaded, 16)
            load_x(Tile(0, 0), False)
            load_x(Tile(0, 1), False)
            fill = slot_rows.rearrange("(n p r) c -> n p (r c)", p=P, r=ZERO_TILES)
            sp.wait_ge(zero_set, 1)
            for n in range(ZERO_FILLS):
                load_xT(Tile(0, n + 2))
                load_x(Tile(0, n + 2))
                sp.dma_start(fill[n], zero_rows[:, :]).then_inc(zero_filled, 16)
            assert ZERO_FILLS % 2 == 0
            first_down = ZERO_FILLS // 2 + 1
            with sp.Fori(first_down, first_down + E) as it:
                for d in range(2):
                    load_xT(Tile(it, d))
                    load_x(Tile(it, d))
                sp.dma_start(down_sb[:, bass.ds(it - first_down, 1), :].rearrange("p e n -> p (e n)"),
                             ffn_w[bass.ds(it - first_down, 1), :, GU:].rearrange("e p n -> p (e n)")
                             ).then_inc(down_loaded, 16)
            for d in range(2):
                load_xT(Tile(first_down + E, d))
                load_x(Tile(first_down + E, d))
            sp.dma_start(down_raw[:, :], ffn_w[E, :, GU:]).then_inc(down_loaded, 16)
            with sp.Fori(first_down + E + 1, tiles // 2) as it:
                for d in range(2):
                    load_xT(Tile(it, d))
                    load_x(Tile(it, d))

            def load_in(t, rows, n, wait_free=True):
                if wait_free:
                    sp.wait_ge(inT_mm, t.index - 1)
                sp.dma_start(in_sb[:, t.parity, 0:C], row_tile(rows, n)).then_inc(in_loaded[t.parity], 16)

            def load_slots(t):
                if isinstance(t.index, int):
                    sp.wait_ge(inT_mm, t.index - 1)
                wait(sp, back_row_done, t.index - 1 - early)
                sp.dma_start(in_sb[:, t.parity, :], row_tile(slot_rows, t.index - early)).then_inc(in_loaded[t.parity], 16)

            def load_add(t, n, wait_free=True):
                if wait_free:
                    sp.wait_ge(y_done, t.index - 1)
                sp.dma_start(add_sb[:, t.parity, :], row_tile(x1_rows, n)).then_inc(add_loaded[t.parity], 16)

            def load_send(u):
                wait(sp, sent[u.parity], u.round * SENT)
                sp.dma_start(send_sb[:, u.parity, :, 0:C], row_tiles(x1_rows, u.index, 2)).then_inc(send_loaded[u.parity], 16)

            sp.wait_ge(zero_filled, 16 * ZERO_FILLS)
            for n in range(2):
                sp.wait_ge(x1_stored[n], 16)
                load_in(Tile(0, n), x1_rows, n, False)
            for b in range(2):
                sp.wait_ge(x1_stored[b], 16 * (tiles // 2))
            for n in range(4):
                load_add(Tile(0, n), n, n >= 2)
                load_in(Tile(0, n + 2), x1_rows, n + 2)
            with sp.Fori(2, pairs // 2) as it:
                for d in range(2):
                    load_in(Tile(it, d + 2), x1_rows, Tile(it, d + 2).index)
                    load_send(Tile(it, d - 4))
                    load_add(Tile(it, d), Tile(it, d).index)
            for n in range(pairs, early):
                load_add(Tile(0, n), n)
                if n + 2 < early:
                    load_in(Tile(0, n + 2), x1_rows, n + 2)
                if n - 4 < pairs:
                    load_send(Tile(0, n - 4))
            for b in range(2):
                sp.wait_ge(sent[b], SENT * (pairs // 2))
            for n in range(early, early + 2):
                load_slots(Tile(0, n))
            with sp.Fori(early // 2 + 1, routed_end // 2) as it:
                for d in range(2):
                    load_slots(Tile(it, d))

            def load_own(q):
                b = q % AHEAD
                wait(sp, out_done, (q - AHEAD + 1) * 4)
                wait(sp, mix_done, (q - AHEAD + 1) * 8)
                for parity in range(2):
                    sp.wait_ge(y_stored[parity], (q * 2 + 2) * 16)
                    sp.wait_ge(y_sent[parity], slot_tiles // 2 * 16)
                sp.dma_start(own_sb[:, b, :, :], row_tiles(sum_rows, q, 4)).then_inc(own_loaded[b], 16)
                for k in range(TOP_K):
                    results = routed_y[FIRST_RESULT + k * tiles * P:FIRST_RESULT + (k + 1) * tiles * P, :]
                    sp.dma_start(got_sb[:, b, k, :, :], row_tiles(results, q, 4)).then_inc(own_loaded[b], 16)

            for n in range(routed_end, routed_end + 2):
                load_in(Tile(0, n), x1_rows, n - slot_tiles)
            for n in range(routed_end, ffn_tiles):
                load_add(Tile(0, n), n - slot_tiles)
                if n + 2 < ffn_tiles:
                    load_in(Tile(0, n + 2), x1_rows, n + 2 - slot_tiles)
                if n % 2:
                    load_own((n - routed_end) // 2)
            for q in range((tiles - early) // 2, quads):
                load_own(q)

        @block.gpsimd
        def _(pool):
            fills = [(ident[:, :], 0.0), (head_block[:, :], 1.0), (head_of_pair[:, :], 1.0), (causal[:, :], 1.0),
                     (before, 1.0), (ones[:, :], 1.0)]
            for dst, value in fills:
                pool.memset(dst, value).then_inc(consts_set, 1)
            pool.wait_ge(consts_set, len(fills))
            blocks = head_block[:, :].rearrange("p (h d) -> p h d", d=D)

            def select(m, op, fill, base, pattern, by_row):
                pool.affine_select(out=m, in_=m, compare_op=op, fill=fill, base=base, pattern=pattern,
                                   channel_multiplier=by_row).then_inc(masks_set, 1)

            select(ident[:, :], ALU.not_equal, 1.0, 0, [[-1, P]], 1)
            select(causal[:, :], ALU.is_ge, 0.0, 0, [[1, P]], -1)
            select(before, ALU.is_ge, 0.0, -1, [[1, P]], -1)
            select(blocks, ALU.is_ge, 0.0, 0, [[-D, hpg], [0, D]], 1)
            pool.memset(v_pair[:, :, :, :], 0.0).then_inc(masks_set, 1)
            pool.wait_ge(masks_set, 5)
            select(blocks, ALU.is_ge, 0.0, D - 1, [[D, hpg], [0, D]], -1)
            pool.wait_ge(masks_set, 6)
            by_pair = head_block[:, :].rearrange("p (j r d) -> p r j d", r=2, d=D)
            pool.tensor_tensor(head_of_pair[:, :], by_pair[:, :, 0, 0], by_pair[:, :, 1, 0], ALU.add).then_inc(masks_set, 1)
            for j in range(2, hpg // 2):
                pool.wait_ge(masks_set, 5 + j)
                pool.tensor_tensor(head_of_pair[:, :], head_of_pair[:, :], by_pair[:, :, j, 0], ALU.add).then_inc(masks_set, 1)
            pool.iota(countdown[:, :], pattern=[[-1, E]], base=E, channel_multiplier=0,
                      allow_small_or_imprecise_dtypes=True).then_inc(masks_set, 1)
            pool.iota(slot_number, pattern=[[1, slot_tiles]], base=0, channel_multiplier=0,
                      allow_small_or_imprecise_dtypes=True).then_inc(masks_set, 1)
            pool.iota(slot_values[:, 1, :], pattern=[[P, slot_tiles]], base=1, channel_multiplier=1,
                      allow_small_or_imprecise_dtypes=True).then_inc(masks_set, 1)
            pool.memset(slot_values[:, 2, :], 0.0).then_inc(tables_set, 1)
            pool.memset(slot_values[:, 0, :], float(tiles * P)).then_inc(tables_set, 1)
            pool.iota(words[:, 1, :], pattern=[[P, tiles]], base=FIRST_RESULT, channel_multiplier=1,
                      allow_small_or_imprecise_dtypes=True).then_inc(tables_set, 1)
            pool.wait_ge(masks_set, MASKS)
            pool.wait_ge(params_loaded, ALL_PARAMS)

            def tile_side(t, split=None):
                i, b = t.index, t.parity
                pool.wait_ge(v_copied, i + 1)
                wait(pool, av_done, i - 1)
                pool.tensor_tensor(v_view(v_pair[:, b, :, :]), v_raw[:, :].rearrange("p (j r d) -> p j r d", r=2, d=D),
                                   bqkv_sb[:, 2 * C:3 * C].rearrange("p (j r d) -> p j r d", r=2, d=D),
                                   ALU.add).then_inc(v_ready, 1)
                if split:
                    other = split.parity
                    pool.wait_ge(x_hi_done, split.index + 1 - WHOLE)
                    pool.tensor_tensor(xT_lo[:, other, :, :], xT_sb[:, other, :, :], xT_hi[:, other, :, :].bitcast(F32),
                                       ALU.subtract).then_inc(x_lo_done, 1)
                for a in range(halves):
                    pool.wait_ge(ker_done, i * 4 + a + 1)
                    wait(pool, score_mm, i * 4 - 4)
                    pool.tensor_tensor(q_pair[:, b, a, :, :],
                                       kerT[:, b, a, :].unsqueeze(1).broadcast_to([P, 2, P]),
                                       head_of_pair[:, :].unsqueeze(2).broadcast_to([P, 2, P]),
                                       ALU.mult).then_inc(qexp_done, 1)
                pool.wait_ge(norm_done, i * 2 + 2)
                wait(pool, ktok_done, i - 1)
                pool.tensor_tensor(k_affine[:, b, :], qkn[:, b, C:2 * C], gk_sb[:, :], ALU.mult).then_inc(affine_done, 1)
                pool.wait_ge(affine_done, i * 2 + 1)
                pool.tensor_tensor(k_affine[:, b, :], k_affine[:, b, :], bk_sb[:, :], ALU.add).then_inc(affine_done, 1)
                pool.wait_ge(scan_done, i * 2 + 2)
                wait(pool, av_done, i - 1)
                pool.tensor_tensor(prod[:, b, :, :], kerT[:, b, 0:halves, :], ksumT[:, b, :, :],
                                   ALU.mult).then_inc(prod_done, 1)
                pool.wait_ge(x_loaded[b], t.round * 16 + 16)
                wait(pool, res_done, i - 1)
                pool.tensor_tensor(xb_sb[:, b, :], x_sb[:, b, :], bo_sb[:, :], ALU.add).then_inc(xb_done, 1)

            tile_side(Tile(0, 0))
            tile_side(Tile(0, 1), Tile(0, 2))
            with pool.Fori(1, tiles // 2 - 1) as it:
                tile_side(Tile(it, 0), Tile(it, 1))
                tile_side(Tile(it, 1), Tile(it, 2))
            tile_side(Tile(0, tiles - 2), Tile(0, tiles - 1))
            tile_side(Tile(0, tiles - 1))

            def carry(done, count, column):
                wait(pool, done, count)
                pool.tensor_tensor(turn[:, column:column + 1], ones[:, 0:1], ones[:, 0:1], ALU.mult).then_inc(done, 1)

            def columns(x, u, count):
                return x[:, :, bass.ds(u.index * count, count)]

            def send(u):
                i, b = u.index, u.parity
                wait(pool, sent[b], u.round * SENT)
                pool.tensor_copy(index_sb[:, b, :, :], columns(position_i, u, 2)).then_inc(index_set, 1)
                pool.tensor_copy(send_sb[:, b, :, C:ROW].rearrange("p j w -> p w j"), columns(words, u, 2)).then_inc(words_set, 1)
                pool.wait_ge(index_set, i + 1)
                pool.wait_ge(words_set, i + 1)
                pool.wait_ge(send_loaded[b], u.round * 16 + 16)
                carry(turn_done, i, 0)
                for j in range(2):
                    for k in range(TOP_K):
                        pool.indirect_dma_start(
                            out=slot_rows, in_=send_sb[:, b, j, :], in_offset=None,
                            out_offset=bass.IndirectOffsetOnAxis(ap=index_sb[:, b, k, j:j + 1], axis=0)
                        ).then_inc(sent[b], 16)

            pool.wait_ge(zero_filled, 16 * ZERO_FILLS)
            pool.wait_ge(tables_set, TABLES)
            pool.wait_ge(position_done, 2)
            for n in range(2):
                send(Tile(0, n))
            with pool.Fori(1, pairs // 2) as it:
                for d in range(2):
                    send(Tile(it, d))

            def send_back(t):
                m, b = t.index - early, t.parity
                pool.wait_ge(back_row_done, m + 1)
                wait(pool, y_sent[b], (t.round - early // 2) * 16)
                carry(back_turn_done, m, 1)
                pool.tensor_copy(back_index[:, b:b + 1], back_row[:, b:b + 1]).then_inc(back_set, 1)
                pool.wait_ge(back_set, m + 1)
                pool.wait_ge(y_done, t.index + 1)
                carry(y_turn_done, m, 2)
                pool.indirect_dma_start(
                    out=routed_y, in_=y_sb[:, b, :], in_offset=None,
                    out_offset=bass.IndirectOffsetOnAxis(ap=back_index[:, b:b + 1], axis=0)).then_inc(y_sent[b], 16)

            for n in range(early, early + 2):
                send_back(Tile(0, n))
            with pool.Fori(early // 2 + 1, routed_end // 2) as it:
                for d in range(2):
                    send_back(Tile(it, d))

        @block.tensor
        def _(pe):
            def products_of_x(dst, t, words):
                b = t.parity
                parts = ((xT_sb, wqkv_sb),) if whole(t) else ((xT_hi, wqkv_hi), (xT_hi, wqkv_lo), (xT_lo, wqkv_hi))
                for a in range(halves):
                    for n, (x_part, w) in enumerate(parts):
                        mm = pe.matmul(dst, x_part[:, b, a, :], w[:, a, words], start=a == 0 and n == 0,
                                       stop=a == halves - 1 and n == len(parts) - 1)
                return mm

            def qk(t):
                i, b = t.index, t.parity
                if whole(t):
                    pe.wait_ge(xT_loaded[b], t.round * 16 + 16)
                else:
                    pe.wait_ge(x_lo_done, i + 1 - WHOLE)
                wait(pe, ker_done, i * 4)
                products_of_x(qk_ps, t, slice(0, 2 * C)).then_inc(qk_mm, 1)

            def values(t):
                i, b = t.index, t.parity
                wait(pe, v_copied, i)
                wait(pe, logit_done, i - 2)
                products_of_x(v_ps, t, slice(2 * C, 3 * C)).then_inc(v_mm, 1)

            def turn_qk(t):
                i, b = t.index, t.parity
                pe.wait_ge(norm_done, i * 2 + 2)
                for n in range(2 * halves):
                    mm = pe.transpose(qkT_ps[:, n * P:(n + 1) * P], qkn[:, b, n * P:(n + 1) * P], ident[:, :])
                mm.then_inc(qkT_mm, 1)

            def score(t):
                i, b = t.index, t.parity
                pe.wait_ge(ker_done, i * 4 + 4)
                for a in range(halves):
                    pe.wait_ge(qexp_done, i * 2 + a + 1)
                    if a == 0:
                        wait(pe, mask_done, i * 4)
                    for j in range(hpg // 2):
                        rows = slice(j * VH, (j + 1) * VH)
                        mm = pe.matmul(score_ps[:, j, a * 2 * P:(a + 1) * 2 * P], kerT[rows, b, halves + a, :],
                                       q_pair[rows, b, a, :, :].rearrange("p r t -> p (r t)"), start=True, stop=True,
                                       skip_group_check=True)
                        if a == halves - 1:
                            mm.then_inc(score_mm, 1)

            def attend(t):
                i, b = t.index, t.parity
                pe.wait_ge(mask_done, i * 4 + 4)
                pe.wait_ge(v_ready, i + 1)
                pe.wait_ge(state_ready, i + 1)
                wait(pe, attn_done, i)
                for a in range(halves):
                    for r in range(2):
                        for j in range(hpg // 2):
                            pair = a * (hpg // 2) + j
                            pe.matmul(num_ps[j * VH:(j + 1) * VH, a, :], v_pair[:, b, pair, r * VH:(r + 1) * VH],
                                      scores[:, b, pair * 2 + r, :], start=r == 0, stop=False, skip_group_check=True)
                    for j in range(hpg // 2):
                        rows = slice(j * VH, (j + 1) * VH)
                        pe.matmul(num_ps[rows, a, :], state[rows, a, :], kerT[rows, b, a, :], start=False, stop=True,
                                  skip_group_check=True)

            def denominators_and_sums(t):
                i, b = t.index, t.parity
                pe.wait_ge(prod_done, i + 1)
                for a in range(halves):
                    mm = pe.matmul(den_ps[:, a, :], head_block[:, :], prod[:, b, a, :], start=True, stop=True,
                                   skip_group_check=True)
                mm.then_inc(num_mm, 1)
                pe.wait_ge(ktok_done, i + 1)
                for a in range(halves):
                    for j in range(hpg // 2):
                        pair = a * (hpg // 2) + j
                        mm = pe.matmul(state_ps[j * VH:(j + 1) * VH, a, :], ktok[:, b, pair * VH:(pair + 1) * VH],
                                       v_view(v_pair[:, b, pair:pair + 1, :]).rearrange("p j r d -> p (j r) d"),
                                       start=False, stop=False, skip_group_check=True)
                mm.then_inc(av_done, 1)

            def project(t, after=None):
                i, b = t.index, t.parity
                if after:
                    pe.wait_ge(v_copied, after.index + 1)
                else:
                    pe.wait_ge(logit_done, i)
                pe.wait_ge(attn_done, i + 1)
                for a in range(halves):
                    mm = pe.matmul(wo_ps, attnT[:, b, a, :], wo_sb[:, a, :], start=a == 0, stop=a == halves - 1)
                mm.then_inc(wo_mm, 1)

            def turn_x1(t):
                i, b = t.index, t.parity
                pe.wait_ge(x1_done, i + 1)
                for a in range(halves):
                    mm = pe.transpose(x1T_ps[:, a, :], x1_sb[:, b, a * P:(a + 1) * P], ident[:, :])
                mm.then_inc(x1T_mm, 1)

            def logit(t):
                pe.wait_ge(x1T_done, t.index + 1)
                for a in range(halves):
                    mm = pe.matmul(logitT_ps, router_sb[:, a, :], x1T_sb[:, a, :], start=a == 0, stop=a == halves - 1)
                mm.then_inc(logit_mm, 1)

            def turn_in(t):
                i, b = t.index, t.parity
                pe.wait_ge(in_loaded[b], t.round * 16 + 16)
                wait(pe, in_lo_done, i)
                for a in range(halves):
                    mm = pe.transpose(inT_ps[:, a, :], in_sb[:, b, a * P:(a + 1) * P], ident[:, :])
                mm.then_inc(inT_mm, 1)

            def gate_up(t, e):
                i, b = t.index, t.parity
                pe.wait_ge(in_lo_done, i + 1)
                if e is None:
                    pe.wait_ge(lo_done, 2)
                wait(pe, h_done, i)
                for which, dst in ((GATE, gate_ps), (UP, up_ps)):
                    if e is None:
                        w_hi, w_lo = shared_hi[:, which, :], shared_lo[:, which, :]
                    else:
                        w_hi, w_lo = (w[which][:, bass.ds(e, 1), :].rearrange("p e n -> p (e n)") for w in (high, low))
                    for a in range(halves):
                        words = slice(a * I, (a + 1) * I)
                        for n, (x_part, w) in enumerate(((in_hi, w_hi), (in_hi, w_lo), (in_lo, w_hi))):
                            mm = pe.matmul(dst, x_part[:, b, a, :], w[:, words], start=a == 0 and n == 0,
                                           stop=a == halves - 1 and n == 2)
                    mm.then_inc(gu_mm, 1)

            def step(after, now, last):
                if after:
                    qk(after)
                    values(after)
                score(now)
                if last:
                    project(last, after)
                if after:
                    turn_qk(after)
                attend(now)
                if last:
                    turn_x1(last)
                if not after:
                    turn_in(Tile(0, 0))
                denominators_and_sums(now)
                if last:
                    logit(last)

            pe.wait_ge(zero_set, 1)
            pe.matmul(bank[6][:, 0:halves * VH], zero_rows[:, 0:P], zero_rows[:, 0:halves * VH], start=True, stop=False,
                      skip_group_check=True)
            pe.wait_ge(wqkv_loaded, 16)
            qk(Tile(0, 0))
            values(Tile(0, 0))
            pe.wait_ge(masks_set, MASKS)
            pe.wait_ge(params_loaded, ALL_PARAMS)
            turn_qk(Tile(0, 0))
            step(Tile(0, 1), Tile(0, 0), None)
            pe.wait_ge(w_lo_done, 1)
            step(Tile(0, 2), Tile(0, 1), Tile(0, 0))
            step(Tile(0, 3), Tile(0, 2), Tile(0, 1))
            with pe.Fori(1, tiles // 2 - 1) as it:
                step(Tile(it, 2), Tile(it, 1), Tile(it, 0))
                step(Tile(it, 3), Tile(it, 2), Tile(it, 1))
            last = Tile(0, tiles - 1)
            step(None, last, Tile(0, tiles - 2))
            gate_up(Tile(0, 0), None)
            project(last)
            turn_x1(last)
            logit(last)

            pe.wait_ge(logit_done, tiles)
            for n in range(tiles):
                mm = pe.transpose(logits_ps[:, n * E:(n + 1) * E], logitsT[:, n * P:(n + 1) * P], ident[0:E, 0:E])
            mm.then_inc(logitsT_mm, 1)

            def turn_h(t, own_last=None):
                i = t.index
                pe.wait_ge(h_done, i + 1)
                if own_last is None:
                    wait(pe, hT_done, i)
                else:
                    pe.wait_ge(hT_lo_done, i - own_last)
                for m in range(inner):
                    mm = pe.transpose(hT_ps[:, m, :], h_sb[:, m * P:(m + 1) * P], ident[:, :])
                mm.then_inc(hT_mm, 1)

            def down(t, e, own=None):
                i = t.index
                if own is None:
                    pe.wait_ge(hT_done, i + 1)
                else:
                    pe.wait_ge(hT_lo_done, i + 1 - own)
                wait(pe, y_done, i)
                for m in range(inner):
                    words = slice(m * C, (m + 1) * C)
                    if own is None:
                        parts = ((hT_sb, down_sb[:, bass.ds(e, 1), words].rearrange("p e n -> p (e n)")),)
                    else:
                        parts = ((hT_hi, down_hi[:, words]), (hT_hi, down_lo[:, words]), (hT_lo, down_hi[:, words]))
                    for n, (h_part, w) in enumerate(parts):
                        mm = pe.matmul(y_ps, h_part[:, m, :], w, start=m == 0 and n == 0,
                                       stop=m == inner - 1 and n == len(parts) - 1)
                mm.then_inc(y_mm, 1)

            def ffn_step(now, e=None, last=None, e_last=None, after=None, between=None, own_last=None):
                gate_up(now, e)
                if between:
                    between()
                if after:
                    turn_in(after)
                if last:
                    down(last, e_last() if callable(e_last) else e_last, own_last)
                turn_h(now, own_last)

            def own_step(it, d, between=None, own_last=0):
                ffn_step(Tile(it, d), None, Tile(it, d - 1), None, Tile(it, d + 1), between, own_last)

            def ranks():
                pe.wait_ge(member_done, 1)
                pe.matmul(rank_ps, before, flat(member), start=True, stop=True).then_inc(rank_mm, 1)
                pe.matmul(total_ps, ones[:, :], flat(member), start=True, stop=True).then_inc(total_mm, 1)

            turn_in(Tile(0, 1))
            turn_h(Tile(0, 0))
            pe.wait_ge(down_loaded, 16 * (E + 1))
            pe.wait_ge(down_lo_done, 1)
            own_step(0, 1)
            own_step(0, 2, ranks)
            with pe.Fori(1, early // 2 - 1) as it:
                own_step(it, 1)
                own_step(it, 2)
            own_step(0, early - 1)
            pe.wait_ge(experts_done, 1)
            pe.wait_ge(lo_done, 2 * E + 2)

            def expert(n):
                return pe.value_load(expert_i[0:1, bass.ds(n, 1)], min_val=0, max_val=E - 1)

            ffn_step(Tile(0, early), expert(0), Tile(0, early - 1), None, Tile(0, early + 1), own_last=0)
            with pe.Fori(0, (slot_tiles - 2) // 2) as it:
                e_last = lambda: expert(it * 2)
                for d in range(1, 3):
                    e = expert(it * 2 + d)
                    ffn_step(Tile(it * 1, early + d), e, Tile(it * 1, early + d - 1), e_last, Tile(it * 1, early + d + 1))
                    e_last = e
            e_last = expert(slot_tiles - 1)
            e_before = expert(slot_tiles - 2)
            n = routed_end - 1
            ffn_step(Tile(0, n), e_last, Tile(0, n - 1), e_before, Tile(0, n + 1))
            ffn_step(Tile(0, n + 1), None, Tile(0, n), e_last, Tile(0, n + 2))
            with pe.Fori(routed_end // 2, ffn_tiles // 2 - 1) as it:
                own_step(it, 1, own_last=slot_tiles)
                own_step(it, 2, own_last=slot_tiles)
            n = ffn_tiles - 1
            ffn_step(Tile(0, n), None, Tile(0, n - 1), None, own_last=slot_tiles)
            down(Tile(0, n), None, slot_tiles)

        @block.scalar
        def _(act):

            def split_hi(e, which):
                dst, src = (w[which][:, bass.ds(e, 1), :].rearrange("p e n -> p (e n)") for w in (high, raw))
                act.activation(dst, src, ACT.Copy).then_inc(hi_done, 1)

            def qk_std(t):
                act.wait_ge(aggr_done, t.index * 2 + 2)
                wait(act, std_eps_done, t.index)
                act.activation(std[:, :], moments[:, :, 1], ACT.Sqrt, scale=C / (C - 1)).then_inc(std_done, 1)

            def normalise(t):
                i, b = t.index, t.parity
                act.wait_ge(shift_done, i + 1)
                wait(act, qkT_mm, i - 1)
                wait(act, affine_done, i * 2 - 2)
                for n in range(2):
                    act.activation(qkn[:, b, n * C:(n + 1) * C], qk_sb[:, n * C:(n + 1) * C], ACT.Identity,
                                   scale=inv_std[:, n:n + 1], bias=shift[:, n:n + 1]).then_inc(norm_done, 1)

            def copy_v(t):
                act.wait_ge(v_mm, t.index + 1)
                wait(act, v_ready, t.index)
                act.activation(v_raw[:, :], v_ps, ACT.Copy).then_inc(v_copied, 1)

            def features(t):
                i, b = t.index, t.parity
                act.wait_ge(qkT_mm, i + 1)
                wait(act, av_done, i - 1)
                for n in range(2 * halves):
                    act.activation(kerT[:, b, n, :], qkT_ps[:, n * P:(n + 1) * P], ACT.Square,
                                   scale=gb_sb[:, 0, n:n + 1], bias=gb_sb[:, 1, n:n + 1]).then_inc(ker_done, 1)

            def key_rows(t):
                i, b = t.index, t.parity
                act.wait_ge(affine_done, i * 2 + 2)
                wait(act, av_done, i - 1)
                act.activation(ktok[:, b, :], k_affine[:, b, :], ACT.Square).then_inc(ktok_done, 1)

            def denominators(t):
                i = t.index
                act.wait_ge(num_mm, i + 1)
                wait(act, inv_den_done, i)
                act.activation(den[:, :, :], den_ps, ACT.Identity, bias=eps_attn[:, :]).then_inc(den_done, 1)

            def x1_std(t):
                act.wait_ge(ln_aggr_done, t.index + 1)
                wait(act, ln_inv_done, t.index)
                act.activation(ln_std[:, :], ln_moments[:, 1:2], ACT.Sqrt, bias=eps_ln[:, :]).then_inc(ln_std_done, 1)

            def x1_out(t):
                i, b = t.index, t.parity
                act.wait_ge(x1_done, i + 1)
                act.dma_start(row_tile(x1_rows, i), x1_sb[:, b, :]).then_inc(x1_stored[b], 16)
                act.wait_ge(x1T_mm, i + 1)
                wait(act, logit_mm, i)
                act.activation(x1T_sb[:, :, :], x1T_ps, ACT.Copy).then_inc(x1T_done, 1)

            def logit_out(t):
                act.wait_ge(logit_mm, t.index + 1)
                act.activation(logitsT[:, bass.ds(t.index * P, P)], logitT_ps, ACT.Identity,
                               bias=router_bias_sb[:, :]).then_inc(logit_done, 1)

            def copy_in(t):
                i, b = t.index, t.parity
                act.wait_ge(inT_mm, i + 1)
                wait(act, gu_mm, i * 2 - 2)
                act.activation(in_hi[:, b, :, :], inT_ps, ACT.Copy).then_inc(in_hi_done, 1)

            def silu(t):
                i = t.index
                act.wait_ge(gu_mm, i * 2 + 1)
                wait(act, hT_mm, i)
                act.activation(h_sb[:, :], gate_ps, ACT.Silu).then_inc(silu_done, 1)

            def split_shared_hi():
                act.wait_ge(gu_loaded, 16)
                for which in (GATE, UP):
                    act.activation(shared_hi[:, which, :], shared_raw[:, which, :], ACT.Copy).then_inc(hi_done, 1)
                act.wait_ge(down_loaded, 16 * (E + 1))
                act.activation(down_hi[:, :], down_raw[:, :], ACT.Copy).then_inc(down_hi_done, 1)

            def split_x_hi(t):
                i, b = t.index, t.parity
                act.wait_ge(xT_loaded[b], t.round * 16 + 16)
                act.wait_ge(v_mm, i - 1)
                act.activation(xT_hi[:, b, :, :], xT_sb[:, b, :, :], ACT.Copy).then_inc(x_hi_done, 1)

            def step(after, now, last, split=None):
                key_rows(now)
                if not after:
                    split_shared_hi()
                if after:
                    copy_v(after)
                if split:
                    split_x_hi(split)
                if after:
                    qk_std(after)
                    normalise(after)
                if last:
                    x1_std(last)
                if after:
                    features(after)
                if last:
                    x1_out(last)
                if not after:
                    copy_in(Tile(0, 0))
                denominators(now)
                if last:
                    logit_out(last)

            act.wait_ge(eps_set, 2)
            act.wait_ge(params_loaded, ALL_PARAMS)
            qk_std(Tile(0, 0))
            normalise(Tile(0, 0))
            copy_v(Tile(0, 0))
            features(Tile(0, 0))
            act.wait_ge(wqkv_loaded, 16)
            act.activation(wqkv_hi[:, :, :], wqkv_sb[:, :, :], ACT.Copy).then_inc(w_hi_done, 1)
            step(Tile(0, 1), Tile(0, 0), None, Tile(0, 2))
            step(Tile(0, 2), Tile(0, 1), Tile(0, 0), Tile(0, 3))
            act.dma_start(shared_raw[:, :, :], ffn_w[E, :, 0:GU].rearrange("p (w n) -> p w n", w=2)).then_inc(gu_loaded, 16)
            step(Tile(0, 3), Tile(0, 2), Tile(0, 1), Tile(0, 4))
            with act.Fori(1, tiles // 2 - 2) as it:
                step(Tile(it, 2), Tile(it, 1), Tile(it, 0), Tile(it, 3))
                step(Tile(it, 3), Tile(it, 2), Tile(it, 1), Tile(it, 4))
            it = tiles // 2 - 2
            step(Tile(it, 2), Tile(it, 1), Tile(it, 0), Tile(it, 3))
            step(Tile(it, 3), Tile(it, 2), Tile(it, 1))
            last = Tile(0, tiles - 1)
            step(None, last, Tile(0, tiles - 2))
            x1_std(last)
            silu(Tile(0, 0))
            x1_out(last)
            logit_out(last)

            act.wait_ge(logitsT_mm, 1)
            for b in range(2):
                act.wait_ge(x1_stored[b], 16 * (tiles // 2))
            act.activation(flat(probs), logits_ps, ACT.Sigmoid).then_inc(probs_done, 1)

            def load_expert(e):
                for which in (GATE, UP):
                    act.dma_start(raw[which][:, bass.ds(e, 1), :].rearrange("p e n -> p (e n)"),
                                  ffn_w[bass.ds(e, 1), :, which * CHUNK:(which + 1) * CHUNK].rearrange("e p n -> p (e n)")
                                  ).then_inc(gu_loaded, 16)

            act.wait_ge(state_ready, tiles + 1)
            load_expert(0)

            def copy_h(t, routed=False):
                i = t.index
                act.wait_ge(hT_mm, i + 1)
                wait(act, y_mm, i)
                act.activation((hT_sb if routed else hT_hi)[:, :, :], hT_ps, ACT.Copy).then_inc(hT_done, 1)

            def copy_y(t):
                i, b = t.index, t.parity
                act.wait_ge(y_mm, i + 1)
                wait(act, y_sent[b], (t.round - early // 2) * 16)
                if isinstance(t.index, int):
                    act.wait_ge(y_stored[b], early // 2 * 16)
                act.activation(y_sb[:, b, :], y_ps, ACT.Copy).then_inc(y_done, 1)

            def store_y(t, n):
                i, b = t.index, t.parity
                act.wait_ge(y_done, i + 1)
                act.dma_start(row_tile(sum_rows, n), y_sb[:, b, :]).then_inc(y_stored[b], 16)

            def split_hi_chunk(t):
                if t.parity == 0:
                    act.wait_ge(gu_loaded, t.round * 32 + 16)
                split_hi(t.round - 1, t.parity)

            def ffn_step(now, after=None, last=None, n=None, routed=False, chunk=False, load=True, between=None,
                         routed_now=False):
                silu(now)
                if after:
                    copy_in(after)
                if between:
                    between()
                if chunk:
                    split_hi_chunk(now)
                if last and routed:
                    copy_y(last)
                copy_h(now, routed_now)
                if last and not routed:
                    store_y(last, n)
                if chunk and load and now.parity == 0:
                    load_expert(now.round)

            def deviations(q):
                act.wait_ge(f_aggr_done, q * 4 + 4)
                wait(act, f_inv_done, q - 1)
                act.activation(f_std[:, q % 2, :], f_moments[:, q % 2, :, 1], ACT.Sqrt,
                               bias=eps_ln[:, :]).then_inc(f_std_done, 1)

            def normalise_quad(q):
                b = q % 2
                act.wait_ge(f_shift_done, q + 1)
                wait(act, out_stored[b], q // 2 * 16)
                for j in range(4):
                    act.activation(out_sb[:, b, j, :], own_sb[:, q % AHEAD, j, :], ACT.Identity, scale=f_inv[:, b, j:j + 1],
                                   bias=f_shift[:, b, j:j + 1]).then_inc(out_done, 1)

            def store_quad(q):
                act.wait_ge(out_done, q * 4 + 4)
                act.dma_start(row_tiles(out, q, 4), out_sb[:, q % 2, :, :]).then_inc(out_stored[q % 2], 16)

            copy_in(Tile(0, 1))
            copy_h(Tile(0, 0))
            ffn_step(Tile(0, 1), Tile(0, 2), Tile(0, 0), 0)
            ffn_step(Tile(0, 2), Tile(0, 3), Tile(0, 1), 1, chunk=True)
            ffn_step(Tile(0, 3), Tile(0, 4), Tile(0, 2), 2, chunk=True)
            ffn_step(Tile(0, 4), Tile(0, 5), Tile(0, 3), 3, chunk=True)
            act.wait_ge(experts_done, 1)
            with act.Fori(2, E - 1) as it:
                for d in (1, 2):
                    ffn_step(Tile(it, d), Tile(it, d + 1), Tile(it, d - 1), it * 2 + d - 1, chunk=True)
            for n in range(2 * E - 1, early + 1):
                ffn_step(Tile(0, n), Tile(0, n + 1), Tile(0, n - 1), n - 1, chunk=n < 2 * E + 2, load=False,
                         routed_now=n >= early)
            for n in range(early + 1, early + 3):
                ffn_step(Tile(0, n), Tile(0, n + 1), Tile(0, n - 1), routed=True, routed_now=True)
            with act.Fori(early // 2 + 1, routed_end // 2 - 1) as it:
                for d in (1, 2):
                    ffn_step(Tile(it, d), Tile(it, d + 1), Tile(it, d - 1), routed=True, routed_now=True)
            for n in (routed_end - 1, routed_end):
                ffn_step(Tile(0, n), Tile(0, n + 1), Tile(0, n - 1), routed=True, routed_now=n < routed_end)
            for n in range(routed_end + 1, ffn_tiles):
                t = Tile(0, n)
                q, half = (n - routed_end) // 2 - 2, (n - routed_end) % 2
                between = None if q < 0 else (lambda: normalise_quad(q)) if half else (lambda: deviations(q))
                ffn_step(t, Tile(0, n + 1) if n + 1 < ffn_tiles else None, Tile(0, n - 1), n - 1 - slot_tiles,
                         between=between)
                if q >= 0 and half:
                    store_quad(q)
            store_y(Tile(0, n), n - slot_tiles)
            for q in range((tiles - early) // 2 - 2, quads):
                deviations(q)
                normalise_quad(q)
                store_quad(q)
            for b in range(2):
                act.wait_ge(out_stored[b], 16 * (quads // 2))

        @block.vector
        def _(dve):
            def split_lo(t):
                part_hi, part_lo, part_raw = (w[t.parity][:, bass.ds(t.round - 1, 1), :].rearrange("p e n -> p (e n)")
                                              for w in (high, low, raw))
                dve.wait_ge(hi_done, t.index + 1)
                dve.tensor_tensor(part_lo, part_raw, part_hi.bitcast(F32), ALU.subtract).then_inc(lo_done, 1)

            def split_shared_lo():
                for which in (GATE, UP):
                    dve.wait_ge(hi_done, which + 1)
                    dve.tensor_tensor(shared_lo[:, which, :], shared_raw[:, which, :], shared_hi[:, which, :].bitcast(F32),
                                      ALU.subtract).then_inc(lo_done, 1)
                dve.wait_ge(down_hi_done, 1)
                dve.tensor_tensor(down_lo[:, :], down_raw[:, :], down_hi[:, :].bitcast(F32),
                                  ALU.subtract).then_inc(down_lo_done, 1)

            def bias_qk(t):
                i, b = t.index, t.parity
                dve.wait_ge(qk_mm, i + 1)
                wait(dve, norm_done, i * 2)
                dve.tensor_tensor(qk_sb[:, :], qk_ps, bqkv_sb[:, 0:2 * C], ALU.add).then_inc(qk_biased, 1)
                wait(dve, aggr_done, i * 2)
                dve.wait_ge(qk_biased, i + 1)
                for n in range(2):
                    dve.bn_stats(stats[:, n, :], qk_sb[:, n * C:(n + 1) * C]).then_inc(stats_done, 1)

            def qk_moments(t):
                dve.wait_ge(stats_done, t.index * 2 + 2)
                wait(dve, qk_carry_done, t.index)
                dve.tensor_tensor(carried[:, 0:1], ones[:, 0:1], ones[:, 0:1], ALU.mult).then_inc(qk_carry_done, 1)
                for n in range(2):
                    dve.bn_aggr(moments[:, n, :], stats[:, n, :]).then_inc(aggr_done, 1)

            def qk_scales(t):
                i = t.index
                dve.wait_ge(std_done, i + 1)
                dve.tensor_scalar(std_eps[:, :], std[:, :], EPS_ATTN, None, ALU.add).then_inc(std_eps_done, 1)
                dve.wait_ge(std_eps_done, i + 1)
                dve.reciprocal(inv_std[:, :], std_eps[:, :]).then_inc(inv_std_done, 1)
                dve.wait_ge(inv_std_done, i + 1)
                dve.scalar_tensor_tensor(out=shift[:, :], in0=moments[:, :, 0], scalar=-1.0, in1=inv_std[:, :],
                                         op0=ALU.mult, op1=ALU.mult).then_inc(shift_done, 1)

            def mask(t, j):
                i, b = t.index, t.parity
                dve.wait_ge(score_mm, i * 4 + j + 1)
                wait(dve, av_done, i - 1)
                dve.tensor_tensor(
                    scores[:, b, :, :].rearrange("p (a j r) t -> p j a r t", a=halves, r=2)[:, j],
                    score_ps[:, j, :].rearrange("p (a r t) -> p a r t", a=halves, r=2),
                    causal[:, :].unsqueeze(1).unsqueeze(1).broadcast_to([P, halves, 2, P]), ALU.mult).then_inc(mask_done, 1)

            def key_sums(t):
                i, b = t.index, t.parity
                dve.wait_ge(ker_done, i * 4 + 4)
                wait(dve, prod_done, i - 1)
                wait(dve, scan_done, i * 2)
                for a in range(halves):
                    dve.tensor_tensor_scan(ksumT[:, b, a, :], ones[:, :], kerT[:, b, halves + a, :],
                                           ksumT[:, 1 - b, a, P - 1:P], ALU.mult, ALU.add).then_inc(scan_done, 1)

            def attn_out(t):
                i, b = t.index, t.parity
                dve.wait_ge(den_done, i + 1)
                wait(dve, attn_done, i)
                dve.reciprocal(inv_den[:, :, :], den[:, :, :]).then_inc(inv_den_done, 1)
                dve.wait_ge(inv_den_done, i + 1)
                wait(dve, wo_mm, i - 1)
                dve.tensor_tensor(attnT[:, b, :, :], num_ps, inv_den[:, :, :], ALU.mult).then_inc(attn_done, 1)

            def add_state(t):
                i = t.index
                dve.wait_ge(av_done, i + 1)
                dve.tensor_tensor(state[:, :, :].rearrange("p a (r d) -> p a r d", d=D),
                                  state_ps.rearrange("p a (r d) -> p a r d", d=D),
                                  head_of_pair[:, :].unsqueeze(1).unsqueeze(3).broadcast_to([P, halves, 2, D]),
                                  ALU.mult).then_inc(state_ready, 1)

            def residual(t):
                i, b = t.index, t.parity
                dve.wait_ge(wo_mm, i + 1)
                dve.wait_ge(xb_done, i + 1)
                wait(dve, x1_done, i)
                dve.tensor_tensor(res[:, :], wo_ps, xb_sb[:, b, :], ALU.add).then_inc(res_done, 1)
                dve.wait_ge(res_done, i + 1)
                wait(dve, ln_aggr_done, i)
                dve.bn_stats(ln_stats[:, :], res[:, :]).then_inc(ln_stats_done, 1)

            def x1_moments(t):
                dve.wait_ge(ln_stats_done, t.index + 1)
                wait(dve, ln_carry_done, t.index)
                dve.tensor_tensor(carried[:, 1:2], ones[:, 0:1], ones[:, 0:1], ALU.mult).then_inc(ln_carry_done, 1)
                dve.bn_aggr(ln_moments[:, :], ln_stats[:, :]).then_inc(ln_aggr_done, 1)

            def make_x1(t):
                i, b = t.index, t.parity
                dve.wait_ge(ln_std_done, i + 1)
                dve.reciprocal(ln_inv[:, :], ln_std[:, :]).then_inc(ln_inv_done, 1)
                dve.wait_ge(ln_inv_done, i + 1)
                if not isinstance(t.round, int) or t.round > 0:
                    dve.wait_ge(x1_stored[b], t.round * 16)
                    dve.wait_ge(x1T_mm, i - 1)
                dve.tensor_scalar(x1_sb[:, b, :], res[:, :], ln_moments[:, 0:1], ln_inv[:, 0:1],
                                  ALU.subtract, ALU.mult).then_inc(x1_done, 1)

            def low_in(t):
                i, b = t.index, t.parity
                dve.wait_ge(in_hi_done, i + 1)
                dve.tensor_tensor(in_lo[:, b, :, :], inT_ps, in_hi[:, b, :, :].bitcast(F32),
                                  ALU.subtract).then_inc(in_lo_done, 1)

            def low_h(t):
                dve.wait_ge(hT_done, t.index + 1)
                dve.tensor_tensor(hT_lo[:, :, :], hT_ps, hT_hi[:, :, :].bitcast(F32), ALU.subtract).then_inc(hT_lo_done, 1)

            def hidden(t):
                i = t.index
                dve.wait_ge(silu_done, i + 1)
                dve.wait_ge(gu_mm, i * 2 + 2)
                dve.tensor_tensor(h_sb[:, :], up_ps, h_sb[:, :], ALU.mult).then_inc(h_done, 1)

            def step(after, now, last):
                if after:
                    bias_qk(after)
                    qk_moments(after)
                mask(now, 0)
                if after:
                    qk_scales(after)
                for j in range(1, hpg // 2):
                    mask(now, j)
                if last:
                    residual(last)
                    x1_moments(last)
                    make_x1(last)
                if after:
                    key_sums(after)
                if not after:
                    split_shared_lo()
                    low_in(Tile(0, 0))
                attn_out(now)
                add_state(now)

            dve.memset(zero_rows[:, :], 0.0).then_inc(zero_set, 1)
            dve.memset(eps_ln[:, :], EPS_LN).then_inc(eps_set, 1)
            dve.memset(eps_attn[:, :], EPS_ATTN).then_inc(eps_set, 1)
            dve.memset(state[:, :, :], 0.0).then_inc(state_ready, 1)
            dve.memset(ksumT[:, 1, :, :], 0.0).then_inc(sums_zeroed, 1)
            dve.wait_ge(sums_zeroed, 1)
            dve.wait_ge(masks_set, MASKS)
            dve.wait_ge(params_loaded, ALL_PARAMS)
            bias_qk(Tile(0, 0))
            qk_moments(Tile(0, 0))
            qk_scales(Tile(0, 0))
            key_sums(Tile(0, 0))
            dve.wait_ge(w_hi_done, 1)
            dve.tensor_tensor(wqkv_lo[:, :, :], wqkv_sb[:, :, :], wqkv_hi[:, :, :].bitcast(F32),
                              ALU.subtract).then_inc(w_lo_done, 1)
            step(Tile(0, 1), Tile(0, 0), None)
            step(Tile(0, 2), Tile(0, 1), Tile(0, 0))
            step(Tile(0, 3), Tile(0, 2), Tile(0, 1))
            with dve.Fori(1, tiles // 2 - 1) as it:
                step(Tile(it, 2), Tile(it, 1), Tile(it, 0))
                step(Tile(it, 3), Tile(it, 2), Tile(it, 1))
            last = Tile(0, tiles - 1)
            step(None, last, Tile(0, tiles - 2))
            residual(last)
            x1_moments(last)
            make_x1(last)

            chained = [0]

            def link(ins):
                chained[0] += 1
                ins.then_inc(route, 1)
                dve.wait_ge(route, chained[0])

            def over_experts(x):
                return x.unsqueeze(2).broadcast_to([P, tiles, E])

            def over_tiles(x):
                return x.unsqueeze(1).broadcast_to([P, tiles, E])

            def pick(onehot, values, best):
                link(dve.tensor_reduce(best, values, AX_X, ALU.max))
                link(dve.tensor_tensor(is_top, values, over_experts(best), ALU.is_equal))
                link(dve.tensor_tensor(picked, is_top, over_tiles(countdown[:, :]), ALU.mult))
                link(dve.tensor_reduce(first, picked, AX_X, ALU.max))
                link(dve.tensor_tensor(onehot, over_tiles(countdown[:, :]), over_experts(first), ALU.is_equal))

            def sum_y(t, late):
                i, b = t.index, t.parity
                dve.wait_ge(y_mm, i + 1)
                dve.wait_ge(add_loaded[b], t.round * 16 + 16 - (slot_tiles // 2 * 16 if late else 0))
                wait(dve, y_stored[b], (t.round - (slot_tiles // 2 if late else 0)) * 16)
                if late:
                    dve.wait_ge(y_sent[b], slot_tiles // 2 * 16)
                dve.tensor_tensor(y_sb[:, b, :], y_ps, add_sb[:, b, :], ALU.add).then_inc(y_done, 1)

            EARLY, ROUTED, LATE = range(3)

            def find_back(t):
                m, b = t.index - early, t.parity

                def slot_column(x):
                    return x[:, :, bass.ds(m, 1)].rearrange("p w n -> p (w n)")

                dve.wait_ge(in_loaded[b], t.round * 16 + 16)
                wait(dve, back_add_done, m)
                dve.tensor_tensor(back_eq[:, :], in_sb[:, b, C:ROW], slot_column(expected), ALU.is_equal
                                  ).then_inc(back_cmp_done, 1)
                dve.wait_ge(back_cmp_done, m + 1)
                wait(dve, back_row_done, m)
                dve.tensor_tensor(back_add[:, :], back_eq[:, :], slot_column(value_if), ALU.mult).then_inc(back_add_done, 1)
                dve.wait_ge(back_add_done, m + 1)
                wait(dve, back_set, m - 1)
                dve.scalar_tensor_tensor(out=back_row[:, b:b + 1], in0=back_add[:, 0:1], scalar=back_add[:, 1:2],
                                         in1=in_sb[:, b, C + 1:ROW], op0=ALU.add, op1=ALU.add).then_inc(back_row_done, 1)

            def ffn_step(now, after=None, last=None, last_in=ROUTED, chunk=False, routed_after=False, own=False):
                hidden(now)
                if after:
                    low_in(after)
                if routed_after:
                    find_back(after)
                if last and last_in != ROUTED:
                    sum_y(last, last_in == LATE)
                if chunk:
                    split_lo(now)
                if own:
                    low_h(now)

            hidden(Tile(0, 0))
            low_in(Tile(0, 1))
            low_h(Tile(0, 0))
            dve.wait_ge(probs_done, 1)
            pick(onehot1, probs, max1)
            ffn_step(Tile(0, 1), Tile(0, 2), Tile(0, 0), EARLY, own=True)
            link(dve.scalar_tensor_tensor(out=rest, in0=onehot1, scalar=-4.0, in1=probs, op0=ALU.mult, op1=ALU.add))
            pick(onehot2, rest, max2)
            dve.tensor_tensor(member, onehot1, onehot2, ALU.add).then_inc(member_done, 1)
            link(dve.memset(reset_by_expert, 1.0))
            link(dve.memset(reset_by_expert[:, :, 0:1], 0.0))
            ffn_step(Tile(0, 2), Tile(0, 3), Tile(0, 1), EARLY, chunk=True, own=True)
            dve.wait_ge(total_mm, 1)
            link(dve.tensor_copy(totals_by_expert, total_ps.rearrange("p (i e) -> p e i", e=E)))
            link(dve.tensor_tensor_scan(flat(running_by_expert), flat(reset_by_expert), flat(totals_by_expert), 0.0,
                                        ALU.mult, ALU.add))
            link(dve.tensor_scalar(tile_n, running_by_expert[:, :, tiles - 1], float(P - 1), None, ALU.add))
            link(dve.tensor_scalar(tile_n, tile_n, P.bit_length() - 1, None, ALU.arith_shift_right))
            link(dve.tensor_copy(tile_f, tile_n))
            link(dve.tensor_tensor_scan(tile_end, ones[:, 0:E], tile_f, 0.0, ALU.mult, ALU.add))
            link(dve.tensor_tensor(slot_base, tile_end, tile_f, ALU.subtract))
            link(dve.tensor_scalar(slot_base, slot_base, float(P), None, ALU.mult))
            ffn_step(Tile(0, 3), Tile(0, 4), Tile(0, 2), EARLY, chunk=True, own=True)
            link(dve.tensor_tensor(position, running_by_expert.rearrange("p e i -> p i e"),
                                   totals_by_expert.rearrange("p e i -> p i e"), ALU.subtract))
            link(dve.tensor_tensor(position, position, over_tiles(slot_base), ALU.add))
            link(dve.tensor_tensor(position, rank_ps.rearrange("p (i e) -> p i e", e=E), position, ALU.add))
            for k, onehot in enumerate((onehot1, onehot2)):
                link(dve.tensor_tensor(picked, position, onehot, ALU.mult))
                link(dve.tensor_reduce(position_f[:, k, :], picked, AX_X, ALU.add))
            dve.tensor_copy(position_i[:, :, :], position_f).then_inc(position_done, 1)
            dve.tensor_scalar(words[:, 0, :], position_f[:, 1, :], 1.0, None, ALU.add).then_inc(position_done, 1)
            ffn_step(Tile(0, 4), Tile(0, 5), Tile(0, 3), EARLY, chunk=True, own=True)
            link(dve.tensor_tensor(expert_cmp,
                                   slot_number[0:1].unsqueeze(2).broadcast_to([1, slot_tiles, E]),
                                   tile_end[0:1, :].unsqueeze(1).broadcast_to([1, slot_tiles, E]), ALU.is_ge))
            link(dve.tensor_reduce(expert_f, expert_cmp, AX_X, ALU.add))
            dve.tensor_scalar(expert_i[:, :], expert_f, float(E - 1), None, ALU.min).then_inc(experts_done, 1)
            link(dve.tensor_tensor(p_sum, max1, max2, ALU.add))
            link(dve.reciprocal(p_inv, p_sum))
            link(dve.tensor_tensor(weight[:, 0, :], max1, p_inv, ALU.mult))
            link(dve.tensor_tensor(weight[:, 1, :], max2, p_inv, ALU.mult))
            with dve.Fori(2, E - 1) as it:
                for d in (1, 2):
                    ffn_step(Tile(it, d), Tile(it, d + 1), Tile(it, d - 1), EARLY, chunk=True, own=True)
            for n in range(2 * E - 1, early + 1):
                ffn_step(Tile(0, n), Tile(0, n + 1), Tile(0, n - 1), EARLY, chunk=n < 2 * E + 2,
                         routed_after=n + 1 >= early, own=n < early)
            for n in (early + 1, early + 2):
                ffn_step(Tile(0, n), Tile(0, n + 1), Tile(0, n - 1), ROUTED, routed_after=True)
            with dve.Fori(early // 2 + 1, routed_end // 2 - 1) as it:
                for d in (1, 2):
                    ffn_step(Tile(it, d), Tile(it, d + 1), Tile(it, d - 1), ROUTED, routed_after=True)
            for n in (routed_end - 1, routed_end):
                ffn_step(Tile(0, n), Tile(0, n + 1), Tile(0, n - 1), ROUTED, own=n == routed_end)
            def mix(q, half):
                b = q % AHEAD
                dve.wait_ge(own_loaded[b], q // AHEAD * GOT + GOT)
                for k in range(TOP_K):
                    for j in (2 * half, 2 * half + 1):
                        if k:
                            dve.wait_ge(mix_done, q * 8 + half * 4 + j % 2 + 1)
                        dve.scalar_tensor_tensor(out=own_sb[:, b, j, :], in0=got_sb[:, b, k, j, :],
                                                 scalar=weight[:, k, q * 4 + j:q * 4 + j + 1], in1=own_sb[:, b, j, :],
                                                 op0=ALU.mult, op1=ALU.add).then_inc(mix_done, 1)
                wait(dve, f_aggr_done, q * 4)
                for j in (2 * half, 2 * half + 1):
                    dve.wait_ge(mix_done, q * 8 + half * 4 + 3 + j % 2)
                    dve.bn_stats(f_stats[:, j, :], own_sb[:, b, j, :]).then_inc(f_stats_done, 1)

            def quad_moments(q):
                dve.wait_ge(f_stats_done, q * 4 + 4)
                wait(dve, f_shift_done, q - 1)
                for j in range(4):
                    dve.bn_aggr(f_moments[:, q % 2, j, :], f_stats[:, j, :]).then_inc(f_aggr_done, 1)

            def quad_scales(q):
                b = q % 2
                dve.wait_ge(f_std_done, q + 1)
                wait(dve, out_done, q * 4 - 4)
                dve.reciprocal(f_inv[:, b, :], f_std[:, b, :]).then_inc(f_inv_done, 1)
                dve.wait_ge(f_inv_done, q + 1)
                dve.scalar_tensor_tensor(out=f_shift[:, b, :], in0=f_moments[:, b, :, 0], scalar=-1.0,
                                         in1=f_inv[:, b, :], op0=ALU.mult, op1=ALU.mult).then_inc(f_shift_done, 1)

            def finish(q, half):
                mix(q, half)
                if half:
                    quad_moments(q)
                elif q:
                    quad_scales(q - 1)

            for n in range(routed_end + 1, ffn_tiles):
                ffn_step(Tile(0, n), Tile(0, n + 1) if n + 1 < ffn_tiles else None, Tile(0, n - 1), LATE,
                         own=True)
                if n >= routed_end + 2:
                    finish((n - routed_end) // 2 - 1, (n - routed_end) % 2)
            sum_y(Tile(0, n), True)
            for q in range((tiles - early) // 2 - 1, quads):
                finish(q, 0)
                finish(q, 1)
            quad_scales(quads - 1)


def kernel(L0_attn_x, L0_attn_Wqkv, L0_attn_bqkv, L0_attn_gamma_q, L0_attn_beta_q, L0_attn_gamma_k,
           L0_attn_beta_k, L0_attn_Wo, L0_attn_bo, L0_ffn_sg_w, L0_ffn_su_w, L0_ffn_sd_w, L0_ffn_router_w,
           L0_ffn_routing_bias, L0_ffn_wg, L0_ffn_wu, L0_ffn_wd):
    import numpy as np
    import concourse.bacc as bacc
    from concourse.bass_utils import run_bass_kernel_spmd

    x = np.asarray(L0_attn_x)
    B, T, C = x.shape
    tiles, halves = B * T // P, C // P
    E = L0_ffn_wg.shape[0]
    slot_tiles = tiles * TOP_K + E

    def by_feature(w):
        return np.asarray(w).reshape(-1, P, w.shape[1]).transpose(1, 0, 2)

    def expert_rows(gate, up, down):
        return np.concatenate([by_feature(np.asarray(w).T).reshape(P, -1) for w in (gate, up, down)], axis=1)

    rows = x.reshape(tiles, P, C)
    columns = [np.asarray(v).reshape(halves, P).T
               for v in (L0_attn_gamma_q, L0_attn_gamma_k, L0_attn_beta_q, L0_attn_beta_k)]
    arrays = {
        "xT": rows.reshape(tiles, P, halves, P).transpose(0, 3, 2, 1),
        "x": rows,
        "wqkv": by_feature(L0_attn_Wqkv),
        "bqkv": L0_attn_bqkv,
        "gb_cols": np.stack(columns, axis=1).reshape(P, 2, 2 * halves),
        "gk_row": L0_attn_gamma_k,
        "bk_row": L0_attn_beta_k,
        "wo": by_feature(L0_attn_Wo),
        "bo": L0_attn_bo,
        "router": by_feature(np.asarray(L0_ffn_router_w).T),
        "router_bias": L0_ffn_routing_bias,
        "ffn_w": np.stack([expert_rows(L0_ffn_wg[e], L0_ffn_wu[e], L0_ffn_wd[e]) for e in range(E)]
                          + [expert_rows(L0_ffn_sg_w, L0_ffn_su_w, L0_ffn_sd_w)]),
    }
    arrays = {name: np.ascontiguousarray(a) for name, a in arrays.items()}
    nc = bacc.Bacc("TRN2", target_bir_lowering=False, num_devices=1)
    ins = {name: nc.dram_tensor(name, a.shape, F32, kind="ExternalInput").ap() for name, a in arrays.items()}
    out = nc.dram_tensor("out", (tiles * P, C), F32, kind="ExternalOutput").ap()
    inner = {name: nc.dram_tensor(name, (rows, width), F32, kind="Internal").ap()
             for name, rows, width in (("x1_rows", tiles * P, C), ("sum_rows", tiles * P, C),
                                       ("slot_rows", slot_tiles * P, C + 2),
                                       ("routed_y", slot_tiles * P + 1 + TOP_K * tiles * P, C))}
    post_ln_block(nc, **ins, out=out, **inner)
    got = run_bass_kernel_spmd(nc, [arrays], core_ids=[0])
    return got.results[0]["out"].reshape(B, T, C)
```
